# Optimizing a Trainium2 kernel written in Bass

```python
import numpy as np
import jax
import jax.numpy as jnp

def _softmax(x, axis=-1):
    return jax.nn.softmax(x, axis=axis)

def _gelu(x):
    return jax.nn.gelu(x, approximate=True)

def _silu(x):
    return jax.nn.silu(x)

def _sigmoid(x):
    return jax.nn.sigmoid(x)

def _layernorm(x, axis=-1, eps=1e-05):
    m = jnp.mean(x, axis=axis, keepdims=True)
    v = jnp.var(x, axis=axis, keepdims=True)
    return (x - m) / jnp.sqrt(v + eps)

def _scatter_add(tgt, idx, src, axis=0):
    return tgt.at[idx].add(src)

def _segment_sum(src, seg, n):
    return jax.ops.segment_sum(src, seg, n)
kernel_name = 'mk_xattn_ffn_d2_seqx_r8_c3dc7c'

def setup_inputs(seed: int=0):
    np.random.seed(seed)
    _w = jnp.asarray

    def _rec_inputs():
        import jax
        import jax.numpy as jnp
        _rk = jax.random.key(seed)
        x = -0.0005207 + 1.001 * jax.random.normal(jax.random.fold_in(_rk, 1), (8, 128, 512), jnp.float32)
        _lenS = 128 - jax.random.randint(jax.random.fold_in(_rk, 7), (8,), 0, max(1, 128 // 4) + 1, jnp.int32)
        _lenS2 = 128 - jax.random.randint(jax.random.fold_in(_rk, 8), (8,), 0, max(1, 128 // 4) + 1, jnp.int32)
        _ctx_4096P = jax.random.normal(jax.random.fold_in(_rk, 11), (8, 16, 512), jnp.float32)
        _ctx_4096c = jax.random.dirichlet(jax.random.fold_in(_rk, 511), 0.3 * jnp.ones((16,), jnp.float32), (8, 128))
        _ctx_4096t = jnp.einsum('bsk,bkd->bsd', _ctx_4096c, _ctx_4096P)
        _ctx_4096t = _ctx_4096t * jax.lax.rsqrt(jnp.mean(jnp.square(_ctx_4096t)) + 1e-12) * 0.953939
        ctx_4096 = -0.00010331 + 0.999899 * (_ctx_4096t + 0.3 * jax.random.normal(jax.random.fold_in(_rk, 611), (8, 128, 512), jnp.float32))
        return (x, ctx_4096)
    x, ctx_4096 = _rec_inputs()

    def _L0_xattn_setup():
        import jax, jax.numpy as jnp
        import numpy as np
        B, Q, D = (8, 64, 512)
        CTX = 512
        H, KV, HD = (16, 4, 96)
        G = H // KV
        key = jax.random.key(seed)
        ks = jax.random.split(key, 6)
        s = 0.02
        return {'latents': jax.random.normal(ks[0], (B, Q, D), jnp.float32), 'context': jax.random.normal(ks[1], (B, CTX, D), jnp.float32), 'Wq': jax.random.normal(ks[2], (H * HD, D), jnp.float32) * s, 'Wk': jax.random.normal(ks[3], (KV * HD, D), jnp.float32) * s, 'Wv': jax.random.normal(ks[4], (KV * HD, D), jnp.float32) * s, 'Wo': jax.random.normal(ks[5], (D, H * HD), jnp.float32) * s}
    _L0_xattn_all = _L0_xattn_setup()
    _L0_xattn_in = {k: v for k, v in _L0_xattn_all.items() if k in ('Wq', 'Wk', 'Wv', 'Wo')}
    del _L0_xattn_all

    def _L0_ffn_setup():
        import jax, jax.numpy as jnp
        import numpy as np
        HID, INT, LAT, NE, K = (512, 1024, 256, 8, 2)
        LN_EPS = 1e-05

        def _layernorm(x, gamma, beta):
            mu = jnp.mean(x, axis=-1, keepdims=True)
            var = jnp.var(x, axis=-1, keepdims=True)
            return (x - mu) * jax.lax.rsqrt(var + LN_EPS) * gamma + beta
        key = jax.random.key(seed)
        ks = jax.random.split(key, 8)
        s = lambda d: 1.0 / np.sqrt(d)
        return {'hidden_states': jax.random.normal(ks[0], (4, 256, HID), jnp.float32), 'gate_w': jax.random.normal(ks[1], (HID, NE), jnp.float32) * s(HID), 'up_w': jax.random.normal(ks[2], (HID, INT), jnp.float32) * s(HID), 'down_w': jax.random.normal(ks[3], (INT, HID), jnp.float32) * s(INT), 'fc1_w': jax.random.normal(ks[4], (HID, LAT), jnp.float32) * s(HID), 'fc2_w': jax.random.normal(ks[5], (LAT, HID), jnp.float32) * s(LAT), 'expert_w': jax.random.normal(ks[6], (LAT, LAT), jnp.float32), 'ln_gamma': jnp.ones((HID,), jnp.float32), 'ln_beta': jnp.zeros((HID,), jnp.float32)}
    _L0_ffn_all = _L0_ffn_setup()
    _L0_ffn_in = {k: v for k, v in _L0_ffn_all.items() if k in ('gate_w', 'up_w', 'down_w', 'fc1_w', 'fc2_w', 'expert_w', 'ln_gamma', 'ln_beta')}
    del _L0_ffn_all

    def _L1_xattn_setup():
        import jax, jax.numpy as jnp
        import numpy as np
        HID = 512
        NHEAD = 32
        NKV = 8
        HDIM = 128
        G = NHEAD // NKV
        key = jax.random.key(seed)
        ks = jax.random.split(key, 6)
        s = 0.02
        B, L = (2, 256)
        return {'query': jax.random.normal(ks[0], (B, L, HID), jnp.float32), 'kv': jax.random.normal(ks[1], (B, L, HID), jnp.float32), 'Wq': jax.random.normal(ks[2], (HID, NHEAD * HDIM), jnp.float32) * s, 'bq': jnp.zeros((NHEAD * HDIM,), jnp.float32), 'Wkv': jax.random.normal(ks[3], (HID, 2 * NKV * HDIM), jnp.float32) * s, 'bkv': jnp.zeros((2 * NKV * HDIM,), jnp.float32), 'Wo': jax.random.normal(ks[4], (NHEAD * HDIM, HID), jnp.float32) * s, 'bo': jnp.zeros((HID,), jnp.float32)}
    _L1_xattn_all = _L1_xattn_setup()
    _L1_xattn_in = {k: v for k, v in _L1_xattn_all.items() if k in ('Wq', 'bq', 'Wkv', 'bkv', 'Wo', 'bo')}
    del _L1_xattn_all

    def _L1_ffn_setup():
        import jax, jax.numpy as jnp
        import numpy as np
        NUM_EXPERTS = 8
        RANK = 32
        ALPHA = 16.0
        TOP_K = 2
        TEMPERATURE = 1.0
        GAMMA = 0.5
        SOFT_TOPK_TEMP = 0.5
        N_GRAM = 2
        EPS = 1e-06
        key = jax.random.key(seed)
        ks = jax.random.split(key, 6)
        d_in, d_out = (512, 512)
        Bsz, T = (4, 256)
        x = jax.random.normal(ks[0], (Bsz, T, d_in), dtype=jnp.float32)
        W = jax.random.normal(ks[1], (d_out, d_in), dtype=jnp.float32) / np.sqrt(d_in)
        b = jax.random.normal(ks[2], (d_out,), dtype=jnp.float32) * 0.01
        A = jax.random.normal(ks[3], (d_in, RANK), dtype=jnp.float32) / np.sqrt(d_in)
        Bmat = jax.random.normal(ks[4], (RANK, d_out), dtype=jnp.float32) * 0.01
        LiMEs = jax.random.normal(ks[5], (NUM_EXPERTS, RANK), dtype=jnp.float32) * 0.1
        return {'x': x, 'W': W, 'b': b, 'A': A, 'Bmat': Bmat, 'LiMEs': LiMEs}
    _L1_ffn_all = _L1_ffn_setup()
    _L1_ffn_in = {k: v for k, v in _L1_ffn_all.items() if k in ('W', 'b', 'A', 'Bmat', 'LiMEs')}
    del _L1_ffn_all
    return {'x': x, 'ctx_4096': ctx_4096, 'L0_xattn_Wq': _L0_xattn_in['Wq'], 'L0_xattn_Wk': _L0_xattn_in['Wk'], 'L0_xattn_Wv': _L0_xattn_in['Wv'], 'L0_xattn_Wo': _L0_xattn_in['Wo'], 'L0_ffn_gate_w': _L0_ffn_in['gate_w'], 'L0_ffn_up_w': _L0_ffn_in['up_w'], 'L0_ffn_down_w': _L0_ffn_in['down_w'], 'L0_ffn_fc1_w': _L0_ffn_in['fc1_w'], 'L0_ffn_fc2_w': _L0_ffn_in['fc2_w'], 'L0_ffn_expert_w': _L0_ffn_in['expert_w'], 'L0_ffn_ln_gamma': _L0_ffn_in['ln_gamma'], 'L0_ffn_ln_beta': _L0_ffn_in['ln_beta'], 'L1_xattn_Wq': _L1_xattn_in['Wq'], 'L1_xattn_bq': _L1_xattn_in['bq'], 'L1_xattn_Wkv': _L1_xattn_in['Wkv'], 'L1_xattn_bkv': _L1_xattn_in['bkv'], 'L1_xattn_Wo': _L1_xattn_in['Wo'], 'L1_xattn_bo': _L1_xattn_in['bo'], 'L1_ffn_W': _L1_ffn_in['W'], 'L1_ffn_b': _L1_ffn_in['b'], 'L1_ffn_A': _L1_ffn_in['A'], 'L1_ffn_Bmat': _L1_ffn_in['Bmat'], 'L1_ffn_LiMEs': _L1_ffn_in['LiMEs']}

def reference(x, ctx_4096, L0_xattn_Wq, L0_xattn_Wk, L0_xattn_Wv, L0_xattn_Wo, L0_ffn_gate_w, L0_ffn_up_w, L0_ffn_down_w, L0_ffn_fc1_w, L0_ffn_fc2_w, L0_ffn_expert_w, L0_ffn_ln_gamma, L0_ffn_ln_beta, L1_xattn_Wq, L1_xattn_bq, L1_xattn_Wkv, L1_xattn_bkv, L1_xattn_Wo, L1_xattn_bo, L1_ffn_W, L1_ffn_b, L1_ffn_A, L1_ffn_Bmat, L1_ffn_LiMEs):
    import jax
    import jax.numpy as jnp

    def _L0_xattn_ref(latents, context, Wq, Wk, Wv, Wo):
        import jax, jax.numpy as jnp
        import numpy as np
        B, Q, D = (8, 64, 512)
        CTX = 512
        H, KV, HD = (16, 4, 96)
        G = H // KV
        b, q_len, _ = latents.shape
        hidden = jnp.concatenate([context, latents], axis=1)
        s_len = hidden.shape[1]
        q = (latents @ Wq.T).reshape(b, q_len, H, HD)
        k = (hidden @ Wk.T).reshape(b, s_len, KV, HD)
        v = (hidden @ Wv.T).reshape(b, s_len, KV, HD)
        q = q.transpose(0, 2, 1, 3).reshape(b, KV, G, q_len, HD)
        k = k.transpose(0, 2, 1, 3)
        v = v.transpose(0, 2, 1, 3)
        scale = 1.0 / jnp.sqrt(jnp.asarray(HD, q.dtype))
        scores = jnp.einsum('bkgqd,bksd->bkgqs', q, k) * scale
        attn = jax.nn.softmax(scores.astype(jnp.float32), axis=-1).astype(q.dtype)
        out = jnp.einsum('bkgqs,bksd->bkgqd', attn, v)
        out = out.reshape(b, H, q_len, HD).transpose(0, 2, 1, 3).reshape(b, q_len, H * HD)
        return out @ Wo.T

    def _L0_ffn_ref(hidden_states, gate_w, up_w, down_w, fc1_w, fc2_w, expert_w, ln_gamma, ln_beta):
        import jax, jax.numpy as jnp
        import numpy as np
        HID, INT, LAT, NE, K = (512, 1024, 256, 8, 2)
        LN_EPS = 1e-05

        def _layernorm(x, gamma, beta):
            mu = jnp.mean(x, axis=-1, keepdims=True)
            var = jnp.var(x, axis=-1, keepdims=True)
            return (x - mu) * jax.lax.rsqrt(var + LN_EPS) * gamma + beta
        logits = jnp.einsum('bsh,he->bse', hidden_states, gate_w)
        routing_weights, selected_experts = jax.lax.top_k(logits, K)
        h = jax.nn.relu(jnp.einsum('bsh,hi->bsi', hidden_states, up_w)) ** 2
        shared_out = jnp.einsum('bsi,ih->bsh', h, down_w)
        x_latent = jnp.einsum('bsh,hl->bsl', hidden_states, fc1_w)
        expert_out = jnp.einsum('bsl,lm->bsm', x_latent, expert_w)
        moe_out = expert_out * jnp.sum(routing_weights, axis=-1, keepdims=True)
        routed_out = jnp.einsum('bsl,lh->bsh', moe_out, fc2_w)
        return _layernorm(shared_out + routed_out, ln_gamma, ln_beta)

    def _L1_xattn_ref(query, kv, Wq, bq, Wkv, bkv, Wo, bo):
        import jax, jax.numpy as jnp
        import numpy as np
        HID = 512
        NHEAD = 32
        NKV = 8
        HDIM = 128
        G = NHEAD // NKV
        B, L, _ = query.shape
        Lk = kv.shape[1]
        scale = jnp.asarray(1.0 / np.sqrt(HDIM), query.dtype)
        q = (query @ Wq + bq).reshape(B, L, NKV, G, HDIM)
        k_, v_ = jnp.split(kv @ Wkv + bkv, 2, axis=-1)
        k = k_.reshape(B, Lk, NKV, HDIM)
        v = v_.reshape(B, Lk, NKV, HDIM)
        scores = jnp.einsum('blkgd,bmkd->bkglm', q, k) * scale
        attn = jax.nn.softmax(scores, axis=-1)
        o = jnp.einsum('bkglm,bmkd->blkgd', attn, v).reshape(B, L, NHEAD * HDIM)
        return o @ Wo + bo

    def _L1_ffn_ref(x, W, b, A, Bmat, LiMEs):
        import jax, jax.numpy as jnp
        import numpy as np
        NUM_EXPERTS = 8
        RANK = 32
        ALPHA = 16.0
        TOP_K = 2
        TEMPERATURE = 1.0
        GAMMA = 0.5
        SOFT_TOPK_TEMP = 0.5
        N_GRAM = 2
        EPS = 1e-06
        Bsz, T, d_in = x.shape
        E = LiMEs.shape[0]
        scaling = ALPHA / RANK
        H = jnp.einsum('btd,od->bto', x, W) + b
        z = jnp.einsum('btd,dr->btr', x, A)
        anchors = jnp.arange(N_GRAM - 1, T, N_GRAM)
        H_slice = H[:, anchors, :E]
        delta_slice = jnp.einsum('bar,er->bae', z[:, anchors], LiMEs)
        H_scale = jnp.maximum(jnp.max(jnp.abs(H_slice)), EPS)
        d_scale = jnp.maximum(jnp.max(jnp.abs(delta_slice)), EPS)
        logits = ((1.0 - GAMMA) * (H_slice / H_scale) + GAMMA * (delta_slice / d_scale)) / TEMPERATURE
        probs = jax.nn.softmax(logits, axis=-1)
        topk_vals, _ = jax.lax.top_k(probs, TOP_K)
        thresh = topk_vals[..., -1:]
        mask = jax.nn.sigmoid((probs - thresh) / SOFT_TOPK_TEMP)
        weights = probs * mask
        weights = weights / (jnp.sum(weights, axis=-1, keepdims=True) + 1e-09)
        weights_full = jnp.repeat(weights, N_GRAM, axis=1)
        p_mix = jnp.einsum('bte,er->btr', weights_full, LiMEs)
        delta = jnp.einsum('btr,ro->bto', z * p_mix, Bmat) * scaling
        return H + delta
    x = x + _L0_xattn_ref(_layernorm(x, axis=-1), ctx_4096, L0_xattn_Wq, L0_xattn_Wk, L0_xattn_Wv, L0_xattn_Wo)
    x = x + _L0_ffn_ref(_layernorm(x, axis=-1), L0_ffn_gate_w, L0_ffn_up_w, L0_ffn_down_w, L0_ffn_fc1_w, L0_ffn_fc2_w, L0_ffn_expert_w, L0_ffn_ln_gamma, L0_ffn_ln_beta)
    x = x + _L1_xattn_ref(_layernorm(x, axis=-1), ctx_4096, L1_xattn_Wq, L1_xattn_bq, L1_xattn_Wkv, L1_xattn_bkv, L1_xattn_Wo, L1_xattn_bo)
    x = x + _L1_ffn_ref(_layernorm(x, axis=-1), L1_ffn_W, L1_ffn_b, L1_ffn_A, L1_ffn_Bmat, L1_ffn_LiMEs)
    return x

_drawn_inputs = setup_inputs


def setup_inputs(seed=0):
    import zlib

    import numpy as np

    out = dict(_drawn_inputs(seed))
    spreads = {'L0_ffn_ln_gamma': (1.0, 0.2),
     'L0_ffn_ln_beta': (0.0, 0.1),
     'L1_xattn_bq': (0.0, 2.0),
     'L1_xattn_bkv': (0.0, 0.1),
     'L1_xattn_bo': (0.0, 0.1)}
    factors = {'L0_xattn_Wq': 5.424,
     'L0_xattn_Wk': 5.937,
     'L1_xattn_Wq': 3.897,
     'L1_ffn_b': 8.0,
     'L1_ffn_A': 8.0,
     'L1_ffn_Bmat': 8.0,
     'L1_ffn_LiMEs': 8.0}
    for name, (base, spread) in spreads.items():
        noise = np.random.default_rng([zlib.crc32(name.encode()), seed]).standard_normal(out[name].shape)
        drawn = base * np.exp(spread * noise) if base else spread * noise
        out[name] = jnp.asarray(drawn.astype(out[name].dtype))
    for name, factor in factors.items():
        out[name] = (out[name] * factor).astype(out[name].dtype)
    return out
```

```python
from contextlib import ExitStack

import numpy as np

import concourse.bass as bass
from concourse import mybir

F32 = mybir.dt.float32
F32R = mybir.dt.float32r
ALU = mybir.AluOpType
ACT = mybir.ActivationFunctionType
AX = mybir.AxisListType
RMAX = bass.bass_isa.ReduceOp.max

P = 128
NB = 8
HID = 512
KT = HID // P
TOK = NB * P
HALF = TOK // 2
G = 4
NE = 8
RANK = 32
LN_EPS = 1e-5


class Attention:

    def __init__(self, name, kv_heads, hd, sources, bias, kv0, q0, o0):
        self.name, self.kv_heads, self.hd, self.sources, self.bias = name, kv_heads, hd, sources, bias
        self.kv0, self.q0, self.o0 = kv0, q0, o0
        self.keys = sources * P
        self.scale = float(1.0 / np.sqrt(hd))
        self.score_banks = self.keys * G // 512
        self.q_uses = G * 2
        self.kv_uses = sources * 4
        self.proj = self.q_uses + self.kv_uses
        self.evacs = self.proj // 2
        self.v_groups = sources

    def proj_q(self, it, u):
        return self.kv_uses + it * self.proj + u + 1

    def proj_kv(self, it, u):
        return it * self.proj + u + 1

    def evac_q(self, it, u):
        return self.kv_uses // 2 + it * self.evacs + u // 2 + 1

    def evac_kv(self, it, u):
        return it * self.evacs + u // 2 + 1


class AttentionSems:

    def __init__(self, sem, prefix):
        self.proj_done = sem(f"{prefix}_proj_done")
        self.act_evac = sem(f"{prefix}_act_evac")
        self.dve_evac = sem(f"{prefix}_dve_evac")
        self.scores_done = sem(f"{prefix}_scores_done")
        self.max_raw = sem(f"{prefix}_max_raw")
        self.max_done = sem(f"{prefix}_max_done")
        self.exp_done = sem(f"{prefix}_exp_done")
        self.rcp_done = sem(f"{prefix}_rcp_done")
        self.norm_done = sem(f"{prefix}_norm_done")
        self.pt_done = sem(f"{prefix}_pt_done")
        self.pt_hi_done = sem(f"{prefix}_pt_hi_done")
        self.pt_lo_done = sem(f"{prefix}_pt_lo_done")
        self.pv_done = sem(f"{prefix}_pv_done")
        self.o_hi_done = sem(f"{prefix}_o_hi_done")
        self.o_lo_done = sem(f"{prefix}_o_lo_done")
        self.y_done = sem(f"{prefix}_y_done")
        self.y_added = sem(f"{prefix}_y_added")
        self.vt_done = sem(f"{prefix}_vt_done")
        self.v_hi_done = sem(f"{prefix}_v_hi_done")
        self.v_lo_done = sem(f"{prefix}_v_lo_done")


class NormSems:

    def __init__(self, sem, prefix):
        self.stat = sem(f"{prefix}_stat")
        self.var = sem(f"{prefix}_var")
        self.rstd = sem(f"{prefix}_rstd")
        self.xn = sem(f"{prefix}_xn")
        self.t = sem(f"{prefix}_t")
        self.hi = sem(f"{prefix}_hi")
        self.lo = sem(f"{prefix}_lo")


class Ffn0Sems:

    def __init__(self, sem, prefix):
        self.gate_split_hi = sem(f"{prefix}_gate_split_hi")
        self.gate_split_lo = sem(f"{prefix}_gate_split_lo")
        self.gate = sem(f"{prefix}_gate")
        self.route_top = sem(f"{prefix}_route_top")
        self.route = sem(f"{prefix}_route")
        self.lin = sem(f"{prefix}_lin")
        self.lin_hi = sem(f"{prefix}_lin_hi")
        self.lin_lo = sem(f"{prefix}_lin_lo")
        self.up = sem(f"{prefix}_up")
        self.relu = sem(f"{prefix}_relu")
        self.sq = sem(f"{prefix}_sq")
        self.h_hi = sem(f"{prefix}_h_hi")
        self.h_lo = sem(f"{prefix}_h_lo")
        self.down = sem(f"{prefix}_down")
        self.added = sem(f"{prefix}_added")
        self.scaled = sem(f"{prefix}_scaled")
        self.beta_added = sem(f"{prefix}_beta_added")


class Ffn1Sems:

    def __init__(self, sem, prefix):
        self.z = sem(f"{prefix}_z")
        self.z_evac = sem(f"{prefix}_z_evac")
        self.small = sem(f"{prefix}_small")
        self.small_evac = sem(f"{prefix}_small_evac")
        self.picked = sem(f"{prefix}_picked")
        self.dve = sem(f"{prefix}_dve")
        self.allmax = sem(f"{prefix}_allmax")
        self.exp = sem(f"{prefix}_exp")
        self.w = sem(f"{prefix}_w")
        self.wT = sem(f"{prefix}_wT")
        self.wT_evac = sem(f"{prefix}_wT_evac")
        self.pmix = sem(f"{prefix}_pmix")
        self.zp = sem(f"{prefix}_zp")
        self.H = sem(f"{prefix}_H")
        self.H_added = sem(f"{prefix}_H_added")
        self.delta = sem(f"{prefix}_delta")
        self.done = sem(f"{prefix}_done")
        self.b_added = sem(f"{prefix}_b_added")


def build_program(nc, A, out):
    L0 = Attention("L0", 4, 96, 2, False, kv0=0, q0=0, o0=0)
    L1 = Attention("L1", 8, 128, 1, True, kv0=5, q0=7, o0=7)
    FC1 = L0.kv_heads
    EXPERT = L0.kv_heads
    UP = EXPERT + 1
    FC2 = L0.kv_heads
    DOWN = FC2 + 1
    F1_A = L1.kv0 + L1.kv_heads
    F1_W = L1.q0 + L1.kv_heads

    with ExitStack() as ctx:
        def sb(name, shape, dt=F32, stack=ctx):
            return stack.enter_context(nc.sbuf_tensor(name, shape, dt))

        def sem(name):
            return ctx.enter_context(nc.semaphore(name))

        x = sb("x", [P, NB, HID])
        xT_hi = sb("xT_hi", [P, KT, TOK], F32R)
        xT_lo = sb("xT_lo", [P, KT, TOK], F32R)
        cT_hi = sb("cT_hi", [P, KT, TOK], F32R)
        cT_lo = sb("cT_lo", [P, KT, TOK], F32R)
        kv_raw = sb("kv_raw", [P, 1032])
        q_raw = sb("q_raw", [P, 2048])
        o_raw = sb("o_raw", [P, 2048])
        kv_hi, kv_lo = sb("kv_hi", [P, 1024], F32R), sb("kv_lo", [P, 1024], F32R)
        q_hi, q_lo = sb("q_hi", [P, 2048], F32R), sb("q_lo", [P, 2048], F32R)
        o_hi, o_lo = sb("o_hi", [P, 2048], F32R), sb("o_lo", [P, 2048], F32R)
        ident = sb("ident", [P, P])
        bias_now = sb("bias_now", [P, 8])
        stats = sb("stats", [P, NB, 6])
        mean_var = sb("mean_var", [P, NB, 2])
        var_eps = sb("var_eps", [P, NB])
        rstd = sb("rstd", [P, NB])
        minus_half = sb("minus_half", [P, NB])
        neg_max_raw = sb("neg_max_raw", [P, 2, G])
        neg_max = sb("neg_max", [P, 2, G])
        exp_sum = sb("exp_sum", [P, 2, G])
        exp_rcp = sb("exp_rcp", [P, 2, G])
        gate_raw = sb("gate_raw", [P, KT, NE])
        gate_hi, gate_lo = sb("gate_hi", [P, KT, NE], F32R), sb("gate_lo", [P, KT, NE], F32R)
        top8 = sb("top8", [P, NB, 8])
        route = sb("route", [P, NB])
        with ExitStack() as st:
            qT = sb("qT", [P, G, TOK], stack=st)
            kT = sb("kT", [P, NB * 2 * P], stack=st)
            vT = sb("vT", [P, 2 * TOK], stack=st)
            prob = sb("prob", [P, 2, G * 2 * P], stack=st)
            pT_hi, pT_lo = sb("pT_hi", [P, 2, 512], F32R, st), sb("pT_lo", [P, 2, 512], F32R, st)
            v_hi, v_lo = sb("v_hi", [P, 16 * 96], F32R, st), sb("v_lo", [P, 16 * 96], F32R, st)
            oT_hi, oT_lo = sb("oT_hi", [P, G, P], F32R, st), sb("oT_lo", [P, G, P], F32R, st)
            bo_bc = sb("bo_bc", [P, HID], stack=st)
        with ExitStack() as st:
            h_hi, h_lo = sb("h_hi", [P, KT, TOK], F32R, st), sb("h_lo", [P, KT, TOK], F32R, st)
            acc = sb("acc", [P, NB, HID], stack=st)
            relu = sb("relu", [P, 2, HALF], stack=st)
            gamma = sb("gamma", [P, HID], stack=st)
            h_f = sb("h_f", [P, 2, HALF], stack=st)
            beta = sb("beta", [P, HID], stack=st)
            xn = sb("xn", [P, 2, HID], stack=st)
        with ExitStack() as st:
            zT = sb("zT", [RANK, TOK], stack=st)
            zp = sb("zp", [RANK, TOK], stack=st)
            wT = sb("wT", [NE, TOK], stack=st)
            b_mat = sb("b_mat", [RANK, HID], stack=st)
            limes = sb("limes", [NE, RANK], stack=st)
            limesT = sb("limesT", [RANK, NE], stack=st)
            b_bc = sb("b_bc", [P, HID], stack=st)
            odd_rows = sb("odd_rows", [P, P], stack=st)
            hd_raw = sb("hd_raw", [P, 2, NB, NE], stack=st)
            hd = sb("hd", [P, 2, NB, NE], stack=st)
            absmax = sb("absmax", [P, 2], stack=st)
            allmax = sb("allmax", [P, 2], stack=st)
            lg = [sb(f"lg{i}", [P, NB, NE], stack=st) for i in range(8)]
            row = [sb(f"row{i}", [P, NB], stack=st) for i in range(6)]
            top8b = sb("top8b", [P, NB, 8], stack=st)

        work = ctx.enter_context(nc.psum_tensor("work", [P, 4, 512], F32))
        pt = ctx.enter_context(nc.psum_tensor("pt", [P, 2, 512], F32))
        ov = ctx.enter_context(nc.psum_tensor("ov", [P, 512], F32))
        yb = ctx.enter_context(nc.psum_tensor("yb", [P, 512], F32))
        y2 = [yb, ov]

        x_loaded = [sem("x_loaded0"), sem("x_loaded1")]
        c_loaded = sem("c_loaded")
        const_loaded = sem("const_loaded")
        ffn1_loaded = sem("ffn1_loaded")
        ffn0_loaded = sem("ffn0_loaded")
        bo_loaded = sem("bo_loaded")
        kv_loaded, kv_hi_done, kv_lo_done = sem("kv_loaded"), sem("kv_hi_done"), sem("kv_lo_done")
        q_loaded, q_hi_done, q_lo_done = sem("q_loaded"), sem("q_hi_done"), sem("q_lo_done")
        o_loaded, o_hi_done, o_lo_done = sem("o_loaded"), sem("o_hi_done"), sem("o_lo_done")
        c_hi_done, c_lo_done = sem("c_hi_done"), sem("c_lo_done")
        out_stored = sem("out_stored")
        pool_set = sem("pool_set")
        bias_copied = sem("bias_copied")

        S0, S1 = AttentionSems(sem, "L0"), AttentionSems(sem, "L1")

        N = [NormSems(sem, f"ln{i}") for i in range(4)]
        NA = NormSems(sem, "ln_acc")
        f0 = Ffn0Sems(sem, "f0")
        bo_added = sem("bo_added")
        f1 = Ffn1Sems(sem, "f1")

        block = ctx.enter_context(nc.Block())

        @block.sync
        def _(sp):
            def load(raw, src, loaded, lo_done, n):
                sp.wait_ge(lo_done, n)
                sp.dma_start(raw, src).then_inc(loaded, 16)

            for h in range(2):
                sp.dma_start(x[:, 4 * h:4 * h + 4, :],
                             A["x"][4 * h:4 * h + 4].rearrange("b t d -> t b d")).then_inc(x_loaded[h], 16)
                if h == 0:
                    sp.dma_start(qT[:, :, :], A["ctxT"]).then_inc(c_loaded, 16)
                    sp.dma_start(ident[:, :], A["ident"]).then_inc(const_loaded, 16)
                    sp.dma_start(gate_raw[:, :, :], A["gate"]).then_inc(const_loaded, 16)
            sp.dma_start(kv_raw[:, 0:768], A["l0_kv"][0]).then_inc(kv_loaded, 16)
            sp.dma_start(q_raw[:, 0:1536], A["l0_q"][0]).then_inc(q_loaded, 16)
            sp.dma_start(o_raw[0:96, :], A["l0_o"][0]).then_inc(o_loaded, 16)
            with sp.Fori(1, L0.kv_heads) as it:
                load(kv_raw[:, 0:768], A["l0_kv"][it], kv_loaded, kv_lo_done, it)
                load(q_raw[:, 0:1536], A["l0_q"][it], q_loaded, q_lo_done, it)
                load(o_raw[0:96, :], A["l0_o"][it], o_loaded, o_lo_done, it)
            load(kv_raw[:, 0:1024], A["fc1"], kv_loaded, kv_lo_done, FC1)
            load(q_raw[:, 0:512], A["expert"], q_loaded, q_lo_done, EXPERT)
            load(o_raw[:, 0:1024], A["fc2"], o_loaded, o_lo_done, FC2)
            sp.wait_ge(S0.y_done, L0.kv_heads * NB)
            sp.wait_ge(S0.o_lo_done, L0.kv_heads * NB)
            sp.dma_start(gamma[:, :], A["gamma"]).then_inc(ffn0_loaded, 16)
            sp.dma_start(beta[:, :], A["beta"]).then_inc(ffn0_loaded, 16)
            load(q_raw[:, :], A["up"][0], q_loaded, q_lo_done, UP)
            load(o_raw[:, :], A["down"][0], o_loaded, o_lo_done, DOWN)
            load(q_raw[:, :], A["up"][1], q_loaded, q_lo_done, UP + 1)
            load(kv_raw[:, 0:1030], A["l1_kv"][0], kv_loaded, kv_lo_done, L1.kv0)
            load(o_raw[:, :], A["down"][1], o_loaded, o_lo_done, DOWN + 1)
            load(q_raw[:, :], A["l1_q"][0], q_loaded, q_lo_done, L1.q0)
            load(o_raw[:, :], A["l1_o"][0], o_loaded, o_lo_done, L1.o0)
            sp.dma_start(bo_bc[:, :], A["bo"]).then_inc(bo_loaded, 16)
            with sp.Fori(1, L1.kv_heads) as it:
                load(kv_raw[:, 0:1030], A["l1_kv"][it], kv_loaded, kv_lo_done, it + L1.kv0)
                load(q_raw[:, :], A["l1_q"][it], q_loaded, q_lo_done, it + L1.q0)
                load(o_raw[:, :], A["l1_o"][it], o_loaded, o_lo_done, it + L1.o0)
            load(kv_raw[:, 0:KT * RANK], A["A"], kv_loaded, kv_lo_done, F1_A)
            load(q_raw[:, :], A["W"], q_loaded, q_lo_done, F1_W)
            sp.wait_ge(S1.y_added, L1.kv_heads * NB)
            for dst, src in ((b_mat, "Bmat"), (limes, "LiMEs"), (limesT, "LiMEsT"), (b_bc, "b"), (odd_rows, "odd_rows")):
                sp.dma_start(dst[:, :], A[src]).then_inc(ffn1_loaded, 16)
            for b in range(NB):
                sp.wait_ge(f1.done, b + 1)
                sp.dma_start(out[b], x[:, b, :]).then_inc(out_stored, 16)
            sp.wait_ge(out_stored, 16 * NB)

        @block.tensor
        def _(pe):
            def product(dst, pairs, first=True, last=True):
                n = len(pairs)
                for k, ((l_hi, l_lo), (r_hi, r_lo)) in enumerate(pairs):
                    pe.matmul(dst, l_hi, r_hi, start=first and k == 0, stop=False)
                    pe.matmul(dst, l_hi, r_lo, start=False, stop=False)
                    mm = pe.matmul(dst, l_lo, r_hi, start=False, stop=last and k == n - 1)
                return mm

            def weights(hi, lo, width, at, n):
                return [(hi[:, k * width + at:k * width + at + n], lo[:, k * width + at:k * width + at + n])
                        for k in range(KT)]

            def columns(hi, lo, at, n):
                return [(hi[:, k, at:at + n], lo[:, k, at:at + n]) for k in range(KT)]

            def project_kv(L, S, it, uses):
                if uses[0] == 0:
                    pe.wait_ge(kv_lo_done, it + (L.kv0 + 1))
                for u in uses:
                    src, is_v, half = u // 4, u // 2 % 2, u % 2
                    hi, lo = (cT_hi, cT_lo) if src == 0 else (xT_hi, xT_lo)
                    if u >= 4:
                        pe.wait_ge(S.act_evac if u % 2 == 0 else S.dve_evac, L.evac_kv(it, u - 4))
                    w = weights(kv_hi, kv_lo, 2 * L.hd, is_v * L.hd, L.hd)
                    product(work[0:L.hd, u % 4, :], list(zip(w, columns(hi, lo, half * HALF, HALF))))\
                        .then_inc(S.proj_done, 1)

            def transpose_v(L, S, it):
                for g in range(L.v_groups):
                    pe.wait_ge(S.act_evac, L.evac_kv(it, 4 * g + 2))
                    pe.wait_ge(S.dve_evac, L.evac_kv(it, 4 * g + 3))
                    if g:
                        pe.wait_ge(S.v_lo_done, it * L.v_groups + g)
                    for j in range(8):
                        mm = pe.transpose(pt[:, j // 4, j % 4 * P:j % 4 * P + L.hd],
                                          vT[0:L.hd, (8 * g + j) * P:(8 * g + j + 1) * P], ident[0:L.hd, 0:L.hd])
                    mm.then_inc(S.vt_done, 1)

            def project_q(L, S, it):
                pe.wait_ge(q_lo_done, it + (L.q0 + 1))
                for u in range(L.q_uses):
                    half, g = u // G, u % G
                    if u < 4:
                        pe.wait_ge(S.act_evac if u % 2 == 0 else S.dve_evac, L.evac_kv(it, L.kv_uses - 4 + u))
                    else:
                        pe.wait_ge(S.act_evac if u % 2 == 0 else S.dve_evac, L.evac_q(it, u - 4))
                    w = weights(q_hi, q_lo, G * L.hd, g * L.hd, L.hd)
                    product(work[0:L.hd, u % 4, :], list(zip(w, columns(xT_hi, xT_lo, half * HALF, HALF))))\
                        .then_inc(S.proj_done, 1)

            def scores(L, S, it, b):
                u = L.q_uses + b * L.score_banks
                if b % 4 == 0:
                    pe.wait_ge(S.act_evac, L.evac_q(it, 4 * (b // 4) + 2))
                    pe.wait_ge(S.dve_evac, L.evac_q(it, 4 * (b // 4) + 3))
                if b * L.score_banks < 4:
                    pe.wait_ge(S.act_evac, L.evac_q(it, 4 + (b * L.score_banks & 2)))
                    pe.wait_ge(S.dve_evac, L.evac_q(it, 4 + (b * L.score_banks & 2) + 1))
                else:
                    pe.wait_ge(S.exp_done, it * (NB * L.score_banks) + (b + 1) * L.score_banks - 4)
                bank = u % 4
                dst = work[:, bank:bank + L.score_banks, :].rearrange("p a (g k) -> p (a g) k", k=L.keys)
                for g in range(G):
                    mm = pe.matmul(dst[:, g, :], qT[0:L.hd, g, b * P:(b + 1) * P],
                                   kT[0:L.hd, b * L.keys:(b + 1) * L.keys], start=True, stop=True)
                mm.then_inc(S.scores_done, 1)

            def transpose_p(L, S, it, b):
                pe.wait_ge(S.norm_done, it * NB + (b + 1))
                if b == 0:
                    pe.wait_ge(S.v_lo_done, (it + 1) * L.v_groups)
                for c in range(L.sources):
                    for g in range(G):
                        mm = pe.transpose(pt[:, c, g * P:(g + 1) * P],
                                          prob[:, b % 2, g * L.keys + c * P:g * L.keys + (c + 1) * P],
                                          ident[:, :])
                mm.then_inc(S.pt_done, 1)

            def values(L, S, it, b):
                pe.wait_ge(S.pt_lo_done, it * NB + (b + 1))
                if b:
                    pe.wait_ge(S.o_lo_done, it * NB + b)
                pairs = []
                for c in range(L.sources):
                    at = (c * NB + b) * L.hd
                    pairs.append(((v_hi[:, at:at + L.hd], v_lo[:, at:at + L.hd]),
                                  (pT_hi[:, c, :], pT_lo[:, c, :])))
                product(ov[0:L.hd, :], pairs).then_inc(S.pv_done, 1)

            def output(L, S, it, b):
                if b == 0:
                    pe.wait_ge(o_lo_done, it + (L.o0 + 1))
                else:
                    pe.wait_ge(S.y_added, it * NB + b)
                pe.wait_ge(S.o_lo_done, it * NB + (b + 1))
                product(yb[:, :], [((oT_hi[0:L.hd, g, :], oT_lo[0:L.hd, g, :]),
                                    (o_hi[0:L.hd, g * HID:(g + 1) * HID], o_lo[0:L.hd, g * HID:(g + 1) * HID]))
                                   for g in range(G)]).then_inc(S.y_done, 1)

            def attention_head(L, S, it, last):
                project_q(L, S, it)
                for i in range(NB + 3):
                    if i < NB:
                        scores(L, S, it, i)
                    elif not last and i == NB:
                        pe.wait_ge(S.exp_done, (it + 1) * (NB * L.score_banks))
                        project_kv(L, S, it + 1, range(L.kv_uses // 2))
                    elif not last and i == NB + 1:
                        project_kv(L, S, it + 1, range(L.kv_uses // 2, L.kv_uses))
                    if 2 <= i < NB + 2:
                        transpose_p(L, S, it, i - 2)
                    if i >= 3:
                        output(L, S, it, i - 3)
                    if 2 <= i < NB + 2:
                        values(L, S, it, i - 2)
                if not last:
                    transpose_v(L, S, it + 1)

            def attention(L, S):
                with pe.Fori(0, L.kv_heads - 1) as it:
                    attention_head(L, S, it, False)
                attention_head(L, S, L.kv_heads - 1, True)

            def transposed_norm(n, banks_free):
                for b in range(NB):
                    pe.wait_ge(n.xn, b + 1)
                    if b < 4:
                        banks_free(b)
                    else:
                        pe.wait_ge(n.lo, b - 3)
                    for k in range(KT):
                        mm = pe.transpose(work[:, b % 4, k * P:(k + 1) * P], xn[:, b % 2, k * P:(k + 1) * P],
                                          ident[:, :])
                    mm.then_inc(n.t, 1)

            def drained(n):
                pe.wait_ge(n.lo, NB)

            pe.wait_ge(const_loaded, 32)
            pe.wait_ge(c_lo_done, KT)
            project_kv(L0, S0, 0, range(4))
            transposed_norm(N[0], lambda b: pe.wait_ge(S0.act_evac if b % 2 == 0 else S0.dve_evac,
                                                       L0.evac_kv(0, b)))
            drained(N[0])
            project_kv(L0, S0, 0, range(4, 8))
            transpose_v(L0, S0, 0)
            attention(L0, S0)

            transposed_norm(N[1], lambda b: pe.wait_ge(S0.exp_done, L0.kv_heads * NB * L0.score_banks))
            drained(N[1])
            pe.wait_ge(f0.gate_split_lo, 1)
            for b in range(NB):
                mm = product(pt[:, 0, b * NE:(b + 1) * NE],
                             [((xT_hi[:, k, b * P:(b + 1) * P], xT_lo[:, k, b * P:(b + 1) * P]),
                               (gate_hi[:, k, :], gate_lo[:, k, :])) for k in range(KT)])
            mm.then_inc(f0.gate, 1)
            pe.wait_ge(kv_lo_done, FC1 + 1)
            for u in range(4):
                half, m = u // 2, u % 2
                product(work[:, u, :], list(zip(weights(kv_hi, kv_lo, 256, m * P, P),
                                                columns(xT_hi, xT_lo, half * HALF, HALF)))).then_inc(f0.lin, 1)
            pe.wait_ge(q_lo_done, EXPERT + 1)
            for u in range(4):
                half, m = u // 2, u % 2
                pe.wait_ge(f0.lin_lo, 2 * half + 2 if 2 * half + 2 > u + 1 else u + 1)
                product(work[:, u, :],
                        [((q_hi[:, k * 256 + m * P:k * 256 + (m + 1) * P], q_lo[:, k * 256 + m * P:k * 256 + (m + 1) * P]),
                          (h_hi[:, k, half * HALF:(half + 1) * HALF], h_lo[:, k, half * HALF:(half + 1) * HALF]))
                         for k in range(2)]).then_inc(f0.lin, 1)
            pe.wait_ge(o_lo_done, FC2 + 1)
            for b in range(NB):
                pe.wait_ge(f0.lin_lo, 4 + (2 if b < 4 else 4))
                if b >= 2:
                    pe.wait_ge(f0.added, b - 1)
                product(y2[b % 2][:, :],
                        [((h_hi[:, 2 + k, b * P:(b + 1) * P], h_lo[:, 2 + k, b * P:(b + 1) * P]),
                          (o_hi[:, k * HID:(k + 1) * HID], o_lo[:, k * HID:(k + 1) * HID]))
                         for k in range(2)]).then_inc(f0.down, 1)

            def mlp_half(hf):
                pe.wait_ge(q_lo_done, hf + (UP + 1))
                for u in range(8):
                    half, m = u // 4, u % 4
                    if u >= 4:
                        pe.wait_ge(f0.relu, hf * 8 + (u - 3))
                    product(work[:, u % 4, :], list(zip(weights(q_hi, q_lo, HID, m * P, P),
                                                        columns(xT_hi, xT_lo, half * HALF, HALF)))).then_inc(f0.up, 1)
                pe.wait_ge(o_lo_done, hf + (DOWN + 1))
                for b in range(NB):
                    pe.wait_ge(f0.h_lo, hf * 8 + (4 if b < 4 else 8))
                    pe.wait_ge(f0.added, hf * 8 + (NB + b - 1))
                    product(y2[b % 2][:, :],
                            [((h_hi[:, m, b * P:(b + 1) * P], h_lo[:, m, b * P:(b + 1) * P]),
                              (o_hi[:, m * HID:(m + 1) * HID], o_lo[:, m * HID:(m + 1) * HID]))
                             for m in range(4)]).then_inc(f0.down, 1)

            with pe.Fori(0, 2) as hf:
                mlp_half(hf)

            pe.wait_ge(f0.relu, 16)
            project_kv(L1, S1, 0, range(4))
            transpose_v(L1, S1, 0)
            transposed_norm(N[2], lambda b: pe.wait_ge(S1.act_evac if b % 2 == 0 else S1.dve_evac,
                                                       L1.evac_kv(0, b)))
            drained(N[2])
            attention(L1, S1)

            transposed_norm(N[3], lambda b: pe.wait_ge(S1.exp_done, L1.kv_heads * NB * L1.score_banks))
            drained(N[3])
            pe.wait_ge(kv_lo_done, F1_A + 1)
            for half in range(2):
                product(work[0:RANK, half, :], list(zip(weights(kv_hi, kv_lo, RANK, 0, RANK),
                                                        columns(xT_hi, xT_lo, half * HALF, HALF)))).then_inc(f1.z, 1)
            pe.wait_ge(q_lo_done, F1_W + 1)
            for b in range(NB):
                product(work[:, 2, b * NE:(b + 1) * NE],
                        [((xT_hi[:, k, b * P:(b + 1) * P], xT_lo[:, k, b * P:(b + 1) * P]),
                          (q_hi[:, k * HID:k * HID + NE], q_lo[:, k * HID:k * HID + NE])) for k in range(KT)])
            pe.wait_ge(ffn1_loaded, 80)
            pe.wait_ge(f1.z_evac, 2)
            for b in range(NB):
                mm = pe.matmul(work[:, 3, b * NE:(b + 1) * NE], zT[:, b * P:(b + 1) * P], limesT[:, :],
                               start=True, stop=True)
            mm.then_inc(f1.small, 1)

            def big_h(b):
                if b >= 2:
                    pe.wait_ge(f1.H_added, b - 1)
                product(y2[b % 2][:, :],
                        [((xT_hi[:, k, b * P:(b + 1) * P], xT_lo[:, k, b * P:(b + 1) * P]),
                          (q_hi[:, k * HID:(k + 1) * HID], q_lo[:, k * HID:(k + 1) * HID]))
                         for k in range(KT)]).then_inc(f1.H, 1)

            big_h(0)
            pe.wait_ge(f1.small_evac, 2)
            pe.matmul(pt[:, 0, 0:2 * NB * NE], odd_rows[:, :], hd_raw[:, :, :, :].rearrange("p a b e -> p (a b e)"),
                      start=True, stop=True).then_inc(f1.picked, 1)
            for b in range(1, NB):
                big_h(b)
            pe.wait_ge(f1.w, 1)
            for b in range(NB):
                mm = pe.transpose(work[0:NE, b // 4, b % 4 * P:(b % 4 + 1) * P], lg[5][:, b, :], ident[:, :])
            mm.then_inc(f1.wT, 1)
            pe.wait_ge(f1.wT_evac, 1)
            for half in range(2):
                mm = pe.matmul(work[0:RANK, 2 + half, :], limes[:, :], wT[:, half * HALF:(half + 1) * HALF],
                               start=True, stop=True)
            mm.then_inc(f1.pmix, 1)
            pe.wait_ge(f1.zp, 2)
            for b in range(NB):
                if b < 2:
                    pe.wait_ge(f1.H_added, NB - 1 + b)
                else:
                    pe.wait_ge(f1.done, b - 1)
                pe.matmul(y2[b % 2][:, :], zp[:, b * P:(b + 1) * P], b_mat[:, :], start=True, stop=True)\
                    .then_inc(f1.delta, 1)

        @block.scalar
        def _(act):
            def split_hi(hi, raw, n, rows, loaded, done, in_use, at, value):
                act.wait_ge(loaded, at * 16 + 16)
                if in_use is not None:
                    act.wait_ge(in_use, value)
                act.activation(hi[0:rows, 0:n], raw[0:rows, 0:n], ACT.Copy).then_inc(done, 1)

            def copy_bias(at):
                act.wait_ge(kv_loaded, at * 16 + 16)
                act.activation(bias_now[:, 0:6], kv_raw[:, 1024:1030], ACT.Copy).then_inc(bias_copied, 1)

            def evac_projection(L, S, dst, bank, done, col):
                act.wait_ge(S.proj_done, done)
                if L.bias:
                    act.activation(dst, work[0:L.hd, bank, :], ACT.Identity, bias=bias_now[:, col:col + 1])\
                        .then_inc(S.act_evac, 1)
                else:
                    act.activation(dst, work[0:L.hd, bank, :], ACT.Copy).then_inc(S.act_evac, 1)

            def evac_kv(L, S, it, uses):
                for u in uses:
                    if u % 2 == 0:
                        src, is_v = u // 4, u // 2 % 2
                        dst = (vT[0:L.hd, src * TOK:src * TOK + HALF] if is_v else
                               kT[0:L.hd, 0:NB * L.keys].rearrange("p (b s k) -> p b s k", b=NB, k=P)[:, 0:4, src, :])
                        evac_projection(L, S, dst, u % 4, L.proj_kv(it, u), G + is_v)

            def evac_v(L, S, it):
                for g in range(L.v_groups):
                    act.wait_ge(S.vt_done, it * L.v_groups + (g + 1))
                    act.activation(v_hi[:, 8 * g * L.hd:8 * (g + 1) * L.hd].rearrange("p (j d) -> p j d", d=L.hd),
                                   pt[:, :, :].rearrange("p a (j d) -> p (a j) d", d=P)[:, :, 0:L.hd], ACT.Copy)\
                        .then_inc(S.v_hi_done, 1)

            def head(L, S, it, last, next_kv, next_q):
                split_hi(o_hi, o_raw, 2048, L.hd, o_loaded, o_hi_done, S.proj_done, it + L.o0, L.proj_q(it, 0))
                for u in range(0, L.q_uses, 2):
                    half, g = u // G, u % G
                    evac_projection(L, S, qT[0:L.hd, g, half * HALF:(half + 1) * HALF], u % 4, L.proj_q(it, u), g)
                for i in range(NB + 2):
                    if i >= NB and not last:
                        evac_kv(L, S, it + 1, range((i - NB) * L.kv_uses // 2, (i - NB + 1) * L.kv_uses // 2))
                    if i >= 2:
                        b = i - 2
                        act.wait_ge(S.pt_done, it * NB + (b + 1))
                        act.activation(pT_hi[:, 0:L.sources, :], pt[:, 0:L.sources, :], ACT.Copy)\
                            .then_inc(S.pt_hi_done, 1)
                    if i < NB:
                        act.wait_ge(S.max_done, it * NB + (i + 1))
                        bank = (L.q_uses + i * L.score_banks) % 4
                        s = work[:, bank:bank + L.score_banks, :].rearrange("p a (g k) -> p (a g) k", k=L.keys)
                        for g in range(G):
                            e = act.activation(prob[:, i % 2, g * L.keys:(g + 1) * L.keys], s[:, g, :], ACT.Exp,
                                               bias=neg_max[:, i % 2, g:g + 1], scale=L.scale,
                                               accum_out=exp_sum[:, i % 2, g:g + 1])
                            if (g + 1) % (G // L.score_banks) == 0:
                                e.then_inc(S.exp_done, 1)
                    if i >= 2:
                        act.wait_ge(S.pv_done, it * NB + (b + 1))
                        act.activation(oT_hi[0:L.hd, :, :], ov[0:L.hd, :].rearrange("p (g q) -> p g q", g=G),
                                       ACT.Copy).then_inc(S.o_hi_done, 1)
                    if i == 2:
                        if L.bias and not last:
                            act.wait_ge(S.dve_evac, L.evac_q(it, L.q_uses - 1))
                            copy_bias(it + (L.kv0 + 1))
                        split_hi(kv_hi, kv_raw, next_kv, P, kv_loaded, kv_hi_done, S.proj_done,
                                 it + (L.kv0 + 1), L.proj_kv(it, L.kv_uses - 1))
                    if i == 5:
                        split_hi(q_hi, q_raw, next_q, P, q_loaded, q_hi_done, S.proj_done,
                                 it + (L.q0 + 1), L.proj_q(it, L.q_uses - 1))
                if not last:
                    evac_v(L, S, it + 1)

            def attention(L, S, next_kv, next_q, own_kv, own_q):
                with act.Fori(0, L.kv_heads - 1) as it:
                    head(L, S, it, False, own_kv, own_q)
                head(L, S, L.kv_heads - 1, True, next_kv, next_q)

            def norm_hi(n):
                for b in range(NB):
                    act.wait_ge(n.t, b + 1)
                    act.activation(xT_hi[:, :, b * P:(b + 1) * P],
                                   work[:, b % 4, :].rearrange("p (k t) -> p k t", k=KT), ACT.Copy)\
                        .then_inc(n.hi, 1)

            split_hi(kv_hi, kv_raw, 768, P, kv_loaded, kv_hi_done, None, 0, 0)
            act.wait_ge(c_loaded, 16)
            for k in range(KT):
                act.activation(cT_hi[:, k, :], qT[:, k, :], ACT.Copy).then_inc(c_hi_done, 1)
            act.wait_ge(const_loaded, 32)
            act.activation(gate_hi[:, :, :], gate_raw[:, :, :], ACT.Copy).then_inc(f0.gate_split_hi, 1)
            evac_kv(L0, S0, 0, range(4))
            split_hi(q_hi, q_raw, 1536, P, q_loaded, q_hi_done, None, 0, 0)
            norm_hi(N[0])
            evac_kv(L0, S0, 0, range(4, 8))
            evac_v(L0, S0, 0)
            attention(L0, S0, 1024, 512, 768, 1536)

            split_hi(o_hi, o_raw, 1024, P, o_loaded, o_hi_done, S0.y_done, FC2, L0.kv_heads * NB)
            norm_hi(N[1])
            for u in range(8):
                half, m = u // 2 % 2, u % 2
                act.wait_ge(f0.lin, u + 1)
                act.activation(h_hi[:, (u // 4) * 2 + m, half * HALF:(half + 1) * HALF], work[:, u % 4, :], ACT.Copy)\
                    .then_inc(f0.lin_hi, 1)
            split_hi(q_hi, q_raw, 2048, P, q_loaded, q_hi_done, f0.lin, UP, 8)
            split_hi(o_hi, o_raw, 2048, P, o_loaded, o_hi_done, f0.down, DOWN, NB)

            def square_hi(hf, u):
                half, m = u // 4, u % 4
                act.wait_ge(f0.sq, hf * 8 + (u + 1))
                act.activation(h_hi[:, m, half * HALF:(half + 1) * HALF], h_f[:, u % 2, :], ACT.Copy)\
                    .then_inc(f0.h_hi, 1)

            def mlp_half(hf):
                for u in range(8):
                    act.wait_ge(f0.up, hf * 8 + (u + 1))
                    act.activation(relu[:, u % 2, :], work[:, u % 4, :], ACT.Relu).then_inc(f0.relu, 1)
                    if u:
                        square_hi(hf, u - 1)
                square_hi(hf, 7)

            mlp_half(0)
            split_hi(q_hi, q_raw, 2048, P, q_loaded, q_hi_done, f0.up, UP + 1, 8)
            copy_bias(L1.kv0)
            split_hi(kv_hi, kv_raw, 1024, P, kv_loaded, kv_hi_done, f0.lin, L1.kv0, 4)
            split_hi(o_hi, o_raw, 2048, P, o_loaded, o_hi_done, f0.down, DOWN + 1, 2 * NB)
            mlp_half(1)
            split_hi(q_hi, q_raw, 2048, P, q_loaded, q_hi_done, f0.up, L1.q0, 16)

            evac_kv(L1, S1, 0, range(4))
            evac_v(L1, S1, 0)
            norm_hi(N[2])
            act.wait_ge(f0.down, 3 * NB)
            attention(L1, S1, KT * RANK, 2048, 1024, 2048)
            norm_hi(N[3])
            act.wait_ge(f1.dve, 10)
            act.activation(lg[2][:, :, :], lg[1][:, :, :], ACT.Exp).then_inc(f1.exp, 1)
            act.wait_ge(f1.dve, 13 + NB + 1)
            act.activation(lg[4][:, :, :], lg[3][:, :, :], ACT.Exp, scale=-2.0).then_inc(f1.exp, 1)

        @block.gpsimd
        def _(pool):
            def split_lo(lo, raw, hi, n, rows, hi_done, done, at):
                pool.wait_ge(hi_done, at + 1)
                pool.tensor_tensor(lo[0:rows, 0:n], raw[0:rows, 0:n], hi[0:rows, 0:n].bitcast(F32), ALU.subtract)\
                    .then_inc(done, 1)

            def normalise(L, S, it, b):
                pool.wait_ge(S.rcp_done, it * NB + (b + 1))
                p = prob[:, b % 2, 0:G * L.keys].rearrange("p (g k) -> p g k", g=G)
                pool.tensor_tensor(p, p, exp_rcp[:, b % 2, :].unsqueeze(2).broadcast_to([P, G, L.keys]), ALU.mult)\
                    .then_inc(S.norm_done, 1)

            def head(L, S, it, next_kv, next_q):
                split_lo(o_lo, o_raw, o_hi, 2048, L.hd, o_hi_done, o_lo_done, it + L.o0)
                for b in range(NB):
                    normalise(L, S, it, b)
                    if b == 2:
                        split_lo(kv_lo, kv_raw, kv_hi, next_kv, P, kv_hi_done, kv_lo_done, it + (L.kv0 + 1))
                    if b == 5:
                        split_lo(q_lo, q_raw, q_hi, next_q, P, q_hi_done, q_lo_done, it + (L.q0 + 1))

            def attention(L, S, next_kv, next_q, own_kv, own_q):
                with pool.Fori(0, L.kv_heads - 1) as it:
                    head(L, S, it, own_kv, own_q)
                head(L, S, L.kv_heads - 1, next_kv, next_q)

            def rstd_of(n):
                for h in range(2):
                    pool.wait_ge(n.var, h + 1)
                    pool.tensor_tensor(rstd[:, 4 * h:4 * h + 4], var_eps[:, 4 * h:4 * h + 4],
                                       minus_half[:, 4 * h:4 * h + 4], ALU.pow).then_inc(n.rstd, 1)

            pool.memset(minus_half[:, :], -0.5).then_inc(pool_set, 1)
            pool.wait_ge(pool_set, 1)
            rstd_of(N[0])
            split_lo(kv_lo, kv_raw, kv_hi, 768, P, kv_hi_done, kv_lo_done, 0)
            for k in range(KT):
                pool.wait_ge(c_hi_done, k + 1)
                pool.tensor_tensor(cT_lo[:, k, :], qT[:, k, :], cT_hi[:, k, :].bitcast(F32), ALU.subtract)\
                    .then_inc(c_lo_done, 1)
            pool.wait_ge(f0.gate_split_hi, 1)
            pool.tensor_tensor(gate_lo[:, :, :], gate_raw[:, :, :], gate_hi[:, :, :].bitcast(F32), ALU.subtract)\
                .then_inc(f0.gate_split_lo, 1)
            split_lo(q_lo, q_raw, q_hi, 1536, P, q_hi_done, q_lo_done, 0)
            attention(L0, S0, 1024, 512, 768, 1536)

            rstd_of(N[1])
            split_lo(o_lo, o_raw, o_hi, 1024, P, o_hi_done, o_lo_done, FC2)
            pool.wait_ge(ffn0_loaded, 32)
            pool.wait_ge(N[1].xn, NB)
            for b in range(NB):
                pool.tensor_tensor(x[:, b, :], x[:, b, :], beta[:, :], ALU.add).then_inc(f0.beta_added, 1)
            split_lo(q_lo, q_raw, q_hi, 2048, P, q_hi_done, q_lo_done, UP)
            split_lo(o_lo, o_raw, o_hi, 2048, P, o_hi_done, o_lo_done, DOWN)

            def mlp_half(hf):
                for u in range(8):
                    pool.wait_ge(f0.relu, hf * 8 + (u + 1))
                    if hf or u >= 2:
                        pool.wait_ge(f0.h_lo, hf * 8 + (u - 1))
                    pool.tensor_tensor(h_f[:, u % 2, :], relu[:, u % 2, :], relu[:, u % 2, :], ALU.mult)\
                        .then_inc(f0.sq, 1)

            mlp_half(0)
            split_lo(q_lo, q_raw, q_hi, 2048, P, q_hi_done, q_lo_done, UP + 1)
            split_lo(kv_lo, kv_raw, kv_hi, 1024, P, kv_hi_done, kv_lo_done, L1.kv0)
            split_lo(o_lo, o_raw, o_hi, 2048, P, o_hi_done, o_lo_done, DOWN + 1)
            mlp_half(1)
            split_lo(q_lo, q_raw, q_hi, 2048, P, q_hi_done, q_lo_done, L1.q0)
            rstd_of(NA)
            for b in range(NB):
                pool.wait_ge(NA.xn, b + 1)
                pool.tensor_tensor(acc[:, b, :], acc[:, b, :], gamma[:, :], ALU.mult).then_inc(f0.scaled, 1)
            rstd_of(N[2])
            pool.wait_ge(bo_loaded, 16)
            pool.wait_ge(N[2].xn, NB)
            for b in range(NB):
                pool.tensor_tensor(x[:, b, :], x[:, b, :], bo_bc[:, :], ALU.add).then_inc(bo_added, 1)
            attention(L1, S1, KT * RANK, 2048, 1024, 2048)
            rstd_of(N[3])
            pool.wait_ge(ffn1_loaded, 80)
            pool.wait_ge(N[3].xn, NB)
            for b in range(NB):
                pool.tensor_tensor(x[:, b, :], x[:, b, :], b_bc[:, :], ALU.add).then_inc(f1.b_added, 1)
            pool.wait_ge(f1.dve, 1)
            pool.partition_all_reduce(allmax[:, :], absmax[:, :], P, RMAX).then_inc(f1.allmax, 1)

        @block.vector
        def _(dve):
            def evac_projection(L, S, dst, bank, done, col):
                dve.wait_ge(S.proj_done, done)
                if L.bias:
                    dve.tensor_scalar(dst, work[0:L.hd, bank, :], bias_now[:, col:col + 1], None, ALU.add)\
                        .then_inc(S.dve_evac, 1)
                else:
                    dve.tensor_copy(dst, work[0:L.hd, bank, :]).then_inc(S.dve_evac, 1)

            def evac_kv(L, S, it, uses):
                for u in uses:
                    if u % 2 == 1:
                        src, is_v = u // 4, u // 2 % 2
                        dst = (vT[0:L.hd, src * TOK + HALF:(src + 1) * TOK] if is_v else
                               kT[0:L.hd, 0:NB * L.keys].rearrange("p (b s k) -> p b s k", b=NB, k=P)[:, 4:8, src, :])
                        evac_projection(L, S, dst, u % 4, L.proj_kv(it, u), G + is_v)

            def evac_v(L, S, it):
                for g in range(L.v_groups):
                    dve.wait_ge(S.v_hi_done, it * L.v_groups + (g + 1))
                    at = slice(8 * g * L.hd, 8 * (g + 1) * L.hd)
                    dve.tensor_tensor(v_lo[:, at].rearrange("p (j d) -> p j d", d=L.hd),
                                      pt[:, :, :].rearrange("p a (j d) -> p (a j) d", d=P)[:, :, 0:L.hd],
                                      v_hi[:, at].bitcast(F32).rearrange("p (j d) -> p j d", d=L.hd),
                                      ALU.subtract).then_inc(S.v_lo_done, 1)

            def add_y(L, S, it, b):
                dve.wait_ge(S.y_done, it * NB + (b + 1))
                dve.tensor_tensor(x[:, b, :], x[:, b, :], yb[:, :], ALU.add).then_inc(S.y_added, 1)

            def head(L, S, it, last):
                for u in range(1, L.q_uses, 2):
                    half, g = u // G, u % G
                    evac_projection(L, S, qT[0:L.hd, g, half * HALF:(half + 1) * HALF], u % 4, L.proj_q(it, u), g)
                for i in range(NB + 3):
                    if i < NB:
                        dve.wait_ge(S.scores_done, it * NB + (i + 1))
                        bank = (L.q_uses + i * L.score_banks) % 4
                        s = work[:, bank:bank + L.score_banks, :].rearrange("p a (g k) -> p (a g) k", k=L.keys)
                        dve.tensor_reduce(neg_max_raw[:, i % 2, :], s, AX.X, ALU.max, negate=True)\
                            .then_inc(S.max_raw, 1)
                        dve.wait_ge(S.max_raw, it * NB + (i + 1))
                        dve.tensor_scalar(neg_max[:, i % 2, :], neg_max_raw[:, i % 2, :], L.scale, None, ALU.mult)\
                            .then_inc(S.max_done, 1)
                    elif not last and i < NB + 2:
                        evac_kv(L, S, it + 1, range((i - NB) * L.kv_uses // 2, (i - NB + 1) * L.kv_uses // 2))
                    if 2 <= i < NB + 2:
                        b = i - 2
                        dve.wait_ge(S.pt_hi_done, it * NB + (b + 1))
                        dve.tensor_tensor(pT_lo[:, 0:L.sources, :], pt[:, 0:L.sources, :],
                                          pT_hi[:, 0:L.sources, :].bitcast(F32), ALU.subtract)\
                            .then_inc(S.pt_lo_done, 1)
                    if i < NB:
                        dve.wait_ge(S.exp_done, it * (NB * L.score_banks) + (i + 1) * L.score_banks)
                        dve.reciprocal(exp_rcp[:, i % 2, :], exp_sum[:, i % 2, :]).then_inc(S.rcp_done, 1)
                    if i >= 3:
                        add_y(L, S, it, i - 3)
                    if 2 <= i < NB + 2:
                        dve.wait_ge(S.o_hi_done, it * NB + (b + 1))
                        dve.tensor_tensor(oT_lo[0:L.hd, :, :], ov[0:L.hd, :].rearrange("p (g q) -> p g q", g=G),
                                          oT_hi[0:L.hd, :, :].bitcast(F32), ALU.subtract).then_inc(S.o_lo_done, 1)
                if not last:
                    evac_v(L, S, it + 1)

            def attention(L, S):
                with dve.Fori(0, L.kv_heads - 1) as it:
                    head(L, S, it, False)
                head(L, S, L.kv_heads - 1, True)

            def statistics(n, src, ready):
                for b in range(NB):
                    ready(b)
                    dve.bn_stats(stats[:, b, :], src[:, b, :]).then_inc(n.stat, 1)
                for b in range(NB):
                    dve.wait_ge(n.stat, NB if b == 0 else NB + b)
                    dve.bn_aggr(mean_var[:, b, :], stats[:, b, :]).then_inc(n.stat, 1)
                dve.wait_ge(n.stat, 2 * NB)
                for h in range(2):
                    dve.tensor_scalar(var_eps[:, 4 * h:4 * h + 4], mean_var[:, 4 * h:4 * h + 4, 1], LN_EPS, None, ALU.add)\
                        .then_inc(n.var, 1)

            def norm_one(n, b, dst, src):
                dve.wait_ge(n.rstd, b // 4 + 1)
                dve.tensor_scalar(dst, src, mean_var[:, b, 0:1], rstd[:, b:b + 1], ALU.subtract, ALU.mult)\
                    .then_inc(n.xn, 1)

            def norm_lo(n, b):
                dve.wait_ge(n.hi, b + 1)
                dve.tensor_tensor(xT_lo[:, :, b * P:(b + 1) * P], work[:, b % 4, :].rearrange("p (k t) -> p k t", k=KT),
                                  xT_hi[:, :, b * P:(b + 1) * P].bitcast(F32), ALU.subtract).then_inc(n.lo, 1)

            def norm_split(n):
                for b in range(NB):
                    if b >= 2:
                        dve.wait_ge(n.t, b - 1)
                    norm_one(n, b, xn[:, b % 2, :], x[:, b, :])
                    if b:
                        norm_lo(n, b - 1)
                norm_lo(n, NB - 1)

            statistics(N[0], x, lambda b: dve.wait_ge(x_loaded[b // 4], 16))
            evac_kv(L0, S0, 0, range(4))
            norm_split(N[0])
            evac_kv(L0, S0, 0, range(4, 8))
            evac_v(L0, S0, 0)
            attention(L0, S0)

            statistics(N[1], x, lambda b: dve.wait_ge(S0.y_added, (L0.kv_heads - 1) * NB + b + 1))
            norm_split(N[1])
            dve.wait_ge(f0.gate, 1)
            for b in range(NB):
                dve.max(top8[:, b, :], pt[:, 0, b * NE:(b + 1) * NE]).then_inc(f0.route_top, 1)
            dve.wait_ge(f0.route_top, NB)
            dve.tensor_tensor(route[:, :], top8[:, :, 0], top8[:, :, 1], ALU.add).then_inc(f0.route, 1)
            for u in range(8):
                half, m = u // 2 % 2, u % 2
                dve.wait_ge(f0.lin_hi, u + 1)
                at = (slice(None), (u // 4) * 2 + m, slice(half * HALF, (half + 1) * HALF))
                dve.tensor_tensor(h_lo[at], work[:, u % 4, :], h_hi[at].bitcast(F32), ALU.subtract)\
                    .then_inc(f0.lin_lo, 1)
            dve.wait_ge(f0.route, 1)
            for b in range(NB):
                dve.wait_ge(f0.down, b + 1)
                dve.tensor_scalar(acc[:, b, :], y2[b % 2][:, :], route[:, b:b + 1], None, ALU.mult)\
                    .then_inc(f0.added, 1)

            def mlp_half(hf):
                for u in range(8):
                    half, m = u // 4, u % 4
                    dve.wait_ge(f0.h_hi, hf * 8 + (u + 1))
                    at = (slice(None), m, slice(half * HALF, (half + 1) * HALF))
                    dve.tensor_tensor(h_lo[at], h_f[:, u % 2, :], h_hi[at].bitcast(F32), ALU.subtract)\
                        .then_inc(f0.h_lo, 1)
                for b in range(NB):
                    dve.wait_ge(f0.down, hf * 8 + (NB + b + 1))
                    dve.wait_ge(f0.added, hf * 8 + (b + 1))
                    dve.tensor_tensor(acc[:, b, :], acc[:, b, :], y2[b % 2][:, :], ALU.add).then_inc(f0.added, 1)

            with dve.Fori(0, 2) as hf:
                mlp_half(hf)
            evac_kv(L1, S1, 0, range(4))
            statistics(NA, acc, lambda b: dve.wait_ge(f0.added, 2 * NB + b + 1))
            for b in range(NB):
                norm_one(NA, b, acc[:, b, :], acc[:, b, :])
            evac_v(L1, S1, 0)
            for b in range(NB):
                dve.wait_ge(f0.scaled, b + 1)
                dve.wait_ge(f0.beta_added, b + 1)
                dve.tensor_tensor(x[:, b, :], x[:, b, :], acc[:, b, :], ALU.add).then_inc(f0.added, 1)

            statistics(N[2], x, lambda b: dve.wait_ge(f0.added, 3 * NB + b + 1))
            norm_split(N[2])
            dve.wait_ge(bo_added, NB)
            attention(L1, S1)

            statistics(N[3], x, lambda b: dve.wait_ge(S1.y_added, (L1.kv_heads - 1) * NB + b + 1))
            norm_split(N[3])
            for half in range(2):
                dve.wait_ge(f1.z, half + 1)
                dve.tensor_copy(zT[:, half * HALF:(half + 1) * HALF], work[0:RANK, half, :]).then_inc(f1.z_evac, 1)
            dve.wait_ge(f1.small, 1)
            dve.wait_ge(ffn1_loaded, 80)
            flat = lambda t: t.rearrange("p b e -> p (b e)")
            dve.tensor_tensor(hd_raw[:, 0, :, :], work[:, 2, 0:NB * NE].rearrange("p (b e) -> p b e", e=NE),
                              b_bc[:, 0:NE].unsqueeze(1).broadcast_to([P, NB, NE]), ALU.add)\
                .then_inc(f1.small_evac, 1)
            dve.tensor_copy(hd_raw[:, 1, :, :], work[:, 3, 0:NB * NE].rearrange("p (b e) -> p b e", e=NE))\
                .then_inc(f1.small_evac, 1)

            def add_h(b):
                dve.wait_ge(f1.H, b + 1)
                dve.wait_ge(f1.b_added, b + 1)
                dve.tensor_tensor(x[:, b, :], x[:, b, :], y2[b % 2][:, :], ALU.add).then_inc(f1.H_added, 1)

            add_h(0)
            dve.wait_ge(f1.picked, 1)
            both = pt[:, 0, 0:2 * NB * NE].rearrange("p (a e) -> p a e", a=2)
            dve.tensor_reduce(absmax[:, :], both, AX.X, ALU.max, apply_absolute_value=True).then_inc(f1.dve, 1)
            dve.tensor_copy(hd[:, :, :, :].rearrange("p a b e -> p (a b e)"), pt[:, 0, 0:2 * NB * NE]).then_inc(f1.dve, 1)
            add_h(1)
            step = [2]

            def chained(ins):
                ins.then_inc(f1.dve, 1)
                step[0] += 1
                dve.wait_ge(f1.dve, step[0])

            def per_row(r):
                return r[:, :].unsqueeze(2).broadcast_to([P, NB, NE])

            dve.wait_ge(f1.allmax, 1)
            chained(dve.tensor_scalar(row[0][:, 0:2], allmax[:, :], 1e-6, None, ALU.max))
            chained(dve.reciprocal(row[1][:, 0:2], row[0][:, 0:2]))
            chained(dve.tensor_scalar(row[2][:, 0:2], row[1][:, 0:2], 0.5, None, ALU.mult))
            chained(dve.tensor_scalar(lg[0][:, :, :], hd[:, 0, :, :], row[2][:, 0:1], None, ALU.mult))
            chained(dve.scalar_tensor_tensor(out=lg[7][:, :, :], in0=hd[:, 1, :, :], scalar=row[2][:, 1:2],
                                             in1=lg[0][:, :, :], op0=ALU.mult, op1=ALU.add))
            chained(dve.tensor_reduce(row[3][:, :], lg[7][:, :, :], AX.X, ALU.max))
            chained(dve.tensor_tensor(lg[1][:, :, :], lg[7][:, :, :], per_row(row[3]), ALU.subtract))
            chained(dve.tensor_scalar(lg[1][:, :, :], lg[1][:, :, :], 1.0, None, ALU.mult))
            assert step[0] == 10
            add_h(2)
            dve.wait_ge(f1.exp, 1)
            chained(dve.tensor_reduce(row[4][:, :], lg[2][:, :, :], AX.X, ALU.add))
            chained(dve.reciprocal(row[5][:, :], row[4][:, :]))
            chained(dve.tensor_tensor(lg[6][:, :, :], lg[2][:, :, :], per_row(row[5]), ALU.mult))
            for b in range(NB):
                chained(dve.max(top8b[:, b, :], lg[6][:, b, :]))
            chained(dve.tensor_tensor(lg[3][:, :, :], lg[6][:, :, :],
                                      top8b[:, :, 1:2].broadcast_to([P, NB, NE]), ALU.subtract))
            assert step[0] == 13 + NB + 1
            add_h(3)
            dve.wait_ge(f1.exp, 2)
            chained(dve.tensor_scalar(lg[0][:, :, :], lg[4][:, :, :], 1.0, None, ALU.add))
            chained(dve.reciprocal(lg[1][:, :, :], lg[0][:, :, :]))
            chained(dve.tensor_tensor(lg[2][:, :, :], lg[1][:, :, :], lg[6][:, :, :], ALU.mult))
            chained(dve.tensor_reduce(row[0][:, :], lg[2][:, :, :], AX.X, ALU.add))
            chained(dve.tensor_scalar(row[1][:, :], row[0][:, :], 1e-9, None, ALU.add))
            chained(dve.reciprocal(row[2][:, :], row[1][:, :]))
            dve.tensor_tensor(lg[5][:, :, :], lg[2][:, :, :], per_row(row[2]), ALU.mult).then_inc(f1.w, 1)
            for b in range(4, NB):
                add_h(b)
            dve.wait_ge(f1.wT, 1)
            dve.tensor_copy(wT[:, :].rearrange("p (a t) -> p a t", a=2), work[0:NE, 0:2, :]).then_inc(f1.wT_evac, 1)
            dve.wait_ge(f1.pmix, 1)
            for half in range(2):
                at = slice(half * HALF, (half + 1) * HALF)
                dve.scalar_tensor_tensor(out=zp[:, at], in0=zT[:, at], scalar=0.5, in1=work[0:RANK, 2 + half, :],
                                         op0=ALU.mult, op1=ALU.mult).then_inc(f1.zp, 1)
            for b in range(NB):
                dve.wait_ge(f1.delta, b + 1)
                dve.wait_ge(f1.H_added, b + 1)
                dve.tensor_tensor(x[:, b, :], x[:, b, :], y2[b % 2][:, :], ALU.add).then_inc(f1.done, 1)


def laid_out(i):
    def tiles(w):
        return w.reshape(-1, P, w.shape[-1]).transpose(1, 0, 2).reshape(P, -1)

    def rows(v):
        return np.broadcast_to(v, (P, v.shape[0]))

    wq, wk, wv, wo = (i[f"L0_xattn_W{n}"] for n in "qkvo")
    per_head = lambda w: w.reshape(4, -1, KT, P).transpose(0, 3, 2, 1)
    a = {
        "x": i["x"],
        "ctxT": i["ctx_4096"].reshape(TOK, KT, P).transpose(2, 1, 0),
        "l0_q": per_head(wq).reshape(4, P, -1),
        "l0_kv": np.concatenate([per_head(wk), per_head(wv)], 3).reshape(4, P, -1),
        "l0_o": wo.reshape(HID, 4, G, 96).transpose(1, 3, 2, 0).reshape(4, 96, -1),
        "gate": i["L0_ffn_gate_w"].reshape(KT, P, NE).transpose(1, 0, 2),
        "up": i["L0_ffn_up_w"].reshape(KT, P, 2, HID).transpose(2, 1, 0, 3).reshape(2, P, -1),
        "down": i["L0_ffn_down_w"].reshape(2, 4, P, HID).transpose(0, 2, 1, 3).reshape(2, P, -1),
        "fc1": tiles(i["L0_ffn_fc1_w"]), "expert": tiles(i["L0_ffn_expert_w"]), "fc2": tiles(i["L0_ffn_fc2_w"]),
        "gamma": rows(i["L0_ffn_ln_gamma"]), "beta": rows(i["L0_ffn_ln_beta"]),
    }
    heads = lambda w, n: w.reshape(KT, P, 8, n).transpose(2, 1, 0, 3)
    wkv, bkv = i["L1_xattn_Wkv"], i["L1_xattn_bkv"]
    a["l1_q"] = heads(i["L1_xattn_Wq"], G * P).reshape(8, P, -1)
    w = np.concatenate([heads(wkv[:, :1024], P), heads(wkv[:, 1024:], P)], 3).reshape(8, P, -1)
    bq = i["L1_xattn_bq"].reshape(8, G, P).transpose(0, 2, 1)
    bk, bv = bkv[:1024].reshape(8, P, 1), bkv[1024:].reshape(8, P, 1)
    a["l1_kv"] = np.concatenate([w, bq, bk, bv], 2)
    a["l1_o"] = i["L1_xattn_Wo"].reshape(8, G, P, HID).transpose(0, 2, 1, 3).reshape(8, P, -1)
    a["bo"] = rows(i["L1_xattn_bo"])
    a["W"] = i["L1_ffn_W"].reshape(HID, KT, P).transpose(2, 1, 0).reshape(P, -1)
    a["A"] = tiles(i["L1_ffn_A"])
    a["b"], a["Bmat"] = rows(i["L1_ffn_b"]), i["L1_ffn_Bmat"]
    a["LiMEs"], a["LiMEsT"] = i["L1_ffn_LiMEs"], i["L1_ffn_LiMEs"].T
    a["ident"] = np.eye(P, dtype=np.float32)
    a["odd_rows"] = np.eye(P, dtype=np.float32)[:, np.arange(P) | 1]
    return {n: np.ascontiguousarray(v) for n, v in a.items()}


def kernel(**inputs):
    import concourse.bacc as bacc
    from concourse.bass_utils import run_bass_kernel_spmd

    nc = bacc.Bacc("TRN2", target_bir_lowering=False, num_devices=1)
    arrays = laid_out({n: np.asarray(v) for n, v in inputs.items()})
    aps = {n: nc.dram_tensor(f"in_{n}", v.shape, mybir.dt.from_np(v.dtype), kind="ExternalInput").ap()
           for n, v in arrays.items()}
    out = nc.dram_tensor("out_0", (NB, P, HID), F32, kind="ExternalOutput").ap()
    build_program(nc, aps, out)
    result = run_bass_kernel_spmd(nc, [{f"in_{n}": v for n, v in arrays.items()}], core_ids=[0])
    return result.results[0]["out_0"]
```

```python
from contextlib import ExitStack

import numpy as np

import concourse.bass as bass
from concourse import mybir

F32 = mybir.dt.float32
F32R = mybir.dt.float32r
ALU = mybir.AluOpType
ACT = mybir.ActivationFunctionType
AX = mybir.AxisListType
RMAX = bass.bass_isa.ReduceOp.max

P = 128
NB = 8
HID = 512
KT = HID // P
TOK = NB * P
HALF = TOK // 2
G = 4
NE = 8
RANK = 32
LN_EPS = 1e-5


class Attention:

    def __init__(self, name, kv_heads, hd, sources, bias, kv0, q0, o0):
        self.name, self.kv_heads, self.hd, self.sources, self.bias = name, kv_heads, hd, sources, bias
        self.kv0, self.q0, self.o0 = kv0, q0, o0
        self.keys = sources * P
        self.scale = float(1.0 / np.sqrt(hd))
        self.score_banks = self.keys * G // 512
        self.q_uses = G * 2
        self.kv_uses = sources * 4
        self.proj = self.q_uses + self.kv_uses
        self.evacs = self.proj // 2
        self.v_groups = sources
        self.double = sources == 1
        self.q_steps = [(4, 5), (), (6, 7)] if sources == 2 else [(4,), (5,), (6, 7)]
        n = self.kv_uses
        self.kv_steps = [range(n // 2), range(n // 2, n * 3 // 4), range(n * 3 // 4, n)]
        order = [("q", u) for u in range(4)]
        for b in range(NB):
            if b == 2:
                order += [("q", u) for u in self.q_steps[2]]
            order += [("s", b)] * self.score_banks
            if b < 2:
                order += [("q", u) for u in self.q_steps[b]]
        order += [("kv", u) for u in range(n)]
        assert len(order) % 4 == 0
        self.order = order
        self.bank = {use: order.index(use) % 4 for use in order}

    def proj_q(self, it, u):
        return self.kv_uses + it * self.proj + u + 1

    def proj_kv(self, it, u):
        return it * self.proj + u + 1

    def evac_q(self, it, u):
        return self.kv_uses // 2 + it * self.evacs + u // 2 + 1

    def evac_kv(self, it, u):
        return it * self.evacs + u // 2 + 1

    def wait_bank(self, pe, S, it, kind, n, q_drained=-1):
        first = self.order.index((kind, n))
        for at in range(first, first + (self.score_banks if kind == "s" else 1)):
            before, m = self.order[at - 4]
            if before == "q" and m > q_drained:
                pe.wait_ge(S.act_evac if m % 2 == 0 else S.dve_evac, self.evac_q(it, m))
            if before == "kv":
                pe.wait_ge(S.act_evac if m % 2 == 0 else S.dve_evac, self.evac_kv(it, m))
        before, m = self.order[at - 4]
        if before == "s":
            nth = m * self.score_banks + (at - 4 - self.order.index((before, m))) + 1
            pe.wait_ge(S.exp_done, it * (NB * self.score_banks) + nth)


class AttentionSems:

    def __init__(self, sem, prefix):
        self.proj_done = sem(f"{prefix}_proj_done")
        self.act_evac = sem(f"{prefix}_act_evac")
        self.dve_evac = sem(f"{prefix}_dve_evac")
        self.scores_done = sem(f"{prefix}_scores_done")
        self.max_raw = sem(f"{prefix}_max_raw")
        self.max_done = sem(f"{prefix}_max_done")
        self.exp_done = sem(f"{prefix}_exp_done")
        self.rcp_done = sem(f"{prefix}_rcp_done")
        self.norm_done = sem(f"{prefix}_norm_done")
        self.pt_done = sem(f"{prefix}_pt_done")
        self.pt_hi_done = sem(f"{prefix}_pt_hi_done")
        self.pt_lo_done = sem(f"{prefix}_pt_lo_done")
        self.pv_done = sem(f"{prefix}_pv_done")
        self.o_hi_done = sem(f"{prefix}_o_hi_done")
        self.o_lo_done = sem(f"{prefix}_o_lo_done")
        self.y_done = sem(f"{prefix}_y_done")
        self.y_added = sem(f"{prefix}_y_added")
        self.vt_done = sem(f"{prefix}_vt_done")
        self.v_hi_done = sem(f"{prefix}_v_hi_done")
        self.v_lo_done = sem(f"{prefix}_v_lo_done")


class NormSems:

    def __init__(self, sem, prefix, bufs):
        self.bufs = bufs
        self.stat = sem(f"{prefix}_stat")
        self.var = sem(f"{prefix}_var")
        self.pool = sem(f"{prefix}_pool")
        self.rstd = sem(f"{prefix}_rstd")
        self.xn = sem(f"{prefix}_xn")
        self.t = sem(f"{prefix}_t")
        self.hi = sem(f"{prefix}_hi")
        self.lo = sem(f"{prefix}_lo")


class Ffn0Sems:

    def __init__(self, sem, prefix):
        self.gate_split_hi = sem(f"{prefix}_gate_split_hi")
        self.gate_split_lo = sem(f"{prefix}_gate_split_lo")
        self.gate = sem(f"{prefix}_gate")
        self.route_top = sem(f"{prefix}_route_top")
        self.route = sem(f"{prefix}_route")
        self.lin = sem(f"{prefix}_lin")
        self.lin_hi = sem(f"{prefix}_lin_hi")
        self.lin_lo = sem(f"{prefix}_lin_lo")
        self.up = sem(f"{prefix}_up")
        self.relu = sem(f"{prefix}_relu")
        self.sq = sem(f"{prefix}_sq")
        self.h_hi = sem(f"{prefix}_h_hi")
        self.h_lo = sem(f"{prefix}_h_lo")
        self.down = sem(f"{prefix}_down")
        self.added = sem(f"{prefix}_added")
        self.scaled = sem(f"{prefix}_scaled")
        self.x_done = sem(f"{prefix}_x_done")
        self.beta_added = sem(f"{prefix}_beta_added")


class Ffn1Sems:

    def __init__(self, sem, prefix):
        self.z = sem(f"{prefix}_z")
        self.z_evac = sem(f"{prefix}_z_evac")
        self.small = sem(f"{prefix}_small")
        self.small_evac = sem(f"{prefix}_small_evac")
        self.picked = sem(f"{prefix}_picked")
        self.dve = sem(f"{prefix}_dve")
        self.allmax = sem(f"{prefix}_allmax")
        self.exp = sem(f"{prefix}_exp")
        self.w = sem(f"{prefix}_w")
        self.wT = sem(f"{prefix}_wT")
        self.wT_evac = sem(f"{prefix}_wT_evac")
        self.pmix = sem(f"{prefix}_pmix")
        self.zp = sem(f"{prefix}_zp")
        self.H = sem(f"{prefix}_H")
        self.H_added = sem(f"{prefix}_H_added")
        self.delta = sem(f"{prefix}_delta")
        self.done = sem(f"{prefix}_done")
        self.b_added = sem(f"{prefix}_b_added")


def build_program(nc, A, out):
    L0 = Attention("L0", 4, 96, 2, False, kv0=0, q0=0, o0=0)
    L1 = Attention("L1", 8, 128, 1, True, kv0=5, q0=7, o0=7)
    FC1 = L0.kv_heads
    EXPERT = L0.kv_heads
    UP = EXPERT + 1
    FC2 = L0.kv_heads
    DOWN = FC2 + 1
    F1_A = L1.kv0 + L1.kv_heads
    F1_W = L1.q0 + L1.kv_heads

    with ExitStack() as ctx:
        def sb(name, shape, dt=F32, stack=ctx):
            return stack.enter_context(nc.sbuf_tensor(name, shape, dt))

        def sem(name):
            return ctx.enter_context(nc.semaphore(name))

        x = sb("x", [P, NB, HID])
        xT_hi = sb("xT_hi", [P, KT, TOK], F32R)
        xT_lo = sb("xT_lo", [P, KT, TOK], F32R)
        cT_hi = sb("cT_hi", [P, KT, TOK], F32R)
        cT_lo = sb("cT_lo", [P, KT, TOK], F32R)
        kv_raw = sb("kv_raw", [P, 1032])
        q_raw = sb("q_raw", [P, 2048])
        o_raw = sb("o_raw", [P, 2048])
        kv_hi, kv_lo = sb("kv_hi", [P, 1024], F32R), sb("kv_lo", [P, 1024], F32R)
        q_hi, q_lo = sb("q_hi", [P, 2048], F32R), sb("q_lo", [P, 2048], F32R)
        o_hi, o_lo = sb("o_hi", [P, 2048], F32R), sb("o_lo", [P, 2048], F32R)
        ident = sb("ident", [P, P])
        bias_now = sb("bias_now", [P, 8])
        stats = sb("stats", [P, NB, 6])
        mean_var = sb("mean_var", [P, NB, 2])
        var_eps = sb("var_eps", [P, NB])
        rstd = sb("rstd", [P, NB])
        minus_half = sb("minus_half", [P, 1])
        minus_one = sb("minus_one", [P, 1])
        minus_mean = sb("minus_mean", [P, NB])
        neg_max_raw = sb("neg_max_raw", [P, 2, G])
        neg_max = sb("neg_max", [P, 2, G])
        exp_sum = sb("exp_sum", [P, 2, G])
        exp_rcp = sb("exp_rcp", [P, 2, G])
        gate_raw = sb("gate_raw", [P, KT, NE])
        gate_hi, gate_lo = sb("gate_hi", [P, KT, NE], F32R), sb("gate_lo", [P, KT, NE], F32R)
        top8 = sb("top8", [P, NB, 8])
        route = sb("route", [P, NB])
        with ExitStack() as st:
            qT = sb("qT", [P, G, TOK], stack=st)
            kT = sb("kT", [P, NB * 2 * P], stack=st)
            vT = sb("vT", [P, 2 * TOK], stack=st)
            prob = sb("prob", [P, 2, G * 2 * P], stack=st)
            pT_hi, pT_lo = sb("pT_hi", [P, 2, 512], F32R, st), sb("pT_lo", [P, 2, 512], F32R, st)
            v_hi, v_lo = sb("v_hi", [P, 16 * 96], F32R, st), sb("v_lo", [P, 16 * 96], F32R, st)
            oT_hi, oT_lo = sb("oT_hi", [P, G, P], F32R, st), sb("oT_lo", [P, G, P], F32R, st)
            bo_bc = sb("bo_bc", [P, HID], stack=st)
        with ExitStack() as st:
            h_hi, h_lo = sb("h_hi", [P, KT, TOK], F32R, st), sb("h_lo", [P, KT, TOK], F32R, st)
            acc = sb("acc", [P, NB, HID], stack=st)
            relu = sb("relu", [P, 2, HALF], stack=st)
            gamma = sb("gamma", [P, HID], stack=st)
            h_f = sb("h_f", [P, 2, HALF], stack=st)
            beta = sb("beta", [P, HID], stack=st)
        with ExitStack() as st:
            zT = sb("zT", [RANK, TOK], stack=st)
            zp = sb("zp", [RANK, TOK], stack=st)
            wT = sb("wT", [NE, TOK], stack=st)
            b_mat = sb("b_mat", [RANK, HID], stack=st)
            limes = sb("limes", [NE, RANK], stack=st)
            limesT = sb("limesT", [RANK, NE], stack=st)
            b_bc = sb("b_bc", [P, HID], stack=st)
            odd_rows = sb("odd_rows", [P, P], stack=st)
            hd_raw = sb("hd_raw", [P, 2, NB, NE], stack=st)
            hd = sb("hd", [P, 2, NB, NE], stack=st)
            absmax = sb("absmax", [P, 2], stack=st)
            allmax = sb("allmax", [P, 2], stack=st)
            lg = [sb(f"lg{i}", [P, NB, NE], stack=st) for i in range(8)]
            row = [sb(f"row{i}", [P, NB], stack=st) for i in range(6)]
            top8b = sb("top8b", [P, NB, 8], stack=st)

        work = ctx.enter_context(nc.psum_tensor("work", [P, 4, 512], F32))
        pt = ctx.enter_context(nc.psum_tensor("pt", [P, 2, 512], F32))
        ov = ctx.enter_context(nc.psum_tensor("ov", [P, 512], F32))
        yb = ctx.enter_context(nc.psum_tensor("yb", [P, 512], F32))
        y2 = [yb, ov]

        def o_buf(L, part, b):
            if L.double and b % 2:
                return (pT_hi, pT_lo)[part][:, 1, :].rearrange("p (g q) -> p g q", g=G)
            return (oT_hi, oT_lo)[part][:, :, :]

        def y_buf(L, b):
            return pt[:, 1, :] if L.double and b % 2 else yb[:, :]

        def xn_buf(n, b):
            if n.bufs == 2:
                return prob[:, b % 2, 0:HID] if n is N[0] else relu[:, b % 2, :]
            return vT[:, b % 4 * HID:(b % 4 + 1) * HID]

        x_loaded = [sem("x_loaded0"), sem("x_loaded1")]
        c_loaded = [sem(f"c_loaded{k}") for k in range(KT)]
        const_loaded = sem("const_loaded")
        ffn1_loaded = sem("ffn1_loaded")
        ffn0_loaded = sem("ffn0_loaded")
        bo_loaded = sem("bo_loaded")
        kv_loaded, kv_hi_done, kv_lo_done = sem("kv_loaded"), sem("kv_hi_done"), sem("kv_lo_done")
        q_loaded, q_hi_done, q_lo_done = sem("q_loaded"), sem("q_hi_done"), sem("q_lo_done")
        o_loaded, o_hi_done, o_lo_done = sem("o_loaded"), sem("o_hi_done"), sem("o_lo_done")
        c_hi_done, c_lo_done, c_lo_pool = sem("c_hi_done"), sem("c_lo_done"), sem("c_lo_pool")
        out_stored = sem("out_stored")
        pool_set = sem("pool_set")
        bias_copied = sem("bias_copied")

        S0, S1 = AttentionSems(sem, "L0"), AttentionSems(sem, "L1")

        N = [NormSems(sem, f"ln{i}", 2 if i in (0, 2) else 4) for i in range(4)]
        NA = NormSems(sem, "ln_acc", NB)
        f0 = Ffn0Sems(sem, "f0")
        bo_added = sem("bo_added")
        f1 = Ffn1Sems(sem, "f1")

        block = ctx.enter_context(nc.Block())

        @block.sync
        def _(sp):
            def load(raw, src, loaded, lo_done, n):
                sp.wait_ge(lo_done, n)
                sp.dma_start(raw, src).then_inc(loaded, 16)

            sp.dma_start(kv_raw[:, 0:768], A["l0_kv"][0]).then_inc(kv_loaded, 16)
            for k in range(KT):
                sp.dma_start(qT[:, k, :], A["ctxT"][:, k, :]).then_inc(c_loaded[k], 16)
            sp.dma_start(x[:, 0:4, :], A["x"][0:4].rearrange("b t d -> t b d")).then_inc(x_loaded[0], 16)
            sp.dma_start(ident[:, :], A["ident"]).then_inc(const_loaded, 16)
            sp.dma_start(gate_raw[:, :, :], A["gate"]).then_inc(const_loaded, 16)
            sp.dma_start(q_raw[:, 0:1536], A["l0_q"][0]).then_inc(q_loaded, 16)
            sp.dma_start(x[:, 4:8, :], A["x"][4:8].rearrange("b t d -> t b d")).then_inc(x_loaded[1], 16)
            sp.dma_start(o_raw[0:96, :], A["l0_o"][0]).then_inc(o_loaded, 16)
            sp.dma_start(bo_bc[:, :], A["bo"]).then_inc(bo_loaded, 16)
            with sp.Fori(1, L0.kv_heads) as it:
                load(kv_raw[:, 0:768], A["l0_kv"][it], kv_loaded, kv_lo_done, it)
                load(q_raw[:, 0:1536], A["l0_q"][it], q_loaded, q_lo_done, it)
                load(o_raw[0:96, :], A["l0_o"][it], o_loaded, o_lo_done, it)
            load(kv_raw[:, 0:1024], A["fc1"], kv_loaded, kv_lo_done, FC1)
            load(q_raw[:, 0:512], A["expert"], q_loaded, q_lo_done, EXPERT)
            load(o_raw[:, 0:1024], A["fc2"], o_loaded, o_lo_done, FC2)
            sp.wait_ge(S0.y_done, L0.kv_heads * NB)
            sp.wait_ge(S0.o_lo_done, L0.kv_heads * NB)
            sp.dma_start(gamma[:, :], A["gamma"]).then_inc(ffn0_loaded, 16)
            sp.dma_start(beta[:, :], A["beta"]).then_inc(ffn0_loaded, 16)
            load(q_raw[:, :], A["up"][0], q_loaded, q_lo_done, UP)
            load(o_raw[:, :], A["down"][0], o_loaded, o_lo_done, DOWN)
            load(q_raw[:, :], A["up"][1], q_loaded, q_lo_done, UP + 1)
            load(kv_raw[:, 0:1030], A["l1_kv"][0], kv_loaded, kv_lo_done, L1.kv0)
            load(o_raw[:, :], A["down"][1], o_loaded, o_lo_done, DOWN + 1)
            load(q_raw[:, :], A["l1_q"][0], q_loaded, q_lo_done, L1.q0)
            load(o_raw[:, :], A["l1_o"][0], o_loaded, o_lo_done, L1.o0)
            with sp.Fori(1, L1.kv_heads) as it:
                load(kv_raw[:, 0:1030], A["l1_kv"][it], kv_loaded, kv_lo_done, it + L1.kv0)
                load(q_raw[:, :], A["l1_q"][it], q_loaded, q_lo_done, it + L1.q0)
                load(o_raw[:, :], A["l1_o"][it], o_loaded, o_lo_done, it + L1.o0)
            load(kv_raw[:, 0:KT * RANK], A["A"], kv_loaded, kv_lo_done, F1_A)
            load(q_raw[:, :], A["W"], q_loaded, q_lo_done, F1_W)
            sp.wait_ge(S1.scores_done, L1.kv_heads * NB)
            for dst, src in ((b_mat, "Bmat"), (limes, "LiMEs"), (limesT, "LiMEsT"), (b_bc, "b"), (odd_rows, "odd_rows")):
                sp.dma_start(dst[:, :], A[src]).then_inc(ffn1_loaded, 16)
            for b in range(NB):
                sp.wait_ge(f1.done, b + 1)
                sp.dma_start(out[b], x[:, b, :]).then_inc(out_stored, 16)
            sp.wait_ge(out_stored, 16 * NB)

        @block.tensor
        def _(pe):
            def product(dst, pairs, first=True, last=True):
                n = len(pairs)
                for k, ((l_hi, l_lo), (r_hi, r_lo)) in enumerate(pairs):
                    pe.matmul(dst, l_hi, r_hi, start=first and k == 0, stop=False)
                    pe.matmul(dst, l_hi, r_lo, start=False, stop=False)
                    mm = pe.matmul(dst, l_lo, r_hi, start=False, stop=last and k == n - 1)
                return mm

            def weights(hi, lo, width, at, n):
                return [(hi[:, k * width + at:k * width + at + n], lo[:, k * width + at:k * width + at + n])
                        for k in range(KT)]

            def columns(hi, lo, at, n):
                return [(hi[:, k, at:at + n], lo[:, k, at:at + n]) for k in range(KT)]

            def project_kv(L, S, it, uses, bank_free=None):
                if uses[0] == 0:
                    pe.wait_ge(kv_lo_done, it + (L.kv0 + 1))
                for u in uses:
                    src, half, is_v = u // 4, u // 2 % 2, u % 2
                    hi, lo = (cT_hi, cT_lo) if src == 0 else (xT_hi, xT_lo)
                    if bank_free:
                        bank_free(u)
                    else:
                        L.wait_bank(pe, S, it - 1, "kv", u)
                    w = weights(kv_hi, kv_lo, 2 * L.hd, is_v * L.hd, L.hd)
                    product(work[0:L.hd, L.bank["kv", u], :], list(zip(w, columns(hi, lo, half * HALF, HALF))))\
                        .then_inc(S.proj_done, 1)

            def transpose_v(L, S, it, g):
                if g:
                    pe.wait_ge(S.v_lo_done, it * L.v_groups + g)
                elif L.double:
                    pe.wait_ge(S.dve_evac, L.evac_q(it, 1))
                else:
                    pe.wait_ge(S.dve_evac, L.evac_kv(it, L.kv_uses - 1))
                for j in range(8):
                    mm = pe.transpose(pt[:, j // 4, j % 4 * P:j % 4 * P + L.hd],
                                      vT[0:L.hd, (8 * g + j) * P:(8 * g + j + 1) * P], ident[0:L.hd, 0:L.hd])
                mm.then_inc(S.vt_done, 1)

            def project_q(L, S, it, uses):
                for u in uses:
                    if u == 0:
                        pe.wait_ge(q_lo_done, it + (L.q0 + 1))
                    half, g = u // G, u % G
                    L.wait_bank(pe, S, it, "q", u)
                    w = weights(q_hi, q_lo, G * L.hd, g * L.hd, L.hd)
                    product(work[0:L.hd, L.bank["q", u], :], list(zip(w, columns(xT_hi, xT_lo, half * HALF, HALF))))\
                        .then_inc(S.proj_done, 1)

            def scores(L, S, it, b):
                if b % 4 == 0:
                    pe.wait_ge(S.act_evac, L.evac_q(it, 4 * (b // 4) + 2))
                    pe.wait_ge(S.dve_evac, L.evac_q(it, 4 * (b // 4) + 3))
                L.wait_bank(pe, S, it, "s", b, 4 * (b // 4) + 3)
                bank = L.bank["s", b]
                dst = work[:, bank:bank + L.score_banks, :].rearrange("p a (g k) -> p (a g) k", k=L.keys)
                for g in range(G):
                    mm = pe.matmul(dst[:, g, :], qT[0:L.hd, g, b * P:(b + 1) * P],
                                   kT[0:L.hd, b * L.keys:(b + 1) * L.keys], start=True, stop=True)
                mm.then_inc(S.scores_done, 1)

            def transpose_p(L, S, it, b):
                pe.wait_ge(S.norm_done, it * NB + (b + 1))
                if b == 0:
                    pe.wait_ge(S.v_lo_done, (it + 1) * L.v_groups)
                for c in range(L.sources):
                    for g in range(G):
                        mm = pe.transpose(pt[:, c, g * P:(g + 1) * P],
                                          prob[:, b % 2, g * L.keys + c * P:g * L.keys + (c + 1) * P],
                                          ident[:, :])
                mm.then_inc(S.pt_done, 1)

            def values(L, S, it, b):
                pe.wait_ge(S.pt_lo_done, it * NB + (b + 1))
                if b:
                    pe.wait_ge(S.o_lo_done, it * NB + b)
                pairs = []
                for c in range(L.sources):
                    at = (c * NB + b) * L.hd
                    pairs.append(((v_hi[:, at:at + L.hd], v_lo[:, at:at + L.hd]),
                                  (pT_hi[:, c, :], pT_lo[:, c, :])))
                product(ov[0:L.hd, :], pairs).then_inc(S.pv_done, 1)

            def output(L, S, it, b, heads=range(G)):
                if heads[0] == 0:
                    if b == 0:
                        pe.wait_ge(o_lo_done, it + (L.o0 + 1))
                    before = 2 if L.double else 1
                    if b >= before:
                        pe.wait_ge(S.y_added, it * NB + (b + 1 - before))
                    pe.wait_ge(S.o_lo_done, it * NB + (b + 1))
                mm = product(y_buf(L, b), [((o_buf(L, 0, b)[0:L.hd, g, :], o_buf(L, 1, b)[0:L.hd, g, :]),
                                            (o_hi[0:L.hd, g * HID:(g + 1) * HID], o_lo[0:L.hd, g * HID:(g + 1) * HID]))
                                           for g in heads], heads[0] == 0, heads[-1] == G - 1)
                if heads[-1] == G - 1:
                    mm.then_inc(S.y_done, 1)

            def attention_head(L, S, it, norm=None):
                project_q(L, S, it, range(2))
                if L.v_groups == 2:
                    transpose_v(L, S, it, 0)
                project_q(L, S, it, range(2, 4))
                transpose_v(L, S, it, L.v_groups - 1)
                for i in range(NB + 3):
                    if i < 2:
                        scores(L, S, it, i)
                        project_q(L, S, it, L.q_steps[i])
                    elif i == 2:
                        transpose_p(L, S, it, 0)
                        project_q(L, S, it, L.q_steps[2])
                        scores(L, S, it, 2)
                        values(L, S, it, 0)
                    elif i < NB:
                        if L.double:
                            transpose_p(L, S, it, i - 2)
                            output(L, S, it, i - 3, (0, 1))
                            scores(L, S, it, i)
                            values(L, S, it, i - 2)
                            output(L, S, it, i - 3, (2, 3))
                        else:
                            scores(L, S, it, i)
                            transpose_p(L, S, it, i - 2)
                            output(L, S, it, i - 3)
                            values(L, S, it, i - 2)
                    else:
                        if norm is None:
                            project_kv(L, S, it + 1, L.kv_steps[i - NB])
                        if i < NB + 2:
                            transpose_p(L, S, it, i - 2)
                        if norm is not None:
                            if i == NB:
                                pe.wait_ge(S.exp_done, (it + 1) * (NB * L.score_banks))
                            transpose_x(norm, 2 * (i - NB))
                            transpose_x(norm, 2 * (i - NB) + 1)
                        output(L, S, it, i - 3)
                        if i < NB + 2:
                            values(L, S, it, i - 2)

            def attention(L, S, norm):
                with pe.Fori(0, L.kv_heads - 1) as it:
                    attention_head(L, S, it)
                attention_head(L, S, L.kv_heads - 1, norm)

            def transpose_x(n, b, bank_free=None):
                pe.wait_ge(n.xn, b + 1)
                if bank_free:
                    bank_free()
                elif b >= 4:
                    pe.wait_ge(n.lo, b - 3)
                for k in range(KT):
                    mm = pe.transpose(work[:, b % 4, k * P:(k + 1) * P], xn_buf(n, b)[:, k * P:(k + 1) * P],
                                      ident[:, :])
                mm.then_inc(n.t, 1)

            def drained(n):
                pe.wait_ge(n.lo, NB)

            pe.wait_ge(const_loaded, 32)
            pe.wait_ge(c_lo_done, 2)
            pe.wait_ge(c_lo_pool, 2)
            project_kv(L0, S0, 0, range(4), lambda u: None)
            for b in range(4):
                transpose_x(N[0], b, lambda: pe.wait_ge(S0.act_evac if b % 2 == 0 else S0.dve_evac,
                                                           L0.evac_kv(0, b)))
            pe.wait_ge(N[0].lo, 4)
            project_kv(L0, S0, 0, range(4, 6), lambda u: None)
            for b in range(4, 6):
                transpose_x(N[0], b, lambda: pe.wait_ge(S0.act_evac if b % 2 == 0 else S0.dve_evac,
                                                           L0.evac_kv(0, b)))
            for b in range(6, 8):
                transpose_x(N[0], b)
            drained(N[0])
            project_kv(L0, S0, 0, range(6, 8), lambda u: None)
            attention(L0, S0, N[1])

            def fc1(half):
                pe.wait_ge(kv_lo_done, FC1 + 1)
                for m in range(2):
                    bank = 2 * half + m
                    pe.wait_ge(N[1].lo, 5 + bank)
                    product(work[:, bank, :], list(zip(weights(kv_hi, kv_lo, 256, m * P, P),
                                                       columns(xT_hi, xT_lo, half * HALF, HALF)))).then_inc(f0.lin, 1)

            def expert(half):
                pe.wait_ge(q_lo_done, EXPERT + 1)
                pe.wait_ge(f0.lin_lo, 4 * half + 2)
                for m in range(2):
                    product(work[:, 2 * half + m, :],
                            [((q_hi[:, k * 256 + m * P:k * 256 + (m + 1) * P],
                               q_lo[:, k * 256 + m * P:k * 256 + (m + 1) * P]),
                              (h_hi[:, k, half * HALF:(half + 1) * HALF], h_lo[:, k, half * HALF:(half + 1) * HALF]))
                             for k in range(2)]).then_inc(f0.lin, 1)

            fc1(0)
            transpose_x(N[1], 6)
            transpose_x(N[1], 7)
            expert(0)
            drained(N[1])
            fc1(1)
            pe.wait_ge(f0.gate_split_lo, 1)
            for b in range(NB):
                mm = product(pt[:, 0, b * NE:(b + 1) * NE],
                             [((xT_hi[:, k, b * P:(b + 1) * P], xT_lo[:, k, b * P:(b + 1) * P]),
                               (gate_hi[:, k, :], gate_lo[:, k, :])) for k in range(KT)])
            mm.then_inc(f0.gate, 1)
            expert(1)
            pe.wait_ge(o_lo_done, FC2 + 1)
            for b in range(NB):
                pe.wait_ge(f0.lin_lo, 4 if b < 4 else 8)
                if b >= 2:
                    pe.wait_ge(f0.added, b - 1)
                product(y2[b % 2][:, :],
                        [((h_hi[:, 2 + k, b * P:(b + 1) * P], h_lo[:, 2 + k, b * P:(b + 1) * P]),
                          (o_hi[:, k * HID:(k + 1) * HID], o_lo[:, k * HID:(k + 1) * HID]))
                         for k in range(2)]).then_inc(f0.down, 1)

            def mlp_half(hf):
                pe.wait_ge(q_lo_done, hf + (UP + 1))
                for u in range(8):
                    half, m = u // 4, u % 4
                    if u >= 4:
                        pe.wait_ge(f0.relu, hf * 8 + (u - 3))
                    product(work[:, u % 4, :], list(zip(weights(q_hi, q_lo, HID, m * P, P),
                                                        columns(xT_hi, xT_lo, half * HALF, HALF)))).then_inc(f0.up, 1)
                pe.wait_ge(o_lo_done, hf + (DOWN + 1))
                for b in range(NB):
                    pe.wait_ge(f0.h_lo, hf * 8 + (4 if b < 4 else 8))
                    pe.wait_ge(f0.added, hf * 8 + (NB + b - 1))
                    product(y2[b % 2][:, :],
                            [((h_hi[:, m, b * P:(b + 1) * P], h_lo[:, m, b * P:(b + 1) * P]),
                              (o_hi[:, m * HID:(m + 1) * HID], o_lo[:, m * HID:(m + 1) * HID]))
                             for m in range(4)]).then_inc(f0.down, 1)

            pe.wait_ge(f0.lin_lo, 8)
            with pe.Fori(0, 2) as hf:
                mlp_half(hf)

            pe.wait_ge(f0.relu, 16)
            for pair in range(2):
                for b in (2 * pair, 2 * pair + 1):
                    transpose_x(N[2], b)
                project_kv(L1, S1, 0, range(2 * pair, 2 * pair + 2),
                           lambda u: pe.wait_ge(N[2].lo, u + 1))
            for b in range(4, NB):
                transpose_x(N[2], b, lambda: pe.wait_ge(S1.act_evac if b % 2 == 0 else S1.dve_evac,
                                                           L1.evac_kv(0, b - 4)))
            drained(N[2])
            attention(L1, S1, N[3])

            def z_half(half):
                pe.wait_ge(kv_lo_done, F1_A + 1)
                pe.wait_ge(N[3].lo, 5 if half == 0 else NB)
                product(work[0:RANK, half, :], list(zip(weights(kv_hi, kv_lo, RANK, 0, RANK),
                                                        columns(xT_hi, xT_lo, half * HALF, HALF)))).then_inc(f1.z, 1)

            def big_h(b):
                if b >= 2:
                    pe.wait_ge(f1.H_added, b - 1)
                product(y2[b % 2][:, :],
                        [((xT_hi[:, k, b * P:(b + 1) * P], xT_lo[:, k, b * P:(b + 1) * P]),
                          (q_hi[:, k * HID:(k + 1) * HID], q_lo[:, k * HID:(k + 1) * HID]))
                         for k in range(KT)]).then_inc(f1.H, 1)

            z_half(0)
            pe.wait_ge(q_lo_done, F1_W + 1)
            pe.wait_ge(S1.y_added, L1.kv_heads * NB)
            big_h(0)
            transpose_x(N[3], 6)
            transpose_x(N[3], 7)
            big_h(1)
            z_half(1)
            for b in range(NB):
                product(work[:, 2, b * NE:(b + 1) * NE],
                        [((xT_hi[:, k, b * P:(b + 1) * P], xT_lo[:, k, b * P:(b + 1) * P]),
                          (q_hi[:, k * HID:k * HID + NE], q_lo[:, k * HID:k * HID + NE])) for k in range(KT)])
            pe.wait_ge(ffn1_loaded, 80)
            pe.wait_ge(f1.z_evac, 2)
            for b in range(NB):
                mm = pe.matmul(work[:, 3, b * NE:(b + 1) * NE], zT[:, b * P:(b + 1) * P], limesT[:, :],
                               start=True, stop=True)
            mm.then_inc(f1.small, 1)

            big_h(2)
            pe.wait_ge(f1.small_evac, 2)
            pe.matmul(pt[:, 0, 0:2 * NB * NE], odd_rows[:, :], hd_raw[:, :, :, :].rearrange("p a b e -> p (a b e)"),
                      start=True, stop=True).then_inc(f1.picked, 1)
            for b in range(3, NB):
                big_h(b)
            pe.wait_ge(f1.w, 1)
            for b in range(NB):
                mm = pe.transpose(work[0:NE, b // 4, b % 4 * P:(b % 4 + 1) * P], lg[5][:, b, :], ident[:, :])
            mm.then_inc(f1.wT, 1)
            pe.wait_ge(f1.wT_evac, 1)
            for half in range(2):
                mm = pe.matmul(work[0:RANK, 2 + half, :], limes[:, :], wT[:, half * HALF:(half + 1) * HALF],
                               start=True, stop=True)
            mm.then_inc(f1.pmix, 1)
            pe.wait_ge(f1.zp, 2)
            for b in range(NB):
                if b < 2:
                    pe.wait_ge(f1.H_added, NB - 1 + b)
                else:
                    pe.wait_ge(f1.done, b - 1)
                pe.matmul(y2[b % 2][:, :], zp[:, b * P:(b + 1) * P], b_mat[:, :], start=True, stop=True)\
                    .then_inc(f1.delta, 1)

        @block.scalar
        def _(act):
            def split_hi(hi, raw, n, rows, loaded, done, in_use, at, value):
                act.wait_ge(loaded, at * 16 + 16)
                if in_use is not None:
                    act.wait_ge(in_use, value)
                act.activation(hi[0:rows, 0:n], raw[0:rows, 0:n], ACT.Copy).then_inc(done, 1)

            def copy_bias(at):
                act.wait_ge(kv_loaded, at * 16 + 16)
                act.activation(bias_now[:, 0:6], kv_raw[:, 1024:1030], ACT.Copy).then_inc(bias_copied, 1)

            def evac_projection(L, S, dst, bank, done, col):
                act.wait_ge(S.proj_done, done)
                if L.bias:
                    act.activation(dst, work[0:L.hd, bank, :], ACT.Identity, bias=bias_now[:, col:col + 1])\
                        .then_inc(S.act_evac, 1)
                else:
                    act.activation(dst, work[0:L.hd, bank, :], ACT.Copy).then_inc(S.act_evac, 1)

            def evac_kv(L, S, it, uses):
                for u in uses:
                    if u % 2 == 0:
                        src, half = u // 4, u // 2 % 2
                        dst = kT[0:L.hd, 0:NB * L.keys].rearrange("p (b s k) -> p b s k", b=NB, k=P)
                        evac_projection(L, S, dst[:, 4 * half:4 * half + 4, src, :], L.bank["kv", u],
                                        L.proj_kv(it, u), G)

            def evac_q(L, S, it, uses):
                for u in uses:
                    if u % 2 == 0:
                        half, g = u // G, u % G
                        evac_projection(L, S, qT[0:L.hd, g, half * HALF:(half + 1) * HALF], L.bank["q", u],
                                        L.proj_q(it, u), g)

            def evac_v(L, S, it, g):
                act.wait_ge(S.vt_done, it * L.v_groups + (g + 1))
                act.activation(v_hi[:, 8 * g * L.hd:8 * (g + 1) * L.hd].rearrange("p (j d) -> p j d", d=L.hd),
                               pt[:, :, :].rearrange("p a (j d) -> p (a j) d", d=P)[:, :, 0:L.hd], ACT.Copy)\
                    .then_inc(S.v_hi_done, 1)

            def oT_upper(L, S, it, b):
                act.wait_ge(S.pv_done, it * NB + (b + 1))
                act.activation(o_buf(L, 0, b)[0:L.hd], ov[0:L.hd, :].rearrange("p (g q) -> p g q", g=G),
                               ACT.Copy).then_inc(S.o_hi_done, 1)

            def head(L, S, it, norm, next_kv, next_q):
                split_hi(o_hi, o_raw, 2048, L.hd, o_loaded, o_hi_done, S.proj_done, it + L.o0, L.proj_q(it, 0))
                evac_q(L, S, it, range(2))
                if L.v_groups == 2:
                    evac_v(L, S, it, 0)
                evac_q(L, S, it, range(2, 4))
                evac_v(L, S, it, L.v_groups - 1)
                for i in range(NB + 3):
                    if i >= NB and norm is None:
                        evac_kv(L, S, it + 1, L.kv_steps[i - NB])
                    b = i - 2
                    if 2 <= i < NB + 2:
                        act.wait_ge(S.pt_done, it * NB + (b + 1))
                        act.activation(pT_hi[:, 0:L.sources, :], pt[:, 0:L.sources, :], ACT.Copy)\
                            .then_inc(S.pt_hi_done, 1)
                    if i == 2:
                        evac_q(L, S, it, L.q_steps[2])
                    if L.double and 3 <= i < NB:
                        oT_upper(L, S, it, b)
                    if i < NB:
                        act.wait_ge(S.max_done, it * NB + (i + 1))
                        bank = L.bank["s", i]
                        s = work[:, bank:bank + L.score_banks, :].rearrange("p a (g k) -> p (a g) k", k=L.keys)
                        for g in range(G):
                            e = act.activation(prob[:, i % 2, g * L.keys:(g + 1) * L.keys], s[:, g, :], ACT.Exp,
                                               bias=neg_max[:, i % 2, g:g + 1], scale=L.scale,
                                               accum_out=exp_sum[:, i % 2, g:g + 1])
                            if (g + 1) % (G // L.score_banks) == 0:
                                e.then_inc(S.exp_done, 1)
                    if i < 2:
                        evac_q(L, S, it, L.q_steps[i])
                    if norm is not None and 4 <= i < NB:
                        normalise_x(norm, i - 4, x[:, i - 4, :])
                    if norm is not None and i >= NB:
                        norm_hi(norm, 2 * (i - NB))
                        normalise_x(norm, i - 4, x[:, i - 4, :])
                        norm_hi(norm, 2 * (i - NB) + 1)
                    if i in (2, NB, NB + 1) or not L.double and 3 <= i < NB:
                        oT_upper(L, S, it, b)
                    if i == 3:
                        if L.bias and norm is None:
                            act.wait_ge(S.dve_evac, L.evac_q(it, L.q_uses - 1))
                            copy_bias(it + (L.kv0 + 1))
                        split_hi(kv_hi, kv_raw, next_kv, P, kv_loaded, kv_hi_done, S.proj_done,
                                 it + (L.kv0 + 1), L.proj_kv(it, L.kv_uses - 1))
                    if i == (8 if norm is None else 5):
                        split_hi(q_hi, q_raw, next_q, P, q_loaded, q_hi_done, S.proj_done,
                                 it + (L.q0 + 1), L.proj_q(it, L.q_uses - 1))

            def attention(L, S, norm, next_kv, next_q, own_kv, own_q):
                with act.Fori(0, L.kv_heads - 1) as it:
                    head(L, S, it, None, own_kv, own_q)
                head(L, S, L.kv_heads - 1, norm, next_kv, next_q)

            def normalise_x(n, b, src, dst=None):
                act.wait_ge(n.rstd, b + 1)
                if dst is None:
                    if b >= n.bufs:
                        act.wait_ge(n.t, b - n.bufs + 1)
                    dst = xn_buf(n, b)
                act.activation(dst, src, ACT.Identity, bias=minus_mean[:, b:b + 1], scale=rstd[:, b:b + 1])\
                    .then_inc(n.xn, 1)

            def norm_hi(n, b):
                act.wait_ge(n.t, b + 1)
                act.activation(xT_hi[:, :, b * P:(b + 1) * P], work[:, b % 4, :].rearrange("p (k t) -> p k t", k=KT),
                               ACT.Copy).then_inc(n.hi, 1)

            split_hi(kv_hi, kv_raw, 768, P, kv_loaded, kv_hi_done, None, 0, 0)
            for k in range(KT):
                act.wait_ge(c_loaded[k], 16)
                act.activation(cT_hi[:, k, :], qT[:, k, :], ACT.Copy).then_inc(c_hi_done, 1)
            act.wait_ge(const_loaded, 32)
            act.activation(gate_hi[:, :, :], gate_raw[:, :, :], ACT.Copy).then_inc(f0.gate_split_hi, 1)
            for b in range(2):
                normalise_x(N[0], b, x[:, b, :])
            evac_kv(L0, S0, 0, range(4))
            split_hi(q_hi, q_raw, 1536, P, q_loaded, q_hi_done, None, 0, 0)
            for b in range(4):
                norm_hi(N[0], b)
                normalise_x(N[0], b + 2, x[:, b + 2, :])
            evac_kv(L0, S0, 0, range(4, 6))
            for b in range(4, NB):
                norm_hi(N[0], b)
                if b + 2 < NB:
                    normalise_x(N[0], b + 2, x[:, b + 2, :])
            evac_kv(L0, S0, 0, range(6, 8))
            attention(L0, S0, N[1], 1024, 512, 768, 1536)

            normalise_x(N[1], NB - 1, x[:, NB - 1, :])
            def lin_hi(w):
                half, which, m = w // 4, w // 2 % 2, w % 2
                act.wait_ge(f0.lin, w + 1)
                act.activation(h_hi[:, 2 * which + m, half * HALF:(half + 1) * HALF], work[:, 2 * half + m, :], ACT.Copy)\
                    .then_inc(f0.lin_hi, 1)

            lin_hi(0)
            lin_hi(1)
            norm_hi(N[1], 6)
            norm_hi(N[1], 7)
            split_hi(o_hi, o_raw, 1024, P, o_loaded, o_hi_done, S0.y_done, FC2, L0.kv_heads * NB)
            for w in range(2, 8):
                lin_hi(w)
            split_hi(q_hi, q_raw, 2048, P, q_loaded, q_hi_done, f0.lin, UP, 8)
            split_hi(o_hi, o_raw, 2048, P, o_loaded, o_hi_done, f0.down, DOWN, NB)

            def square_hi(hf, u):
                half, m = u // 4, u % 4
                act.wait_ge(f0.sq, hf * 8 + (u + 1))
                act.activation(h_hi[:, m, half * HALF:(half + 1) * HALF], h_f[:, u % 2, :], ACT.Copy)\
                    .then_inc(f0.h_hi, 1)

            def mlp_half(hf):
                for u in range(8):
                    act.wait_ge(f0.up, hf * 8 + (u + 1))
                    act.activation(relu[:, u % 2, :], work[:, u % 4, :], ACT.Relu).then_inc(f0.relu, 1)
                    if u:
                        square_hi(hf, u - 1)
                square_hi(hf, 7)

            mlp_half(0)
            split_hi(q_hi, q_raw, 2048, P, q_loaded, q_hi_done, f0.up, UP + 1, 8)
            copy_bias(L1.kv0)
            split_hi(kv_hi, kv_raw, 1024, P, kv_loaded, kv_hi_done, f0.lin, L1.kv0, 8)
            split_hi(o_hi, o_raw, 2048, P, o_loaded, o_hi_done, f0.down, DOWN + 1, 2 * NB)
            mlp_half(1)
            split_hi(q_hi, q_raw, 2048, P, q_loaded, q_hi_done, f0.up, L1.q0, 16)

            for j in range(NB + 6):
                if j < NB:
                    normalise_x(NA, j, acc[:, j, :], acc[:, j, :])
                if 3 <= j < NB + 3:
                    normalise_x(N[2], j - 3, x[:, j - 3, :])
                if 4 <= j < NB + 4:
                    norm_hi(N[2], j - 4)
                if j == 6:
                    evac_kv(L1, S1, 0, range(0, 2))
                if j == 8:
                    evac_kv(L1, S1, 0, range(2, 4))
            act.wait_ge(f0.down, 3 * NB)
            attention(L1, S1, N[3], KT * RANK, 2048, 1024, 2048)
            normalise_x(N[3], NB - 1, x[:, NB - 1, :])
            norm_hi(N[3], 6)
            norm_hi(N[3], 7)
            act.wait_ge(f1.dve, 10)
            act.activation(lg[2][:, :, :], lg[1][:, :, :], ACT.Exp).then_inc(f1.exp, 1)
            act.wait_ge(f1.dve, 13 + NB + 1)
            act.activation(lg[4][:, :, :], lg[3][:, :, :], ACT.Exp, scale=-2.0).then_inc(f1.exp, 1)

        @block.gpsimd
        def _(pool):
            def split_lo(lo, raw, hi, n, rows, hi_done, done, at):
                pool.wait_ge(hi_done, at + 1)
                pool.tensor_tensor(lo[0:rows, 0:n], raw[0:rows, 0:n], hi[0:rows, 0:n].bitcast(F32), ALU.subtract)\
                    .then_inc(done, 1)

            def normalise(L, S, it, b):
                pool.wait_ge(S.rcp_done, it * NB + (b + 1))
                p = prob[:, b % 2, 0:G * L.keys].rearrange("p (g k) -> p g k", g=G)
                pool.tensor_tensor(p, p, exp_rcp[:, b % 2, :].unsqueeze(2).broadcast_to([P, G, L.keys]), ALU.mult)\
                    .then_inc(S.norm_done, 1)

            def head(L, S, it, next_kv, next_q, norm=None):
                split_lo(o_lo, o_raw, o_hi, 2048, L.hd, o_hi_done, o_lo_done, it + L.o0)
                for b in range(NB):
                    normalise(L, S, it, b)
                    if norm is not None and b >= 4:
                        rstd_of(norm, b - 4)
                    if b == 3:
                        split_lo(kv_lo, kv_raw, kv_hi, next_kv, P, kv_hi_done, kv_lo_done, it + (L.kv0 + 1))
                    if b == (7 if norm is None else 5):
                        split_lo(q_lo, q_raw, q_hi, next_q, P, q_hi_done, q_lo_done, it + (L.q0 + 1))
                if norm is not None:
                    for b in range(4, NB):
                        rstd_of(norm, b)

            def attention(L, S, norm, next_kv, next_q, own_kv, own_q):
                with pool.Fori(0, L.kv_heads - 1) as it:
                    head(L, S, it, own_kv, own_q)
                head(L, S, L.kv_heads - 1, next_kv, next_q, norm)

            def rstd_of(n, b):
                at = slice(b, b + 1)
                pool.wait_ge(n.var, b + 1)
                pool.tensor_tensor(rstd[:, at], var_eps[:, at], minus_half[:, :], ALU.pow).then_inc(n.pool, 1)
                pool.wait_ge(n.pool, 2 * b + 1)
                pool.tensor_tensor(minus_mean[:, at], mean_var[:, b, 0:1], rstd[:, at], ALU.mult).then_inc(n.pool, 1)
                pool.wait_ge(n.pool, 2 * b + 2)
                pool.tensor_tensor(minus_mean[:, at], minus_mean[:, at], minus_one[:, :], ALU.mult).then_inc(n.rstd, 1)

            pool.memset(minus_half[:, :], -0.5).then_inc(pool_set, 1)
            pool.memset(minus_one[:, :], -1.0).then_inc(pool_set, 1)
            pool.wait_ge(pool_set, 2)
            split_lo(kv_lo, kv_raw, kv_hi, 768, P, kv_hi_done, kv_lo_done, 0)
            for k in range(2, KT):
                pool.wait_ge(c_hi_done, k + 1)
                pool.tensor_tensor(cT_lo[:, k, :], qT[:, k, :], cT_hi[:, k, :].bitcast(F32), ALU.subtract)\
                    .then_inc(c_lo_pool, 1)
            for b in range(NB):
                rstd_of(N[0], b)
            pool.wait_ge(f0.gate_split_hi, 1)
            pool.tensor_tensor(gate_lo[:, :, :], gate_raw[:, :, :], gate_hi[:, :, :].bitcast(F32), ALU.subtract)\
                .then_inc(f0.gate_split_lo, 1)
            split_lo(q_lo, q_raw, q_hi, 1536, P, q_hi_done, q_lo_done, 0)
            attention(L0, S0, N[1], 1024, 512, 768, 1536)

            split_lo(o_lo, o_raw, o_hi, 1024, P, o_hi_done, o_lo_done, FC2)
            pool.wait_ge(ffn0_loaded, 32)
            pool.wait_ge(N[1].xn, NB)
            for b in range(NB):
                pool.tensor_tensor(x[:, b, :], x[:, b, :], beta[:, :], ALU.add).then_inc(f0.beta_added, 1)
            split_lo(q_lo, q_raw, q_hi, 2048, P, q_hi_done, q_lo_done, UP)
            split_lo(o_lo, o_raw, o_hi, 2048, P, o_hi_done, o_lo_done, DOWN)

            def mlp_half(hf):
                for u in range(8):
                    pool.wait_ge(f0.relu, hf * 8 + (u + 1))
                    if hf or u >= 2:
                        pool.wait_ge(f0.h_lo, hf * 8 + (u - 1))
                    pool.tensor_tensor(h_f[:, u % 2, :], relu[:, u % 2, :], relu[:, u % 2, :], ALU.mult)\
                        .then_inc(f0.sq, 1)

            mlp_half(0)
            split_lo(q_lo, q_raw, q_hi, 2048, P, q_hi_done, q_lo_done, UP + 1)
            split_lo(kv_lo, kv_raw, kv_hi, 1024, P, kv_hi_done, kv_lo_done, L1.kv0)
            split_lo(o_lo, o_raw, o_hi, 2048, P, o_hi_done, o_lo_done, DOWN + 1)
            mlp_half(1)
            split_lo(q_lo, q_raw, q_hi, 2048, P, q_hi_done, q_lo_done, L1.q0)
            for j in range(NB + 2):
                if j < NB:
                    rstd_of(NA, j)
                if 1 <= j < NB + 1:
                    b = j - 1
                    pool.wait_ge(NA.xn, b + 1)
                    pool.tensor_tensor(acc[:, b, :], acc[:, b, :], gamma[:, :], ALU.mult).then_inc(f0.scaled, 1)
                    pool.wait_ge(f0.scaled, b + 1)
                    pool.wait_ge(f0.beta_added, b + 1)
                    pool.tensor_tensor(x[:, b, :], x[:, b, :], acc[:, b, :], ALU.add).then_inc(f0.x_done, 1)
                if j >= 2:
                    rstd_of(N[2], j - 2)
            pool.wait_ge(bo_loaded, 16)
            pool.wait_ge(N[2].xn, NB)
            for b in range(NB):
                pool.tensor_tensor(x[:, b, :], x[:, b, :], bo_bc[:, :], ALU.add).then_inc(bo_added, 1)
            attention(L1, S1, N[3], KT * RANK, 2048, 1024, 2048)
            pool.wait_ge(ffn1_loaded, 80)
            for b in range(NB):
                pool.wait_ge(N[3].xn, b + 1)
                pool.tensor_tensor(x[:, b, :], x[:, b, :], b_bc[:, :], ALU.add).then_inc(f1.b_added, 1)
            pool.wait_ge(f1.dve, 1)
            pool.partition_all_reduce(allmax[:, :], absmax[:, :], P, RMAX).then_inc(f1.allmax, 1)

        @block.vector
        def _(dve):
            def evac_projection(L, S, dst, bank, done, col):
                dve.wait_ge(S.proj_done, done)
                if L.bias:
                    dve.tensor_scalar(dst, work[0:L.hd, bank, :], bias_now[:, col:col + 1], None, ALU.add)\
                        .then_inc(S.dve_evac, 1)
                else:
                    dve.tensor_copy(dst, work[0:L.hd, bank, :]).then_inc(S.dve_evac, 1)

            def evac_kv(L, S, it, uses):
                for u in uses:
                    if u % 2 == 1:
                        at = u // 4 * TOK + u // 2 % 2 * HALF
                        evac_projection(L, S, vT[0:L.hd, at:at + HALF], L.bank["kv", u], L.proj_kv(it, u), G + 1)

            def evac_q(L, S, it, uses):
                for u in uses:
                    if u % 2 == 1:
                        half, g = u // G, u % G
                        evac_projection(L, S, qT[0:L.hd, g, half * HALF:(half + 1) * HALF], L.bank["q", u],
                                        L.proj_q(it, u), g)

            def evac_v(L, S, it, g):
                dve.wait_ge(S.v_hi_done, it * L.v_groups + (g + 1))
                at = slice(8 * g * L.hd, 8 * (g + 1) * L.hd)
                dve.tensor_tensor(v_lo[:, at].rearrange("p (j d) -> p j d", d=L.hd),
                                  pt[:, :, :].rearrange("p a (j d) -> p (a j) d", d=P)[:, :, 0:L.hd],
                                  v_hi[:, at].bitcast(F32).rearrange("p (j d) -> p j d", d=L.hd),
                                  ALU.subtract).then_inc(S.v_lo_done, 1)

            def add_y(L, S, it, b):
                dve.wait_ge(S.y_done, it * NB + (b + 1))
                dve.tensor_tensor(x[:, b, :], x[:, b, :], y_buf(L, b), ALU.add).then_inc(S.y_added, 1)

            def head(L, S, it, norm=None):
                evac_q(L, S, it, range(2))
                if L.v_groups == 2:
                    evac_v(L, S, it, 0)
                evac_q(L, S, it, range(2, 4))
                evac_v(L, S, it, L.v_groups - 1)
                for i in range(NB + 3):
                    b = i - 2
                    if i >= NB and norm is None:
                        evac_kv(L, S, it + 1, L.kv_steps[i - NB])
                    if i == 2 or L.double and 3 <= i < NB + 2:
                        pT_lower(L, S, it, b)
                    if i == 2:
                        evac_q(L, S, it, L.q_steps[2])
                    if i < NB:
                        negative_max(L, S, it, i)
                    if not L.double and 3 <= i < NB + 2:
                        pT_lower(L, S, it, b)
                    if L.double and 2 <= i < NB + 2:
                        oT_lower(L, S, it, b)
                    if L.double and i >= 3:
                        add_share(L, S, it, i - 3, norm)
                    if i < NB:
                        dve.wait_ge(S.exp_done, it * (NB * L.score_banks) + (i + 1) * L.score_banks)
                        dve.reciprocal(exp_rcp[:, i % 2, :], exp_sum[:, i % 2, :]).then_inc(S.rcp_done, 1)
                    if i < 2:
                        evac_q(L, S, it, L.q_steps[i])
                    if norm is not None and i >= NB:
                        norm_lo(norm, 2 * (i - NB))
                        norm_lo(norm, 2 * (i - NB) + 1)
                    if not L.double and i >= 3:
                        add_share(L, S, it, i - 3, norm)
                    if not L.double and 2 <= i < NB + 2:
                        oT_lower(L, S, it, b)

            def negative_max(L, S, it, b):
                dve.wait_ge(S.scores_done, it * NB + (b + 1))
                bank = L.bank["s", b]
                s = work[:, bank:bank + L.score_banks, :].rearrange("p a (g k) -> p (a g) k", k=L.keys)
                dve.tensor_reduce(neg_max_raw[:, b % 2, :], s, AX.X, ALU.max, negate=True)\
                    .then_inc(S.max_raw, 1)
                dve.wait_ge(S.max_raw, it * NB + (b + 1))
                dve.tensor_scalar(neg_max[:, b % 2, :], neg_max_raw[:, b % 2, :], L.scale, None, ALU.mult)\
                    .then_inc(S.max_done, 1)

            def add_share(L, S, it, b, norm):
                add_y(L, S, it, b)
                if norm is not None:
                    dve.wait_ge(S.y_added, it * NB + (b + 1))
                    statistics(norm, x, b)

            def pT_lower(L, S, it, b):
                dve.wait_ge(S.pt_hi_done, it * NB + (b + 1))
                dve.tensor_tensor(pT_lo[:, 0:L.sources, :], pt[:, 0:L.sources, :],
                                  pT_hi[:, 0:L.sources, :].bitcast(F32), ALU.subtract).then_inc(S.pt_lo_done, 1)

            def oT_lower(L, S, it, b):
                dve.wait_ge(S.o_hi_done, it * NB + (b + 1))
                dve.tensor_tensor(o_buf(L, 1, b)[0:L.hd], ov[0:L.hd, :].rearrange("p (g q) -> p g q", g=G),
                                  o_buf(L, 0, b)[0:L.hd].bitcast(F32), ALU.subtract).then_inc(S.o_lo_done, 1)

            def attention(L, S, norm):
                with dve.Fori(0, L.kv_heads - 1) as it:
                    head(L, S, it)
                head(L, S, L.kv_heads - 1, norm)

            def statistics(n, src, b):
                dve.bn_stats(stats[:, b, :], src[:, b, :]).then_inc(n.stat, 1)
                dve.wait_ge(n.stat, 2 * b + 1)
                dve.bn_aggr(mean_var[:, b, :], stats[:, b, :]).then_inc(n.stat, 1)
                dve.wait_ge(n.stat, 2 * b + 2)
                dve.tensor_scalar(var_eps[:, b:b + 1], mean_var[:, b, 1:2], LN_EPS, None, ALU.add).then_inc(n.var, 1)

            def norm_lo(n, b):
                dve.wait_ge(n.hi, b + 1)
                dve.tensor_tensor(xT_lo[:, :, b * P:(b + 1) * P], work[:, b % 4, :].rearrange("p (k t) -> p k t", k=KT),
                                  xT_hi[:, :, b * P:(b + 1) * P].bitcast(F32), ALU.subtract).then_inc(n.lo, 1)

            for k in range(2):
                dve.wait_ge(c_hi_done, k + 1)
                dve.tensor_tensor(cT_lo[:, k, :], qT[:, k, :], cT_hi[:, k, :].bitcast(F32), ALU.subtract)\
                    .then_inc(c_lo_done, 1)
            for b in range(4):
                dve.wait_ge(x_loaded[0], 16)
                statistics(N[0], x, b)
            evac_kv(L0, S0, 0, range(4))
            for b in range(4):
                dve.wait_ge(x_loaded[1], 16)
                statistics(N[0], x, 4 + b)
                norm_lo(N[0], b)
            evac_kv(L0, S0, 0, range(4, 6))
            for b in range(4, NB):
                norm_lo(N[0], b)
            evac_kv(L0, S0, 0, range(6, 8))
            attention(L0, S0, N[1])

            def lin_lo(w):
                half, which, m = w // 4, w // 2 % 2, w % 2
                dve.wait_ge(f0.lin_hi, w + 1)
                at = (slice(None), 2 * which + m, slice(half * HALF, (half + 1) * HALF))
                dve.tensor_tensor(h_lo[at], work[:, 2 * half + m, :], h_hi[at].bitcast(F32), ALU.subtract)\
                    .then_inc(f0.lin_lo, 1)

            lin_lo(0)
            lin_lo(1)
            norm_lo(N[1], 6)
            norm_lo(N[1], 7)
            for w in range(2, 6):
                lin_lo(w)
            dve.wait_ge(f0.gate, 1)
            for b in range(NB):
                dve.max(top8[:, b, :], pt[:, 0, b * NE:(b + 1) * NE]).then_inc(f0.route_top, 1)
            dve.wait_ge(f0.route_top, NB)
            dve.tensor_tensor(route[:, :], top8[:, :, 0], top8[:, :, 1], ALU.add).then_inc(f0.route, 1)
            lin_lo(6)
            lin_lo(7)
            dve.wait_ge(f0.route, 1)
            for b in range(NB):
                dve.wait_ge(f0.down, b + 1)
                dve.tensor_scalar(acc[:, b, :], y2[b % 2][:, :], route[:, b:b + 1], None, ALU.mult)\
                    .then_inc(f0.added, 1)

            def square_lo(hf, u):
                half, m = u // 4, u % 4
                dve.wait_ge(f0.h_hi, hf * 8 + (u + 1))
                at = (slice(None), m, slice(half * HALF, (half + 1) * HALF))
                dve.tensor_tensor(h_lo[at], h_f[:, u % 2, :], h_hi[at].bitcast(F32), ALU.subtract)\
                    .then_inc(f0.h_lo, 1)

            def add_down(hf, b):
                dve.wait_ge(f0.down, hf * 8 + (NB + b + 1))
                dve.wait_ge(f0.added, hf * 8 + (b + 1))
                dve.tensor_tensor(acc[:, b, :], acc[:, b, :], y2[b % 2][:, :], ALU.add).then_inc(f0.added, 1)

            for u in range(8):
                square_lo(0, u)
            for b in range(NB):
                add_down(0, b)
            for u in range(8):
                square_lo(1, u)
            for j in range(NB + 6):
                if j < NB:
                    add_down(1, j)
                    dve.wait_ge(f0.added, 2 * NB + j + 1)
                    statistics(NA, acc, j)
                if 2 <= j < NB + 2:
                    dve.wait_ge(f0.x_done, j - 1)
                    statistics(N[2], x, j - 2)
                if 5 <= j < NB + 5:
                    norm_lo(N[2], j - 5)
                if j == 6:
                    evac_kv(L1, S1, 0, range(0, 2))
                if j == 8:
                    evac_kv(L1, S1, 0, range(2, 4))

            dve.wait_ge(bo_added, NB)
            attention(L1, S1, N[3])

            def evac_z(half):
                dve.wait_ge(f1.z, half + 1)
                dve.tensor_copy(zT[:, half * HALF:(half + 1) * HALF], work[0:RANK, half, :]).then_inc(f1.z_evac, 1)

            def add_h(b):
                dve.wait_ge(f1.H, b + 1)
                dve.wait_ge(f1.b_added, b + 1)
                dve.tensor_tensor(x[:, b, :], x[:, b, :], y2[b % 2][:, :], ALU.add).then_inc(f1.H_added, 1)

            evac_z(0)
            norm_lo(N[3], 6)
            norm_lo(N[3], 7)
            add_h(0)
            add_h(1)
            evac_z(1)
            dve.wait_ge(f1.small, 1)
            dve.wait_ge(ffn1_loaded, 80)
            flat = lambda t: t.rearrange("p b e -> p (b e)")
            dve.tensor_tensor(hd_raw[:, 0, :, :], work[:, 2, 0:NB * NE].rearrange("p (b e) -> p b e", e=NE),
                              b_bc[:, 0:NE].unsqueeze(1).broadcast_to([P, NB, NE]), ALU.add)\
                .then_inc(f1.small_evac, 1)
            dve.tensor_copy(hd_raw[:, 1, :, :], work[:, 3, 0:NB * NE].rearrange("p (b e) -> p b e", e=NE))\
                .then_inc(f1.small_evac, 1)

            dve.wait_ge(f1.picked, 1)
            both = pt[:, 0, 0:2 * NB * NE].rearrange("p (a e) -> p a e", a=2)
            dve.tensor_reduce(absmax[:, :], both, AX.X, ALU.max, apply_absolute_value=True).then_inc(f1.dve, 1)
            dve.tensor_copy(hd[:, :, :, :].rearrange("p a b e -> p (a b e)"), pt[:, 0, 0:2 * NB * NE]).then_inc(f1.dve, 1)
            add_h(2)
            step = [2]

            def chained(ins):
                ins.then_inc(f1.dve, 1)
                step[0] += 1
                dve.wait_ge(f1.dve, step[0])

            def per_row(r):
                return r[:, :].unsqueeze(2).broadcast_to([P, NB, NE])

            dve.wait_ge(f1.allmax, 1)
            chained(dve.tensor_scalar(row[0][:, 0:2], allmax[:, :], 1e-6, None, ALU.max))
            chained(dve.reciprocal(row[1][:, 0:2], row[0][:, 0:2]))
            chained(dve.tensor_scalar(row[2][:, 0:2], row[1][:, 0:2], 0.5, None, ALU.mult))
            chained(dve.tensor_scalar(lg[0][:, :, :], hd[:, 0, :, :], row[2][:, 0:1], None, ALU.mult))
            chained(dve.scalar_tensor_tensor(out=lg[7][:, :, :], in0=hd[:, 1, :, :], scalar=row[2][:, 1:2],
                                             in1=lg[0][:, :, :], op0=ALU.mult, op1=ALU.add))
            chained(dve.tensor_reduce(row[3][:, :], lg[7][:, :, :], AX.X, ALU.max))
            chained(dve.tensor_tensor(lg[1][:, :, :], lg[7][:, :, :], per_row(row[3]), ALU.subtract))
            chained(dve.tensor_scalar(lg[1][:, :, :], lg[1][:, :, :], 1.0, None, ALU.mult))
            assert step[0] == 10
            add_h(3)
            dve.wait_ge(f1.exp, 1)
            chained(dve.tensor_reduce(row[4][:, :], lg[2][:, :, :], AX.X, ALU.add))
            chained(dve.reciprocal(row[5][:, :], row[4][:, :]))
            chained(dve.tensor_tensor(lg[6][:, :, :], lg[2][:, :, :], per_row(row[5]), ALU.mult))
            for b in range(NB):
                chained(dve.max(top8b[:, b, :], lg[6][:, b, :]))
            chained(dve.tensor_tensor(lg[3][:, :, :], lg[6][:, :, :],
                                      top8b[:, :, 1:2].broadcast_to([P, NB, NE]), ALU.subtract))
            assert step[0] == 13 + NB + 1
            add_h(4)
            dve.wait_ge(f1.exp, 2)
            chained(dve.tensor_scalar(lg[0][:, :, :], lg[4][:, :, :], 1.0, None, ALU.add))
            chained(dve.reciprocal(lg[1][:, :, :], lg[0][:, :, :]))
            chained(dve.tensor_tensor(lg[2][:, :, :], lg[1][:, :, :], lg[6][:, :, :], ALU.mult))
            chained(dve.tensor_reduce(row[0][:, :], lg[2][:, :, :], AX.X, ALU.add))
            chained(dve.tensor_scalar(row[1][:, :], row[0][:, :], 1e-9, None, ALU.add))
            chained(dve.reciprocal(row[2][:, :], row[1][:, :]))
            dve.tensor_tensor(lg[5][:, :, :], lg[2][:, :, :], per_row(row[2]), ALU.mult).then_inc(f1.w, 1)
            for b in range(5, NB):
                add_h(b)
            dve.wait_ge(f1.wT, 1)
            dve.tensor_copy(wT[:, :].rearrange("p (a t) -> p a t", a=2), work[0:NE, 0:2, :]).then_inc(f1.wT_evac, 1)
            dve.wait_ge(f1.pmix, 1)
            for half in range(2):
                at = slice(half * HALF, (half + 1) * HALF)
                dve.scalar_tensor_tensor(out=zp[:, at], in0=zT[:, at], scalar=0.5, in1=work[0:RANK, 2 + half, :],
                                         op0=ALU.mult, op1=ALU.mult).then_inc(f1.zp, 1)
            for b in range(NB):
                dve.wait_ge(f1.delta, b + 1)
                dve.wait_ge(f1.H_added, b + 1)
                dve.tensor_tensor(x[:, b, :], x[:, b, :], y2[b % 2][:, :], ALU.add).then_inc(f1.done, 1)


def laid_out(i):
    def tiles(w):
        return w.reshape(-1, P, w.shape[-1]).transpose(1, 0, 2).reshape(P, -1)

    def rows(v):
        return np.broadcast_to(v, (P, v.shape[0]))

    wq, wk, wv, wo = (i[f"L0_xattn_W{n}"] for n in "qkvo")
    per_head = lambda w: w.reshape(4, -1, KT, P).transpose(0, 3, 2, 1)
    a = {
        "x": i["x"],
        "ctxT": i["ctx_4096"].reshape(TOK, KT, P).transpose(2, 1, 0),
        "l0_q": per_head(wq).reshape(4, P, -1),
        "l0_kv": np.concatenate([per_head(wk), per_head(wv)], 3).reshape(4, P, -1),
        "l0_o": wo.reshape(HID, 4, G, 96).transpose(1, 3, 2, 0).reshape(4, 96, -1),
        "gate": i["L0_ffn_gate_w"].reshape(KT, P, NE).transpose(1, 0, 2),
        "up": i["L0_ffn_up_w"].reshape(KT, P, 2, HID).transpose(2, 1, 0, 3).reshape(2, P, -1),
        "down": i["L0_ffn_down_w"].reshape(2, 4, P, HID).transpose(0, 2, 1, 3).reshape(2, P, -1),
        "fc1": tiles(i["L0_ffn_fc1_w"]), "expert": tiles(i["L0_ffn_expert_w"]), "fc2": tiles(i["L0_ffn_fc2_w"]),
        "gamma": rows(i["L0_ffn_ln_gamma"]), "beta": rows(i["L0_ffn_ln_beta"]),
    }
    heads = lambda w, n: w.reshape(KT, P, 8, n).transpose(2, 1, 0, 3)
    wkv, bkv = i["L1_xattn_Wkv"], i["L1_xattn_bkv"]
    a["l1_q"] = heads(i["L1_xattn_Wq"], G * P).reshape(8, P, -1)
    w = np.concatenate([heads(wkv[:, :1024], P), heads(wkv[:, 1024:], P)], 3).reshape(8, P, -1)
    bq = i["L1_xattn_bq"].reshape(8, G, P).transpose(0, 2, 1)
    bk, bv = bkv[:1024].reshape(8, P, 1), bkv[1024:].reshape(8, P, 1)
    a["l1_kv"] = np.concatenate([w, bq, bk, bv], 2)
    a["l1_o"] = i["L1_xattn_Wo"].reshape(8, G, P, HID).transpose(0, 2, 1, 3).reshape(8, P, -1)
    a["bo"] = rows(i["L1_xattn_bo"])
    a["W"] = i["L1_ffn_W"].reshape(HID, KT, P).transpose(2, 1, 0).reshape(P, -1)
    a["A"] = tiles(i["L1_ffn_A"])
    a["b"], a["Bmat"] = rows(i["L1_ffn_b"]), i["L1_ffn_Bmat"]
    a["LiMEs"], a["LiMEsT"] = i["L1_ffn_LiMEs"], i["L1_ffn_LiMEs"].T
    a["ident"] = np.eye(P, dtype=np.float32)
    a["odd_rows"] = np.eye(P, dtype=np.float32)[:, np.arange(P) | 1]
    return {n: np.ascontiguousarray(v) for n, v in a.items()}


def kernel(**inputs):
    import concourse.bacc as bacc
    from concourse.bass_utils import run_bass_kernel_spmd

    nc = bacc.Bacc("TRN2", target_bir_lowering=False, num_devices=1)
    arrays = laid_out({n: np.asarray(v) for n, v in inputs.items()})
    aps = {n: nc.dram_tensor(f"in_{n}", v.shape, mybir.dt.from_np(v.dtype), kind="ExternalInput").ap()
           for n, v in arrays.items()}
    out = nc.dram_tensor("out_0", (NB, P, HID), F32, kind="ExternalOutput").ap()
    build_program(nc, aps, out)
    result = run_bass_kernel_spmd(nc, [{f"in_{n}": v for n, v in arrays.items()}], core_ids=[0])
    return result.results[0]["out_0"]
```

```python
from contextlib import ExitStack

import numpy as np

import concourse.bass as bass
from concourse import mybir

F32 = mybir.dt.float32
F32R = mybir.dt.float32r
ALU = mybir.AluOpType
ACT = mybir.ActivationFunctionType
AX = mybir.AxisListType
RMAX = bass.bass_isa.ReduceOp.max

P = 128
NB = 8
HID = 512
KT = HID // P
TOK = NB * P
HALF = TOK // 2
G = 4
NE = 8
RANK = 32
LN_EPS = 1e-5


class Attention:

    def __init__(self, name, kv_heads, hd, sources, bias, kv0, q0, o0, halves, tail=None):
        self.name, self.kv_heads, self.hd, self.sources, self.bias = name, kv_heads, hd, sources, bias
        self.kv0, self.q0, self.o0 = kv0, q0, o0
        self.halves = halves
        self.keys = sources * P
        self.scale = float(1.0 / np.sqrt(hd))
        self.score_banks = self.keys * G // 512
        self.q_uses = G * 2
        self.kv_uses = sources * 4
        self.proj = self.q_uses + self.kv_uses
        self.evacs = self.proj // 2
        self.v_groups = sources
        self.tiles = 3 if hd == 96 else G
        self.double = sources == 1
        self.q_steps = [(4, 5), (), (6, 7)] if sources == 2 else [(4,), (5,), (6, 7)]
        early = min(self.kv_uses, 6)
        self.ahead = [("kv", u) for u in range(early)] + [("q", u) for u in range(4)]\
            + [("kv", u) for u in range(early, self.kv_uses)]
        n = len(self.ahead)
        self.ahead_steps = [self.ahead[:n // 2], self.ahead[n // 2:n * 3 // 4], self.ahead[n * 3 // 4:]]
        order = []
        for b in range(NB):
            if b == 2:
                order += [("q", u) for u in self.q_steps[2]]
            order += [("s", b)] * self.score_banks
            if b < 2:
                order += [("q", u) for u in self.q_steps[b]]
        order += self.ahead
        assert len(order) % 4 == 0
        own = order[:-len(self.ahead)]
        if tail:
            at = own.index(("s", 5)) + self.score_banks
            own = own[:at] + tail
        self.orders = {False: order, True: own}
        self.bank = {use: order.index(use) % 4 for use in order}
        self.last_bank = {use: own.index(use) % 4 for use in own}

    def score_bank(self, b, last):
        return (self.last_bank if last else self.bank)["s", b]

    def place(self, kind, u):
        return self.ahead.index((kind, u)) if (kind, u) in self.ahead else len(self.ahead) + u - 4

    def projected(self, it, kind, u):
        return it * self.proj + self.place(kind, u) + 1

    def evacuated(self, it, kind, u):
        return it * self.evacs + self.place(kind, u) // 2 + 1

    def wait_bank(self, pe, S, it, kind, n, q_drained=-1, last=False, drained=None):
        order = self.orders[last]
        first = order.index((kind, n))
        for at in range(max(first, 4), first + (self.score_banks if kind == "s" else 1)):
            before, m = order[at - 4]
            if drained and before in drained:
                pe.wait_ge(drained[before], m + 1)
            if (before == "q" and m > q_drained) or before == "kv":
                of = it + 1 if (before, m) in self.ahead else it
                pe.wait_ge(S.act_evac if m % 2 == 0 else S.dve_evac, self.evacuated(of, before, m))
            if before == "s" and (kind != "s" or at == first + self.score_banks - 1):
                nth = m * self.score_banks + (at - 4 - order.index((before, m))) + 1
                pe.wait_ge(S.exp_done, it * (NB * self.score_banks) + nth)


class AttentionSems:

    def __init__(self, sem, prefix):
        self.proj_done = sem(f"{prefix}_proj_done")
        self.act_evac = sem(f"{prefix}_act_evac")
        self.dve_evac = sem(f"{prefix}_dve_evac")
        self.scores_done = sem(f"{prefix}_scores_done")
        self.max_raw = sem(f"{prefix}_max_raw")
        self.max_done = sem(f"{prefix}_max_done")
        self.exp_done = sem(f"{prefix}_exp_done")
        self.rcp_done = sem(f"{prefix}_rcp_done")
        self.norm_done = sem(f"{prefix}_norm_done")
        self.pt_done = sem(f"{prefix}_pt_done")
        self.pt_hi_done = sem(f"{prefix}_pt_hi_done")
        self.pt_lo_done = sem(f"{prefix}_pt_lo_done")
        self.pv_done = sem(f"{prefix}_pv_done")
        self.o_hi_done = sem(f"{prefix}_o_hi_done")
        self.o_lo_done = sem(f"{prefix}_o_lo_done")
        self.y_done = sem(f"{prefix}_y_done")
        self.y_added = sem(f"{prefix}_y_added")
        self.vt_done = sem(f"{prefix}_vt_done")
        self.v_hi_done = sem(f"{prefix}_v_hi_done")
        self.v_lo_done = sem(f"{prefix}_v_lo_done")


class NormSems:

    def __init__(self, sem, prefix, bufs, banks):
        self.bufs = bufs
        self.banks = banks
        self.stat = sem(f"{prefix}_stat")
        self.var = sem(f"{prefix}_var")
        self.rstd = sem(f"{prefix}_rstd")
        self.shift = sem(f"{prefix}_shift")
        self.xn = sem(f"{prefix}_xn")
        self.t = sem(f"{prefix}_t")
        self.hi = sem(f"{prefix}_hi")
        self.lo = sem(f"{prefix}_lo")


class Ffn0Sems:

    def __init__(self, sem, prefix):
        self.gate_split_hi = sem(f"{prefix}_gate_split_hi")
        self.gate_split_lo = sem(f"{prefix}_gate_split_lo")
        self.gate = sem(f"{prefix}_gate")
        self.gate_copied = sem(f"{prefix}_gate_copied")
        self.route_top = sem(f"{prefix}_route_top")
        self.route = sem(f"{prefix}_route")
        self.lin = sem(f"{prefix}_lin")
        self.lin_hi = sem(f"{prefix}_lin_hi")
        self.lin_lo = sem(f"{prefix}_lin_lo")
        self.up = sem(f"{prefix}_up")
        self.relu = sem(f"{prefix}_relu")
        self.sq = sem(f"{prefix}_sq")
        self.h_hi = sem(f"{prefix}_h_hi")
        self.h_lo = sem(f"{prefix}_h_lo")
        self.down = sem(f"{prefix}_down")
        self.added = sem(f"{prefix}_added")
        self.scaled = sem(f"{prefix}_scaled")
        self.x_done = sem(f"{prefix}_x_done")
        self.beta_added = sem(f"{prefix}_beta_added")


class Ffn1Sems:

    def __init__(self, sem, prefix):
        self.z = sem(f"{prefix}_z")
        self.z_evac = sem(f"{prefix}_z_evac")
        self.small = sem(f"{prefix}_small")
        self.dve = sem(f"{prefix}_dve")
        self.allmax = sem(f"{prefix}_allmax")
        self.exp = sem(f"{prefix}_exp")
        self.w = sem(f"{prefix}_w")
        self.wT = sem(f"{prefix}_wT")
        self.wT_evac = sem(f"{prefix}_wT_evac")
        self.pmix = sem(f"{prefix}_pmix")
        self.zp = sem(f"{prefix}_zp")
        self.H = sem(f"{prefix}_H")
        self.H_added = sem(f"{prefix}_H_added")
        self.delta = sem(f"{prefix}_delta")
        self.done = sem(f"{prefix}_done")
        self.b_added = sem(f"{prefix}_b_added")


def build_program(nc, A, out):
    L0 = Attention("L0", 4, 96, 2, False, kv0=0, q0=0, o0=0, halves=0,
                   tail=[("x", 0), ("x", 1), ("s", 6), ("s", 6), ("s", 7), ("s", 7), ("x", 2), ("x", 3),
                         ("lin", 0), ("lin", 1), ("x", 4), ("x", 5)])
    L1 = Attention("L1", 8, 128, 1, True, kv0=5, q0=7, o0=7, halves=4,
                   tail=[("x", 0), ("s", 6), ("x", 1), ("s", 7), ("x", 2), ("x", 3), ("h", 0), ("x", 4), ("h", 1),
                         ("x", 5), ("z", 0), ("x", 6), ("h", 2), ("x", 7), ("h", 3), ("z", 1)]
                   + [("h", b) for b in range(4, NB)])
    FC1 = L0.kv_heads
    EXPERT = L0.kv_heads
    UP = EXPERT + 1
    FC2 = L0.kv_heads
    DOWN = FC2 + 1
    F1_A = L1.kv0 + L1.kv_heads
    F1_W = L1.q0 + L1.kv_heads

    with ExitStack() as ctx:
        def sb(name, shape, dt=F32, stack=ctx):
            return stack.enter_context(nc.sbuf_tensor(name, shape, dt))

        def sem(name):
            return ctx.enter_context(nc.semaphore(name))

        x = sb("x", [P, NB, HID])
        xT_hi = sb("xT_hi", [P, KT, TOK], F32R)
        xT_lo = sb("xT_lo", [P, KT, TOK], F32R)
        cT_hi = sb("cT_hi", [P, KT, TOK], F32R)
        cT_lo = sb("cT_lo", [P, KT, TOK], F32R)
        kv_raw = sb("kv_raw", [P, 1032])
        q_raw = sb("q_raw", [P, 2048])
        o_raw = sb("o_raw", [P, 2048])
        kv_hi, kv_lo = sb("kv_hi", [P, 1024], F32R), sb("kv_lo", [P, 1024], F32R)
        q_hi, q_lo = sb("q_hi", [P, 2048], F32R), sb("q_lo", [P, 2048], F32R)
        o_hi, o_lo = sb("o_hi", [P, 2048], F32R), sb("o_lo", [P, 2048], F32R)
        ident = sb("ident", [P, P])
        bias_now = sb("bias_now", [P, 8])
        stats = sb("stats", [P, NB, 6])
        mean_var = sb("mean_var", [P, NB, 2])
        var_eps = sb("var_eps", [P, NB])
        rstd = sb("rstd", [P, NB])
        minus_half = sb("minus_half", [P, 1])
        minus_mean = sb("minus_mean", [P, NB])
        neg_max_raw = sb("neg_max_raw", [P, 2, G])
        neg_max = sb("neg_max", [P, 2, G])
        exp_sum = sb("exp_sum", [P, 2, G])
        exp_rcp = sb("exp_rcp", [P, 2, G])
        gate_raw = sb("gate_raw", [P, KT, NE])
        gate_hi, gate_lo = sb("gate_hi", [P, KT, NE], F32R), sb("gate_lo", [P, KT, NE], F32R)
        top8 = sb("top8", [P, NB, 8])
        route = sb("route", [P, NB])
        with ExitStack() as st:
            qT = sb("qT", [P, G, TOK], stack=st)
            kT = sb("kT", [P, NB * 2 * P], stack=st)
            vT = sb("vT", [P, 2 * TOK], stack=st)
            prob = sb("prob", [P, 2, G * 2 * P], stack=st)
            pT_hi, pT_lo = sb("pT_hi", [P, 2, 512], F32R, st), sb("pT_lo", [P, 2, 512], F32R, st)
            v_hi, v_lo = sb("v_hi", [P, 16 * 96], F32R, st), sb("v_lo", [P, 16 * 96], F32R, st)
            oT_hi, oT_lo = sb("oT_hi", [P, G, P], F32R, st), sb("oT_lo", [P, G, P], F32R, st)
            bo_bc = sb("bo_bc", [P, HID], stack=st)
        with ExitStack() as st:
            h_hi, h_lo = sb("h_hi", [P, KT, TOK], F32R, st), sb("h_lo", [P, KT, TOK], F32R, st)
            acc = sb("acc", [P, NB, HID], stack=st)
            relu = sb("relu", [P, 2, HALF], stack=st)
            gamma = sb("gamma", [P, HID], stack=st)
            h_f = sb("h_f", [P, 2, HALF], stack=st)
            beta = sb("beta", [P, HID], stack=st)
        with ExitStack() as st:
            ZH = RANK + NE
            zT = sb("zT", [ZH, TOK], stack=st)
            zp = sb("zp", [RANK, TOK], stack=st)
            wT = sb("wT", [NE, HALF], stack=st)
            b_mat = sb("b_mat", [RANK, HID], stack=st)
            limes = sb("limes", [NE, RANK], stack=st)
            pick = sb("pick", [ZH, 2 * NE], stack=st)
            z_bias = sb("z_bias", [ZH, 1], stack=st)
            b_bc = sb("b_bc", [P, HID], stack=st)
            AC = HALF // P
            hd = sb("hd", [P, 2, AC, NE], stack=st)
            absmax = sb("absmax", [P, 2], stack=st)
            allmax = sb("allmax", [P, 2], stack=st)
            lg = [sb(f"lg{i}", [P, AC, NE], stack=st) for i in range(8)]
            row = [sb(f"row{i}", [P, AC], stack=st) for i in range(6)]
            top8b = sb("top8b", [P, AC, 8], stack=st)

        work = ctx.enter_context(nc.psum_tensor("work", [P, 4, 512], F32))
        pt = ctx.enter_context(nc.psum_tensor("pt", [P, 2, 512], F32))
        ov = ctx.enter_context(nc.psum_tensor("ov", [P, 512], F32))
        yb = ctx.enter_context(nc.psum_tensor("yb", [P, 512], F32))
        y2 = [yb, ov]
        logitsT = relu[:, :, :].rearrange("p a t -> p (a t)")
        d2 = [ov[:, :], pt[:, 1, :]]

        def o_buf(L, part, b):
            if L.double and b % 2:
                return (pT_hi, pT_lo)[part][:, 1, :].rearrange("p (g q) -> p g q", g=G)
            return (oT_hi, oT_lo)[part][:, :, :]

        ov_heads = ov[:, :].rearrange("p (g q) -> p g q", g=G)

        def o_parts(L):
            if L.tiles == G:
                return [((slice(0, L.hd),), (slice(0, L.hd),))]
            third = L.hd // 3
            return [((slice(0, L.hd), slice(0, 3)), (slice(0, L.hd), slice(0, 3)))]\
                + [((slice(L.hd, P), t), (slice(third * t, third * (t + 1)), 3)) for t in range(3)]

        def y_buf(L, b):
            return pt[:, 1, :] if L.double and b % 2 else yb[:, :]

        def xn_buf(n, b):
            if n.bufs == 2:
                return relu[:, b % 2, :]
            if n is N[0]:
                return prob[:, b // 2 % 2, b % 2 * HID:(b % 2 + 1) * HID]
            return vT[:, b % 4 * HID:(b % 4 + 1) * HID]

        def x_bank(n, b):
            if n is N[0]:
                return (pt[:, 0, :], pt[:, 1, :], ov[:, :], yb[:, :])[b % 4]
            return pt[:, b % 2, :] if n is N[2] else work[:, n.banks[b], :]

        x_loaded = [sem("x_loaded0"), sem("x_loaded1")]
        c_loaded = [sem(f"c_loaded{k}") for k in range(KT)]
        const_loaded = sem("const_loaded")
        ffn1_loaded = sem("ffn1_loaded")
        ffn0_loaded = sem("ffn0_loaded")
        bo_loaded = sem("bo_loaded")
        kv_loaded, kv_hi_done, kv_lo_done = sem("kv_loaded"), sem("kv_hi_done"), sem("kv_lo_done")
        q_loaded, q_hi_done, q_lo_done = sem("q_loaded"), sem("q_hi_done"), sem("q_lo_done")
        o_loaded, o_hi_done, o_lo_done = sem("o_loaded"), sem("o_hi_done"), sem("o_lo_done")
        c_hi_done, c_lo_done, c_lo_pool = sem("c_hi_done"), sem("c_lo_done"), sem("c_lo_pool")
        out_stored = sem("out_stored")
        q_half_done, q_lo_half = sem("q_half_done"), sem("q_lo_half")
        pool_set = sem("pool_set")
        bias_copied = sem("bias_copied")

        S0, S1 = AttentionSems(sem, "L0"), AttentionSems(sem, "L1")

        N = [NormSems(sem, "ln0", 4, ()),
             NormSems(sem, "ln1", 4, [L0.last_bank["x", b] for b in range(6)] + [2, 3]),
             NormSems(sem, "ln2", 2, ()),
             NormSems(sem, "ln3", 4, [L1.last_bank["x", b] for b in range(NB)])]
        NA = NormSems(sem, "ln_acc", NB, ())
        f0 = Ffn0Sems(sem, "f0")
        bo_added = sem("bo_added")
        f1 = Ffn1Sems(sem, "f1")

        block = ctx.enter_context(nc.Block())

        @block.sync
        def _(sp):
            def load(raw, src, loaded, lo_done, n):
                sp.wait_ge(lo_done, n)
                sp.dma_start(raw, src).then_inc(loaded, 16)

            sp.dma_start(kv_raw[:, 0:768], A["l0_kv"][0]).then_inc(kv_loaded, 16)
            for k in range(KT):
                sp.dma_start(qT[:, k, :], A["ctxT"][:, k, :]).then_inc(c_loaded[k], 16)
            sp.dma_start(x[:, 0:4, :], A["x"][0:4].rearrange("b t d -> t b d")).then_inc(x_loaded[0], 16)
            sp.dma_start(ident[:, :], A["ident"]).then_inc(const_loaded, 16)
            sp.dma_start(gate_raw[:, :, :], A["gate"]).then_inc(const_loaded, 16)
            sp.dma_start(q_raw[:, 0:1536], A["l0_q"][0]).then_inc(q_loaded, 16)
            sp.dma_start(x[:, 4:8, :], A["x"][4:8].rearrange("b t d -> t b d")).then_inc(x_loaded[1], 16)
            sp.dma_start(o_raw[:, 0:1536], A["l0_o"][0]).then_inc(o_loaded, 16)
            sp.dma_start(bo_bc[:, :], A["bo"]).then_inc(bo_loaded, 16)
            with sp.Fori(1, L0.kv_heads) as it:
                load(kv_raw[:, 0:768], A["l0_kv"][it], kv_loaded, kv_lo_done, it)
                load(q_raw[:, 0:1536], A["l0_q"][it], q_loaded, q_lo_done, it)
                load(o_raw[:, 0:1536], A["l0_o"][it], o_loaded, o_lo_done, it)
            load(kv_raw[:, 0:1024], A["fc1"], kv_loaded, kv_lo_done, FC1)
            load(q_raw[:, 0:512], A["expert"], q_loaded, q_lo_done, EXPERT)
            load(o_raw[:, 0:1024], A["fc2"], o_loaded, o_lo_done, FC2)
            sp.wait_ge(S0.y_done, L0.kv_heads * NB)
            sp.wait_ge(S0.o_lo_done, L0.kv_heads * NB)
            sp.dma_start(gamma[:, :], A["gamma"]).then_inc(ffn0_loaded, 16)
            sp.dma_start(beta[:, :], A["beta"]).then_inc(ffn0_loaded, 16)
            load(q_raw[:, :], A["up"][0], q_loaded, q_lo_done, UP)
            load(o_raw[:, :], A["down"][0], o_loaded, o_lo_done, DOWN)
            load(q_raw[:, :], A["up"][1], q_loaded, q_lo_done, UP + 1)
            load(kv_raw[:, 0:1030], A["l1_kv"][0], kv_loaded, kv_lo_done, L1.kv0)
            load(o_raw[:, :], A["down"][1], o_loaded, o_lo_done, DOWN + 1)
            load(q_raw[:, :], A["l1_q"][0], q_loaded, q_lo_done, L1.q0)
            load(o_raw[:, :], A["l1_o"][0], o_loaded, o_lo_done, L1.o0)
            with sp.Fori(1, L1.kv_heads) as it:
                load(kv_raw[:, 0:1030], A["l1_kv"][it], kv_loaded, kv_lo_done, it + L1.kv0)
                load(q_raw[:, :], A["l1_q"][it], q_loaded, q_lo_done, it + L1.q0)
                load(o_raw[:, :], A["l1_o"][it], o_loaded, o_lo_done, it + L1.o0)
            load(kv_raw[:, 0:KT * ZH], A["A"], kv_loaded, kv_lo_done, F1_A)
            load(q_raw[:, :], A["W"], q_loaded, q_lo_done, F1_W)
            sp.wait_ge(S1.scores_done, L1.kv_heads * NB)
            for dst, src in ((b_mat, "Bmat"), (limes, "LiMEs"), (pick, "pick"), (b_bc, "b"), (z_bias, "z_bias")):
                sp.dma_start(dst[:, :], A[src]).then_inc(ffn1_loaded, 16)
            for b in range(NB):
                sp.wait_ge(f1.done, b + 1)
                sp.dma_start(out[b], x[:, b, :]).then_inc(out_stored, 16)
            sp.wait_ge(out_stored, 16 * NB)

        @block.tensor
        def _(pe):
            def product(dst, pairs, first=True, last=True):
                n = len(pairs)
                for k, ((l_hi, l_lo), (r_hi, r_lo)) in enumerate(pairs):
                    pe.matmul(dst, l_hi, r_hi, start=first and k == 0, stop=False)
                    pe.matmul(dst, l_hi, r_lo, start=False, stop=False)
                    mm = pe.matmul(dst, l_lo, r_hi, start=False, stop=last and k == n - 1)
                return mm

            def weights(hi, lo, width, at, n):
                return [(hi[:, k * width + at:k * width + at + n], lo[:, k * width + at:k * width + at + n])
                        for k in range(KT)]

            def columns(hi, lo, at, n):
                return [(hi[:, k, at:at + n], lo[:, k, at:at + n]) for k in range(KT)]

            def project(L, S, it, kind, u, bank_free=None):
                if u == 0:
                    if kind == "kv":
                        pe.wait_ge(kv_lo_done, it + (L.kv0 + 1))
                    else:
                        pe.wait_ge(q_lo_done, it + (L.q0 + 1))
                if bank_free:
                    pe.wait_ge(*bank_free)
                else:
                    L.wait_bank(pe, S, it - 1 if (kind, u) in L.ahead else it, kind, u)
                if kind == "kv":
                    half = u // 2 % 2
                    hi, lo = (cT_hi, cT_lo) if u // 4 == 0 else (xT_hi, xT_lo)
                    w = weights(kv_hi, kv_lo, 2 * L.hd, u % 2 * L.hd, L.hd)
                else:
                    half = u // G
                    hi, lo = xT_hi, xT_lo
                    w = weights(q_hi, q_lo, G * L.hd, u % G * L.hd, L.hd)
                product(work[0:L.hd, L.bank[kind, u], :], list(zip(w, columns(hi, lo, half * HALF, HALF))))\
                    .then_inc(S.proj_done, 1)

            def transpose_v(L, S, it, g):
                if g:
                    pe.wait_ge(S.v_lo_done, it * L.v_groups + g)
                else:
                    pe.wait_ge(S.dve_evac, L.evacuated(it, "kv", 3))
                    if L.double:
                        pe.wait_ge(S.max_done, it * NB + 1)
                for j in range(8):
                    mm = pe.transpose(pt[:, j // 4, j % 4 * P:j % 4 * P + L.hd],
                                      vT[0:L.hd, (8 * g + j) * P:(8 * g + j + 1) * P], ident[0:L.hd, 0:L.hd])
                mm.then_inc(S.vt_done, 1)

            def scores(L, S, it, b, norm=None):
                if b == 0:
                    pe.wait_ge(S.act_evac, it * L.evacs + len(L.ahead) // 2)
                    pe.wait_ge(S.dve_evac, it * L.evacs + len(L.ahead) // 2)
                if b == 4:
                    pe.wait_ge(S.act_evac, L.evacuated(it, "q", 6))
                    pe.wait_ge(S.dve_evac, L.evacuated(it, "q", 7))
                L.wait_bank(pe, S, it, "s", b, 7 if b == 4 else -1, norm is not None, norm and {"x": norm.lo})
                bank = L.score_bank(b, norm is not None)
                dst = work[:, bank:bank + L.score_banks, :].rearrange("p a (g k) -> p (a g) k", k=L.keys)
                for g in range(G):
                    mm = pe.matmul(dst[:, g, :], qT[0:L.hd, g, b * P:(b + 1) * P],
                                   kT[0:L.hd, b * L.keys:(b + 1) * L.keys], start=True, stop=True)
                mm.then_inc(S.scores_done, 1)

            def transpose_p(L, S, it, b):
                pe.wait_ge(S.norm_done, it * NB + (b + 1))
                if b == 0:
                    pe.wait_ge(S.v_lo_done, (it + 1) * L.v_groups)
                for c in range(L.sources):
                    for g in range(G):
                        mm = pe.transpose(pt[:, c, g * P:(g + 1) * P],
                                          prob[:, b % 2, g * L.keys + c * P:g * L.keys + (c + 1) * P],
                                          ident[:, :])
                    mm.then_inc(S.pt_done, 1)

            def values(L, S, it, b):
                if b:
                    pe.wait_ge(S.o_lo_done, it * NB + b)
                for c in range(L.sources):
                    pe.wait_ge(S.pt_lo_done, (it * NB + b) * L.sources + (c + 1))
                    at = (c * NB + b) * L.hd
                    mm = product(ov[0:L.hd, :], [((v_hi[:, at:at + L.hd], v_lo[:, at:at + L.hd]),
                                                  (pT_hi[:, c, :], pT_lo[:, c, :]))], c == 0, c == L.sources - 1)
                mm.then_inc(S.pv_done, 1)

            def output(L, S, it, b, tiles=None):
                tiles = tiles or range(L.tiles)
                if tiles[0] == 0:
                    if b == 0:
                        pe.wait_ge(o_lo_done, it + (L.o0 + 1))
                    before = 2 if L.double else 1
                    if b >= before:
                        pe.wait_ge(S.y_added, it * NB + (b + 1 - before))
                    pe.wait_ge(S.o_lo_done, it * NB + (b + 1))
                mm = product(y_buf(L, b), [((o_buf(L, 0, b)[:, g, :], o_buf(L, 1, b)[:, g, :]),
                                            (o_hi[:, g * HID:(g + 1) * HID], o_lo[:, g * HID:(g + 1) * HID]))
                                           for g in tiles], tiles[0] == 0, tiles[-1] == L.tiles - 1)
                if tiles[-1] == L.tiles - 1:
                    mm.then_inc(S.y_done, 1)

            def attention_head(L, S, it, norm=None):
                if L.v_groups == 2:
                    transpose_v(L, S, it, 0)
                for i in range(NB + 3):
                    if i < 2:
                        scores(L, S, it, i)
                        for u in L.q_steps[i]:
                            project(L, S, it, "q", u)
                            if u == 4:
                                transpose_v(L, S, it, L.v_groups - 1)
                    elif i == 2:
                        transpose_p(L, S, it, 0)
                        project(L, S, it, "q", 6)
                        values(L, S, it, 0)
                        project(L, S, it, "q", 7)
                        scores(L, S, it, 2)
                    elif i < NB:
                        if L.double:
                            transpose_p(L, S, it, i - 2)
                            output(L, S, it, i - 3, (0, 1))
                            scores(L, S, it, i, norm)
                            values(L, S, it, i - 2)
                            if norm is not None and i >= 5:
                                early_x(L, S, norm, i - 5)
                            output(L, S, it, i - 3, (2, 3))
                        else:
                            if norm is not None and i == 6:
                                early_x(L, S, norm, 0)
                                early_x(L, S, norm, 1)
                            if i == 3:
                                transpose_p(L, S, it, 1)
                            scores(L, S, it, i, norm)
                            if i > 3:
                                transpose_p(L, S, it, i - 2)
                            output(L, S, it, i - 3)
                            values(L, S, it, i - 2)
                    elif L.double and norm is not None:
                        if i < NB + 2:
                            transpose_p(L, S, it, i - 2)
                        early_x(L, S, norm, i - 5)
                        output(L, S, it, i - 3)
                        if i < NB + 2:
                            values(L, S, it, i - 2)
                            big_h(i - NB)
                    elif norm is not None:
                        if i < NB + 2:
                            transpose_p(L, S, it, i - 2)
                        if i == NB:
                            early_x(L, S, norm, 2)
                            early_x(L, S, norm, 3)
                        else:
                            early_x(L, S, norm, i - 5)
                            fc1(0, i - NB - 1)
                        output(L, S, it, i - 3)
                        if i < NB + 2:
                            values(L, S, it, i - 2)
                    else:
                        for kind, u in L.ahead_steps[i - NB]:
                            project(L, S, it + 1, kind, u)
                        if i < NB + 2:
                            transpose_p(L, S, it, i - 2)
                        output(L, S, it, i - 3)
                        if i < NB + 2:
                            values(L, S, it, i - 2)

            def early_x(L, S, norm, b):
                L.wait_bank(pe, S, L.kv_heads - 1, "x", b, last=True, drained={**drained_by, "x": norm.lo})
                transpose_x(norm, b, ())

            drained_by = {"x": N[3].lo, "h": f1.H_added, "z": f1.z_evac}

            def fc1(half, m):
                pe.wait_ge(kv_lo_done, FC1 + 1)
                pe.wait_ge(N[1].lo, 4 if half == 0 else NB)
                pe.wait_ge(S0.exp_done, L0.kv_heads * NB * L0.score_banks)
                product(work[:, 2 * half + m, :], list(zip(weights(kv_hi, kv_lo, 256, m * P, P),
                                                           columns(xT_hi, xT_lo, half * HALF, HALF))))\
                    .then_inc(f0.lin, 1)

            def big_h(b):
                if b == 0:
                    pe.wait_ge(q_lo_done, F1_W + 1)
                pe.wait_ge(N[3].lo, b + 1)
                L1.wait_bank(pe, S1, L1.kv_heads - 1, "h", b, last=True, drained=drained_by)
                product(work[:, L1.last_bank["h", b], :],
                        [((xT_hi[:, k, b * P:(b + 1) * P], xT_lo[:, k, b * P:(b + 1) * P]),
                          (q_hi[:, k * HID:(k + 1) * HID], q_lo[:, k * HID:(k + 1) * HID]))
                         for k in range(KT)]).then_inc(f1.H, 1)

            def attention(L, S, norm):
                with pe.Fori(0, L.kv_heads - 1) as it:
                    attention_head(L, S, it)
                attention_head(L, S, L.kv_heads - 1, norm)

            def transpose_x(n, b, bank_free=None):
                pe.wait_ge(n.xn, b + 1)
                if bank_free:
                    pe.wait_ge(*bank_free)
                elif bank_free is None and b >= 4:
                    pe.wait_ge(n.lo, b - 3)
                for k in range(KT):
                    mm = pe.transpose(x_bank(n, b)[:, k * P:(k + 1) * P], xn_buf(n, b)[:, k * P:(k + 1) * P],
                                      ident[:, :])
                mm.then_inc(n.t, 1)

            def drained(n):
                pe.wait_ge(n.lo, NB)

            def project_context(u, ks, first, last):
                w = weights(kv_hi, kv_lo, 2 * L0.hd, u % 2 * L0.hd, L0.hd)
                c = columns(cT_hi, cT_lo, u // 2 * HALF, HALF)
                return product(work[0:L0.hd, L0.bank["kv", u], :], [(w[k], c[k]) for k in ks], first, last)

            pe.wait_ge(kv_lo_done, 1)
            for k in range(2):
                pe.wait_ge(c_lo_done, k + 1)
                for u in range(4):
                    project_context(u, [k], k == 0, False)
            pe.wait_ge(c_lo_pool, 1)
            pe.wait_ge(c_lo_done, 3)
            pe.wait_ge(const_loaded, 32)
            for u in range(4):
                project_context(u, [2, 3], False, True).then_inc(S0.proj_done, 1)
                transpose_x(N[0], u, ())

            def evac_of(L, S, kind, u):
                return (S.act_evac if u % 2 == 0 else S.dve_evac), L.evacuated(0, kind, u)

            pe.wait_ge(N[0].lo, 4)
            project(L0, S0, 0, "kv", 4, evac_of(L0, S0, "kv", 0))
            transpose_x(N[0], 4)
            project(L0, S0, 0, "kv", 5, evac_of(L0, S0, "kv", 1))
            transpose_x(N[0], 5)
            transpose_x(N[0], 6)
            project(L0, S0, 0, "q", 0, evac_of(L0, S0, "kv", 2))
            transpose_x(N[0], 7)
            project(L0, S0, 0, "q", 1, evac_of(L0, S0, "kv", 3))
            project(L0, S0, 0, "q", 2, evac_of(L0, S0, "kv", 4))
            project(L0, S0, 0, "q", 3, evac_of(L0, S0, "kv", 5))
            drained(N[0])
            project(L0, S0, 0, "kv", 6, evac_of(L0, S0, "q", 0))
            project(L0, S0, 0, "kv", 7, evac_of(L0, S0, "q", 1))
            attention(L0, S0, N[1])

            def expert(half, tiles=range(2)):
                pe.wait_ge(q_lo_done, EXPERT + 1)
                pe.wait_ge(f0.lin_lo, 4 * half + 2)
                for m in tiles:
                    product(work[:, 2 * half + m, :],
                            [((q_hi[:, k * 256 + m * P:k * 256 + (m + 1) * P],
                               q_lo[:, k * 256 + m * P:k * 256 + (m + 1) * P]),
                              (h_hi[:, k, half * HALF:(half + 1) * HALF], h_lo[:, k, half * HALF:(half + 1) * HALF]))
                             for k in range(2)]).then_inc(f0.lin, 1)

            def gate(half):
                pe.wait_ge(f0.gate_split_lo, 1)
                return product(pt[0:NE, half, :], [((gate_hi[:, k, :], gate_lo[:, k, :]), xt)
                                                   for k, xt in enumerate(columns(xT_hi, xT_lo, half * HALF, HALF))])

            gate(0)
            transpose_x(N[1], 6, (N[1].lo, 5))
            expert(0, [0])
            transpose_x(N[1], 7, (N[1].lo, 6))
            expert(0, [1])
            drained(N[1])
            fc1(1, 0)
            fc1(1, 1)
            gate(1).then_inc(f0.gate, 1)
            expert(1)
            pe.wait_ge(f0.gate_copied, 1)
            for b in range(NB):
                mm = pe.transpose(pt[:, 0, b * NE:(b + 1) * NE], logitsT[0:NE, b * P:(b + 1) * P], ident[0:NE, 0:NE])
            mm.then_inc(f0.gate, 1)
            pe.wait_ge(o_lo_done, FC2 + 1)
            for b in range(NB):
                pe.wait_ge(f0.lin_lo, 4 if b < 4 else 8)
                if b >= 2:
                    pe.wait_ge(f0.added, b - 1)
                product(y2[b % 2][:, :],
                        [((h_hi[:, 2 + k, b * P:(b + 1) * P], h_lo[:, 2 + k, b * P:(b + 1) * P]),
                          (o_hi[:, k * HID:(k + 1) * HID], o_lo[:, k * HID:(k + 1) * HID]))
                         for k in range(2)]).then_inc(f0.down, 1)

            def mlp_half(hf, norm=None):
                pe.wait_ge(q_lo_done, hf + (UP + 1))
                for u in range(8):
                    half, m = u // 4, u % 4
                    if u >= 4:
                        pe.wait_ge(f0.relu, hf * 8 + (u - 3))
                    product(work[:, u % 4, :], list(zip(weights(q_hi, q_lo, HID, m * P, P),
                                                        columns(xT_hi, xT_lo, half * HALF, HALF)))).then_inc(f0.up, 1)
                pe.wait_ge(o_lo_done, hf + (DOWN + 1))
                for b in range(NB):
                    pe.wait_ge(f0.h_lo, hf * 8 + (4 if b < 4 else 8))
                    pe.wait_ge(f0.added, hf * 8 + (NB + b - 1))
                    product(y2[b % 2][:, :],
                            [((h_hi[:, m, b * P:(b + 1) * P], h_lo[:, m, b * P:(b + 1) * P]),
                              (o_hi[:, m * HID:(m + 1) * HID], o_lo[:, m * HID:(m + 1) * HID]))
                             for m in range(4)]).then_inc(f0.down, 1)
                    if norm is not None and b >= 4:
                        transpose_x(norm, b - 4, (norm.lo, b - 5) if b >= 6 else (f0.route, 1))
                    if norm is not None and b % 2 == 1:
                        project(L1, S1, 0, "kv", b // 2, (f0.relu, 16))

            pe.wait_ge(f0.lin_lo, 8)
            mlp_half(0)
            mlp_half(1, N[2])

            pe.wait_ge(N[2].lo, 4)
            for u in range(2):
                project(L1, S1, 0, "q", u, evac_of(L1, S1, "kv", u))
                transpose_x(N[2], 4 + u, (N[2].lo, 3 + u))
            project(L1, S1, 0, "q", 2, evac_of(L1, S1, "kv", 2))
            transpose_x(N[2], 6, (N[2].lo, 5))
            transpose_x(N[2], 7, (N[2].lo, 6))
            project(L1, S1, 0, "q", 3, evac_of(L1, S1, "kv", 3))
            drained(N[2])
            attention(L1, S1, N[3])

            def z_half(half):
                if half == 0:
                    pe.wait_ge(kv_lo_done, F1_A + 1)
                pe.wait_ge(N[3].lo, 4 * half + 4)
                L1.wait_bank(pe, S1, L1.kv_heads - 1, "z", half, last=True, drained=drained_by)
                product(work[0:ZH, L1.last_bank["z", half], :],
                        list(zip(weights(kv_hi, kv_lo, ZH, 0, ZH), columns(xT_hi, xT_lo, half * HALF, HALF))))\
                    .then_inc(f1.z, 1)

            z_half(0)
            early_x(L1, S1, N[3], 6)
            big_h(2)
            early_x(L1, S1, N[3], 7)
            big_h(3)
            z_half(1)
            big_h(4)
            pe.wait_ge(ffn1_loaded, 80)
            pe.wait_ge(f1.z_evac, 2)
            pe.wait_ge(S1.y_added, L1.kv_heads * NB)
            small = pt[:, 0, 0:2 * AC * NE].rearrange("p (a c e) -> p a c e", a=2, c=AC)
            for c in range(AC):
                mm = pe.matmul(small[:, :, c, :], zT[:, 2 * P * c + 1:2 * P * (c + 1):2], pick[:, :],
                               start=True, stop=True)
            mm.then_inc(f1.small, 1)
            for b in range(5, NB):
                big_h(b)
            pe.wait_ge(f1.w, 1)
            for c in range(AC):
                mm = pe.transpose(pt[0:NE, 1, c * P:(c + 1) * P], lg[5][:, c, :], ident[:, :])
            mm.then_inc(f1.wT, 1)
            pe.wait_ge(f1.wT_evac, 1)
            pe.matmul(yb[0:RANK, :], limes[:, :], wT[:, :], start=True, stop=True).then_inc(f1.pmix, 1)
            for b in range(NB):
                pe.wait_ge(f1.zp, 1 if b < 4 else 2)
                if b >= 2:
                    pe.wait_ge(f1.done, b - 1)
                pe.matmul(d2[b % 2], zp[:, b * P:(b + 1) * P], b_mat[:, :], start=True, stop=True)\
                    .then_inc(f1.delta, 1)

        @block.scalar
        def _(act):
            def split_hi(hi, raw, start, end, rows, loaded, in_use, at, value):
                act.wait_ge(loaded, at * 16 + 16)
                if in_use is not None:
                    act.wait_ge(in_use, value)
                return act.activation(hi[0:rows, start:end], raw[0:rows, start:end], ACT.Copy)

            def copy_bias(at):
                act.wait_ge(kv_loaded, at * 16 + 16)
                act.activation(bias_now[:, 0:6], kv_raw[:, 1024:1030], ACT.Copy).then_inc(bias_copied, 1)

            def evac_projection(L, S, dst, bank, done, col):
                act.wait_ge(S.proj_done, done)
                if L.bias:
                    act.activation(dst, work[0:L.hd, bank, :], ACT.Identity, bias=bias_now[:, col:col + 1])\
                        .then_inc(S.act_evac, 1)
                else:
                    act.activation(dst, work[0:L.hd, bank, :], ACT.Copy).then_inc(S.act_evac, 1)

            def evacuate(L, S, it, *uses):
                for kind, u in uses:
                    if u % 2 == 0:
                        if kind == "kv":
                            src, half = u // 4, u // 2 % 2
                            dst = kT[0:L.hd, 0:NB * L.keys].rearrange("p (b s k) -> p b s k", b=NB, k=P)
                            dst = dst[:, 4 * half:4 * half + 4, src, :]
                        else:
                            half, g = u // G, u % G
                            dst = qT[0:L.hd, g, half * HALF:(half + 1) * HALF]
                        evac_projection(L, S, dst, L.bank[kind, u], L.projected(it, kind, u), G if kind == "kv" else g)

            def evac_v(L, S, it, g):
                act.wait_ge(S.vt_done, it * L.v_groups + (g + 1))
                act.activation(v_hi[:, 8 * g * L.hd:8 * (g + 1) * L.hd].rearrange("p (j d) -> p j d", d=L.hd),
                               pt[:, :, :].rearrange("p a (j d) -> p (a j) d", d=P)[:, :, 0:L.hd], ACT.Copy)\
                    .then_inc(S.v_hi_done, 1)

            def pT_upper(L, S, it, b):
                for c in range(L.sources):
                    act.wait_ge(S.pt_done, (it * NB + b) * L.sources + (c + 1))
                    act.activation(pT_hi[:, c, :], pt[:, c, :], ACT.Copy).then_inc(S.pt_hi_done, 1)

            def oT_upper(L, S, it, b):
                act.wait_ge(S.pv_done, it * NB + (b + 1))
                for dst, src in o_parts(L):
                    copy = act.activation(o_buf(L, 0, b)[dst], ov_heads[src], ACT.Copy)
                copy.then_inc(S.o_hi_done, 1)

            def lin_hi(w):
                half, which, m = w // 4, w // 2 % 2, w % 2
                act.wait_ge(f0.lin, w + 1)
                act.activation(h_hi[:, 2 * which + m, half * HALF:(half + 1) * HALF], work[:, 2 * half + m, :], ACT.Copy)\
                    .then_inc(f0.lin_hi, 1)

            def head(L, S, it, norm, next_kv, next_q):
                if L.v_groups == 2:
                    evac_v(L, S, it, 0)
                for i in range(NB + 3):
                    if not L.double and i >= 4:
                        oT_upper(L, S, it, i - 3)
                    if norm is not None and not L.double and i == 6:
                        norm_hi(norm, 0)
                        norm_hi(norm, 1)
                    if i >= NB and norm is None:
                        evacuate(L, S, it + 1, *L.ahead_steps[i - NB])
                    b = i - 2
                    if i == (2 if L.double else 1) or 4 <= i < NB + 2:
                        pT_upper(L, S, it, max(b, 0))
                    if (i if L.double else i - 1) in (3, 4, 5):
                        next_weights(L, S, it, i if L.double else i - 1, norm, next_kv, next_q)
                    if i == 2:
                        evacuate(L, S, it, ("q", 6))
                    if i == 2 or L.double and 3 <= i < NB:
                        oT_upper(L, S, it, b)
                    if i == 2:
                        pT_upper(L, S, it, 1)
                    if i < NB:
                        act.wait_ge(S.max_done, it * NB + (i + 1))
                        bank = L.score_bank(i, norm is not None)
                        s = work[:, bank:bank + L.score_banks, :].rearrange("p a (g k) -> p (a g) k", k=L.keys)
                        for g in range(G):
                            e = act.activation(prob[:, i % 2, g * L.keys:(g + 1) * L.keys], s[:, g, :], ACT.Exp,
                                               bias=neg_max[:, i % 2, g:g + 1], scale=L.scale,
                                               accum_out=exp_sum[:, i % 2, g:g + 1])
                            if (g + 1) % (G // L.score_banks) == 0:
                                e.then_inc(S.exp_done, 1)
                    if i < 2:
                        evacuate(L, S, it, *[("q", u) for u in L.q_steps[i]])
                    if i == 0:
                        evac_v(L, S, it, L.v_groups - 1)
                        split_hi(o_hi, o_raw, 0, L.tiles * HID, P, o_loaded, S.scores_done, it + L.o0, it * NB + 1)\
                            .then_inc(o_hi_done, 1)
                    if norm is not None and 4 <= i < NB:
                        normalise_x(norm, i - 4, x[:, i - 4, :])
                    if norm is not None and L.double:
                        if i >= NB:
                            normalise_x(norm, i - 4, x[:, i - 4, :])
                        if i >= 5:
                            norm_hi(norm, i - 5)
                    elif norm is not None and i == NB:
                        norm_hi(norm, 2)
                        norm_hi(norm, 3)
                    if norm is not None and not L.double and i >= NB:
                        normalise_x(norm, i - 4, x[:, i - 4, :])
                        if i > NB:
                            norm_hi(norm, i - 5)
                            lin_hi(i - NB - 1)
                    if L.double and i in (NB, NB + 1):
                        oT_upper(L, S, it, b)

            def next_weights(L, S, it, i, norm, next_kv, next_q):
                if i == 3:
                    if L.bias and norm is None:
                        act.wait_ge(S.dve_evac, L.evacuated(it, "q", 7))
                        copy_bias(it + (L.kv0 + 1))
                    split_hi(kv_hi, kv_raw, 0, next_kv, P, kv_loaded, S.proj_done, it + (L.kv0 + 1),
                             L.projected(it, "q", 7)).then_inc(kv_hi_done, 1)
                if i == 4:
                    split_hi(q_hi, q_raw, 0, next_q // 2, P, q_loaded, S.proj_done, it + (L.q0 + 1),
                             L.projected(it, "q", 7)).then_inc(q_half_done, 1)
                if i == 5:
                    split_hi(q_hi, q_raw, next_q // 2, next_q, P, q_loaded, S.proj_done, it + (L.q0 + 1),
                             L.projected(it, "q", 7)).then_inc(q_hi_done, 1)

            def attention(L, S, norm, next_kv, next_q, own_kv, own_q):
                with act.Fori(0, L.kv_heads - 1) as it:
                    head(L, S, it, None, own_kv, own_q)
                head(L, S, L.kv_heads - 1, norm, next_kv, next_q)

            def normalise_x(n, b, src, dst=None):
                act.wait_ge(n.shift, b + 1)
                if dst is None:
                    if b >= n.bufs:
                        act.wait_ge(n.t, b - n.bufs + 1)
                    dst = xn_buf(n, b)
                act.activation(dst, src, ACT.Identity, bias=minus_mean[:, b:b + 1], scale=rstd[:, b:b + 1])\
                    .then_inc(n.xn, 1)

            def norm_hi(n, b):
                act.wait_ge(n.t, b + 1)
                act.activation(xT_hi[:, :, b * P:(b + 1) * P], x_bank(n, b).rearrange("p (k t) -> p k t", k=KT),
                               ACT.Copy).then_inc(n.hi, 1)

            split_hi(kv_hi, kv_raw, 0, 768, P, kv_loaded, None, 0, 0).then_inc(kv_hi_done, 1)
            for k in range(KT):
                act.wait_ge(c_loaded[k], 16)
                act.activation(cT_hi[:, k, :], qT[:, k, :], ACT.Copy).then_inc(c_hi_done, 1)
            act.wait_ge(const_loaded, 32)
            act.activation(gate_hi[:, :, :], gate_raw[:, :, :], ACT.Copy).then_inc(f0.gate_split_hi, 1)
            for b in range(4):
                normalise_x(N[0], b, x[:, b, :])
            split_hi(q_hi, q_raw, 0, 1536, P, q_loaded, None, 0, 0).then_inc(q_hi_done, 1)
            for b in range(4):
                norm_hi(N[0], b)
            evacuate(L0, S0, 0, *L0.ahead[0:4])
            for b in range(4, NB):
                normalise_x(N[0], b, x[:, b, :])
            norm_hi(N[0], 4)
            evacuate(L0, S0, 0, ("kv", 4))
            for b in range(5, NB):
                norm_hi(N[0], b)
            evacuate(L0, S0, 0, *L0.ahead[6:])
            attention(L0, S0, N[1], 1024, 512, 768, 1536)

            norm_hi(N[1], 6)
            normalise_x(N[1], NB - 1, x[:, NB - 1, :])
            lin_hi(2)
            norm_hi(N[1], 7)
            lin_hi(3)
            split_hi(o_hi, o_raw, 0, 1024, P, o_loaded, S0.y_done, FC2, L0.kv_heads * NB).then_inc(o_hi_done, 1)
            for w in range(4, 8):
                lin_hi(w)
            split_hi(q_hi, q_raw, 0, 2048, P, q_loaded, f0.lin, UP, 8).then_inc(q_hi_done, 1)
            split_hi(o_hi, o_raw, 0, 2048, P, o_loaded, f0.down, DOWN, NB).then_inc(o_hi_done, 1)

            def square_hi(hf, u):
                half, m = u // 4, u % 4
                act.wait_ge(f0.sq, hf * 8 + (u + 1))
                act.activation(h_hi[:, m, half * HALF:(half + 1) * HALF], h_f[:, u % 2, :], ACT.Copy)\
                    .then_inc(f0.h_hi, 1)

            def mlp_half(hf):
                for u in range(8):
                    act.wait_ge(f0.up, hf * 8 + (u + 1))
                    act.activation(relu[:, u % 2, :], work[:, u % 4, :], ACT.Relu).then_inc(f0.relu, 1)
                    if u:
                        square_hi(hf, u - 1)
                square_hi(hf, 7)

            mlp_half(0)
            split_hi(q_hi, q_raw, 0, 2048, P, q_loaded, f0.up, UP + 1, 8).then_inc(q_hi_done, 1)
            copy_bias(L1.kv0)
            split_hi(kv_hi, kv_raw, 0, 1024, P, kv_loaded, f0.lin, L1.kv0, 8).then_inc(kv_hi_done, 1)
            split_hi(o_hi, o_raw, 0, 2048, P, o_loaded, f0.down, DOWN + 1, 2 * NB).then_inc(o_hi_done, 1)
            mlp_half(1)
            split_hi(q_hi, q_raw, 0, 2048, P, q_loaded, f0.up, L1.q0, 16).then_inc(q_hi_done, 1)

            for j in range(NB):
                if j >= 4:
                    norm_hi(N[2], j - 4)
                if j >= 3:
                    normalise_x(N[2], j - 3, x[:, j - 3, :])
                if j == NB - 1:
                    act.wait_ge(f0.down, 3 * NB)
                    evacuate(L1, S1, 0, ("kv", 0))
                normalise_x(NA, j, acc[:, j, :], acc[:, j, :])
            normalise_x(N[2], 5, x[:, 5, :])
            evacuate(L1, S1, 0, ("kv", 2))
            norm_hi(N[2], 4)
            normalise_x(N[2], 6, x[:, 6, :])
            norm_hi(N[2], 5)
            evacuate(L1, S1, 0, ("q", 0))
            normalise_x(N[2], 7, x[:, 7, :])
            evacuate(L1, S1, 0, ("q", 2))
            norm_hi(N[2], 6)
            norm_hi(N[2], 7)
            attention(L1, S1, N[3], KT * ZH, 2048, 1024, 2048)
            normalise_x(N[3], NB - 1, x[:, NB - 1, :])
            norm_hi(N[3], 6)
            norm_hi(N[3], 7)
            act.wait_ge(f1.dve, 10)
            act.activation(lg[2][:, :, :], lg[1][:, :, :], ACT.Exp).then_inc(f1.exp, 1)
            act.wait_ge(f1.dve, 13 + AC + 1)
            act.activation(lg[4][:, :, :], lg[3][:, :, :], ACT.Exp, scale=-2.0).then_inc(f1.exp, 1)

        @block.gpsimd
        def _(pool):
            def split_lo(lo, raw, hi, n, rows, hi_done, done, at):
                pool.wait_ge(hi_done, at + 1)
                pool.tensor_tensor(lo[0:rows, 0:n], raw[0:rows, 0:n], hi[0:rows, 0:n].bitcast(F32), ALU.subtract)\
                    .then_inc(done, 1)

            def split_lo_part(lo, raw, hi, start, end, hi_done, at):
                pool.wait_ge(hi_done, at + 1)
                return pool.tensor_tensor(lo[:, start:end], raw[:, start:end], hi[:, start:end].bitcast(F32),
                                          ALU.subtract)

            def normalise(L, S, it, b):
                pool.wait_ge(S.rcp_done, it * NB + (b + 1))
                p = prob[:, b % 2, 0:G * L.keys].rearrange("p (g k) -> p g k", g=G)
                pool.tensor_tensor(p, p, exp_rcp[:, b % 2, :].unsqueeze(2).broadcast_to([P, G, L.keys]), ALU.mult)\
                    .then_inc(S.norm_done, 1)

            def add_b(b):
                pool.wait_ge(ffn1_loaded, 80)
                pool.wait_ge(N[3].xn, b + 1)
                pool.tensor_tensor(x[:, b, :], x[:, b, :], b_bc[:, :], ALU.add).then_inc(f1.b_added, 1)

            def head(L, S, it, next_kv, next_q, norm=None):
                for b in range(NB):
                    if norm is not None and b >= 4:
                        rstd_of(norm, b - 4)
                    normalise(L, S, it, b)
                    if b == 0:
                        split_lo(o_lo, o_raw, o_hi, L.tiles * HID, P, o_hi_done, o_lo_done, it + L.o0)
                    if b == 3:
                        split_lo(kv_lo, kv_raw, kv_hi, next_kv, P, kv_hi_done, kv_lo_done, it + (L.kv0 + 1))
                    if b == 4:
                        split_lo_part(q_lo, q_raw, q_hi, 0, next_q // 2, q_half_done, it + L.halves)\
                            .then_inc(q_lo_half, 1)
                    if b == 5:
                        split_lo_part(q_lo, q_raw, q_hi, next_q // 2, next_q, q_hi_done, it + (L.q0 + 1))\
                            .then_inc(q_lo_done, 1)
                if norm is not None:
                    for b in range(4, NB):
                        rstd_of(norm, b)
                        if L.double:
                            add_b(b - 4)

            def attention(L, S, norm, next_kv, next_q, own_kv, own_q):
                with pool.Fori(0, L.kv_heads - 1) as it:
                    head(L, S, it, own_kv, own_q)
                head(L, S, L.kv_heads - 1, next_kv, next_q, norm)

            def rstd_of(n, b):
                at = slice(b, b + 1)
                pool.wait_ge(n.var, b + 1)
                pool.tensor_tensor(rstd[:, at], var_eps[:, at], minus_half[:, :], ALU.pow).then_inc(n.rstd, 1)

            pool.memset(minus_half[:, :], -0.5).then_inc(pool_set, 1)
            pool.wait_ge(pool_set, 1)
            split_lo(kv_lo, kv_raw, kv_hi, 768, P, kv_hi_done, kv_lo_done, 0)
            pool.wait_ge(c_hi_done, 3)
            pool.tensor_tensor(cT_lo[:, 2, :], qT[:, 2, :], cT_hi[:, 2, :].bitcast(F32), ALU.subtract)\
                .then_inc(c_lo_pool, 1)
            for b in range(4):
                rstd_of(N[0], b)
            split_lo(q_lo, q_raw, q_hi, 1536, P, q_hi_done, q_lo_done, 0)
            for b in range(4, NB):
                rstd_of(N[0], b)
            pool.wait_ge(f0.gate_split_hi, 1)
            pool.tensor_tensor(gate_lo[:, :, :], gate_raw[:, :, :], gate_hi[:, :, :].bitcast(F32), ALU.subtract)\
                .then_inc(f0.gate_split_lo, 1)
            attention(L0, S0, N[1], 1024, 512, 768, 1536)

            split_lo(o_lo, o_raw, o_hi, 1024, P, o_hi_done, o_lo_done, FC2)
            pool.wait_ge(ffn0_loaded, 32)
            pool.wait_ge(N[1].xn, NB)
            for b in range(NB):
                pool.tensor_tensor(x[:, b, :], x[:, b, :], beta[:, :], ALU.add).then_inc(f0.beta_added, 1)
            split_lo(q_lo, q_raw, q_hi, 2048, P, q_hi_done, q_lo_done, UP)
            split_lo(o_lo, o_raw, o_hi, 2048, P, o_hi_done, o_lo_done, DOWN)

            def mlp_half(hf):
                for u in range(8):
                    pool.wait_ge(f0.relu, hf * 8 + (u + 1))
                    if hf or u >= 2:
                        pool.wait_ge(f0.h_lo, hf * 8 + (u - 1))
                    pool.tensor_tensor(h_f[:, u % 2, :], relu[:, u % 2, :], relu[:, u % 2, :], ALU.mult)\
                        .then_inc(f0.sq, 1)

            mlp_half(0)
            split_lo(q_lo, q_raw, q_hi, 2048, P, q_hi_done, q_lo_done, UP + 1)
            split_lo(kv_lo, kv_raw, kv_hi, 1024, P, kv_hi_done, kv_lo_done, L1.kv0)
            split_lo(o_lo, o_raw, o_hi, 2048, P, o_hi_done, o_lo_done, DOWN + 1)
            mlp_half(1)
            split_lo(q_lo, q_raw, q_hi, 2048, P, q_hi_done, q_lo_done, L1.q0)
            pool.wait_ge(bo_loaded, 16)
            for j in range(NB + 4):
                if j < NB:
                    rstd_of(NA, j)
                if 1 <= j < NB + 1:
                    b = j - 1
                    pool.wait_ge(NA.xn, b + 1)
                    pool.tensor_tensor(acc[:, b, :], acc[:, b, :], gamma[:, :], ALU.mult).then_inc(f0.scaled, 1)
                if 2 <= j < NB + 2:
                    rstd_of(N[2], j - 2)
                if j >= 4:
                    b = j - 4
                    pool.wait_ge(N[2].xn, b + 1)
                    pool.tensor_tensor(x[:, b, :], x[:, b, :], bo_bc[:, :], ALU.add).then_inc(bo_added, 1)
            attention(L1, S1, N[3], KT * ZH, 2048, 1024, 2048)
            for b in range(4, NB):
                add_b(b)
            pool.wait_ge(f1.dve, 1)
            pool.partition_all_reduce(allmax[:, :], absmax[:, :], P, RMAX).then_inc(f1.allmax, 1)

        @block.vector
        def _(dve):
            def evac_projection(L, S, dst, bank, done, col):
                dve.wait_ge(S.proj_done, done)
                if L.bias:
                    dve.tensor_scalar(dst, work[0:L.hd, bank, :], bias_now[:, col:col + 1], None, ALU.add)\
                        .then_inc(S.dve_evac, 1)
                else:
                    dve.tensor_copy(dst, work[0:L.hd, bank, :]).then_inc(S.dve_evac, 1)

            def evacuate(L, S, it, *uses):
                for kind, u in uses:
                    if u % 2 == 1:
                        half, g = u // G, u % G
                        if kind == "kv":
                            at = u // 4 * TOK + u // 2 % 2 * HALF
                            dst = vT[0:L.hd, at:at + HALF]
                        else:
                            dst = qT[0:L.hd, g, half * HALF:(half + 1) * HALF]
                        evac_projection(L, S, dst, L.bank[kind, u], L.projected(it, kind, u), G + 1 if kind == "kv" else g)

            def evac_v(L, S, it, g):
                dve.wait_ge(S.v_hi_done, it * L.v_groups + (g + 1))
                at = slice(8 * g * L.hd, 8 * (g + 1) * L.hd)
                dve.tensor_tensor(v_lo[:, at].rearrange("p (j d) -> p j d", d=L.hd),
                                  pt[:, :, :].rearrange("p a (j d) -> p (a j) d", d=P)[:, :, 0:L.hd],
                                  v_hi[:, at].bitcast(F32).rearrange("p (j d) -> p j d", d=L.hd),
                                  ALU.subtract).then_inc(S.v_lo_done, 1)

            def add_y(L, S, it, b):
                dve.wait_ge(S.y_done, it * NB + (b + 1))
                dve.tensor_tensor(x[:, b, :], x[:, b, :], y_buf(L, b), ALU.add).then_inc(S.y_added, 1)

            def head(L, S, it, norm=None):
                if L.v_groups == 2:
                    evac_v(L, S, it, 0)
                for i in range(NB + 3):
                    b = i - 2
                    if not L.double and i >= 4:
                        oT_lower(L, S, it, i - 3)
                    if norm is not None and not L.double and i == 6:
                        norm_lo(norm, 0)
                        norm_lo(norm, 1)
                    if i >= NB and norm is None:
                        evacuate(L, S, it + 1, *L.ahead_steps[i - NB])
                    if L.double and (i == 2 or 4 <= i < NB + 2):
                        pT_lower(L, S, it, b)
                    if i == 2:
                        oT_lower(L, S, it, 0)
                        evacuate(L, S, it, ("q", 7))
                    if i < NB:
                        negative_max(L, S, it, i, norm is not None)
                    if i == 2:
                        pT_lower(L, S, it, 1)
                    if not L.double and (i == 1 or 4 <= i < NB + 2):
                        pT_lower(L, S, it, max(b, 0))
                    if norm is not None and i >= 4:
                        shift(norm, i - 4)
                    if L.double and 3 <= i < NB + 2:
                        oT_lower(L, S, it, b)
                    if i >= 3:
                        add_share(L, S, it, i - 3, norm)
                    if i < NB:
                        dve.wait_ge(S.exp_done, it * (NB * L.score_banks) + (i + 1) * L.score_banks)
                        dve.reciprocal(exp_rcp[:, i % 2, :], exp_sum[:, i % 2, :]).then_inc(S.rcp_done, 1)
                    if i == 0:
                        evac_v(L, S, it, L.v_groups - 1)
                    if i < 2:
                        evacuate(L, S, it, *[("q", u) for u in L.q_steps[i]])
                    if norm is not None and L.double and i >= 5:
                        norm_lo(norm, i - 5)
                        if i > NB:
                            add_h(i - NB - 1)
                    elif norm is not None and not L.double and i == NB:
                        norm_lo(norm, 2)
                        norm_lo(norm, 3)
                    elif norm is not None and i > NB:
                        norm_lo(norm, i - 5)
                        lin_lo(i - NB - 1)
                if norm is not None:
                    shift(norm, NB - 1)

            def negative_max(L, S, it, b, last):
                dve.wait_ge(S.scores_done, it * NB + (b + 1))
                bank = L.score_bank(b, last)
                s = work[:, bank:bank + L.score_banks, :].rearrange("p a (g k) -> p (a g) k", k=L.keys)
                dve.tensor_reduce(neg_max_raw[:, b % 2, :], s, AX.X, ALU.max, negate=True)\
                    .then_inc(S.max_raw, 1)
                dve.wait_ge(S.max_raw, it * NB + (b + 1))
                dve.tensor_scalar(neg_max[:, b % 2, :], neg_max_raw[:, b % 2, :], L.scale, None, ALU.mult)\
                    .then_inc(S.max_done, 1)

            def add_share(L, S, it, b, norm):
                if L.bias and b == 0:
                    dve.wait_ge(bo_added, NB)
                add_y(L, S, it, b)
                if norm is not None:
                    dve.wait_ge(S.y_added, it * NB + (b + 1))
                    statistics(norm, x, b)

            def lin_lo(w):
                half, which, m = w // 4, w // 2 % 2, w % 2
                dve.wait_ge(f0.lin_hi, w + 1)
                at = (slice(None), 2 * which + m, slice(half * HALF, (half + 1) * HALF))
                dve.tensor_tensor(h_lo[at], work[:, 2 * half + m, :], h_hi[at].bitcast(F32), ALU.subtract)\
                    .then_inc(f0.lin_lo, 1)

            def pT_lower(L, S, it, b):
                for c in range(L.sources):
                    dve.wait_ge(S.pt_hi_done, (it * NB + b) * L.sources + (c + 1))
                    dve.tensor_tensor(pT_lo[:, c, :], pt[:, c, :], pT_hi[:, c, :].bitcast(F32), ALU.subtract)\
                        .then_inc(S.pt_lo_done, 1)

            def oT_lower(L, S, it, b):
                dve.wait_ge(S.o_hi_done, it * NB + (b + 1))
                for dst, src in o_parts(L):
                    lower = dve.tensor_tensor(o_buf(L, 1, b)[dst], ov_heads[src],
                                              o_buf(L, 0, b)[dst].bitcast(F32), ALU.subtract)
                lower.then_inc(S.o_lo_done, 1)

            def attention(L, S, norm):
                with dve.Fori(0, L.kv_heads - 1) as it:
                    head(L, S, it)
                head(L, S, L.kv_heads - 1, norm)

            def statistics(n, src, b):
                dve.bn_stats(stats[:, b, :], src[:, b, :]).then_inc(n.stat, 1)
                dve.wait_ge(n.stat, 2 * b + 1)
                dve.bn_aggr(mean_var[:, b, :], stats[:, b, :]).then_inc(n.stat, 1)
                dve.wait_ge(n.stat, 2 * b + 2)
                dve.tensor_scalar(var_eps[:, b:b + 1], mean_var[:, b, 1:2], LN_EPS, None, ALU.add).then_inc(n.var, 1)

            def shift(n, b):
                dve.wait_ge(n.rstd, b + 1)
                dve.scalar_tensor_tensor(out=minus_mean[:, b:b + 1], in0=mean_var[:, b, 0:1], scalar=-1.0,
                                         in1=rstd[:, b:b + 1], op0=ALU.mult, op1=ALU.mult).then_inc(n.shift, 1)

            def add_h(b):
                dve.wait_ge(f1.H, b + 1)
                dve.wait_ge(f1.b_added, b + 1)
                dve.tensor_tensor(x[:, b, :], x[:, b, :], work[:, L1.last_bank["h", b], :], ALU.add)\
                    .then_inc(f1.H_added, 1)

            def norm_lo(n, b):
                dve.wait_ge(n.hi, b + 1)
                dve.tensor_tensor(xT_lo[:, :, b * P:(b + 1) * P], x_bank(n, b).rearrange("p (k t) -> p k t", k=KT),
                                  xT_hi[:, :, b * P:(b + 1) * P].bitcast(F32), ALU.subtract).then_inc(n.lo, 1)

            for k in (0, 1, 3):
                dve.wait_ge(c_hi_done, k + 1)
                dve.tensor_tensor(cT_lo[:, k, :], qT[:, k, :], cT_hi[:, k, :].bitcast(F32), ALU.subtract)\
                    .then_inc(c_lo_done, 1)
            dve.wait_ge(x_loaded[0], 16)
            for b in range(4):
                statistics(N[0], x, b)
                if b:
                    shift(N[0], b - 1)
            shift(N[0], 3)
            evacuate(L0, S0, 0, ("kv", 1))
            for b in range(4):
                norm_lo(N[0], b)
            evacuate(L0, S0, 0, ("kv", 3))
            dve.wait_ge(x_loaded[1], 16)
            for b in range(4, NB):
                statistics(N[0], x, b)
                if b > 4:
                    shift(N[0], b - 1)
            shift(N[0], NB - 1)
            norm_lo(N[0], 4)
            evacuate(L0, S0, 0, ("kv", 5))
            for b in range(5, NB):
                norm_lo(N[0], b)
            evacuate(L0, S0, 0, *L0.ahead[6:])
            attention(L0, S0, N[1])

            norm_lo(N[1], 6)
            lin_lo(2)
            norm_lo(N[1], 7)
            lin_lo(3)
            lin_lo(4)
            lin_lo(5)
            dve.wait_ge(f0.gate, 1)
            dve.tensor_copy(logitsT[0:NE, :], pt[0:NE, :, :].rearrange("p a t -> p (a t)")).then_inc(f0.gate_copied, 1)
            lin_lo(6)
            lin_lo(7)
            dve.wait_ge(f0.gate, 2)
            for b in range(NB):
                dve.max(top8[:, b, :], pt[:, 0, b * NE:(b + 1) * NE]).then_inc(f0.route_top, 1)
            dve.wait_ge(f0.route_top, NB)
            dve.tensor_tensor(route[:, :], top8[:, :, 0], top8[:, :, 1], ALU.add).then_inc(f0.route, 1)
            dve.wait_ge(f0.route, 1)
            for b in range(NB):
                dve.wait_ge(f0.down, b + 1)
                dve.tensor_scalar(acc[:, b, :], y2[b % 2][:, :], route[:, b:b + 1], None, ALU.mult)\
                    .then_inc(f0.added, 1)

            def square_lo(hf, u):
                half, m = u // 4, u % 4
                dve.wait_ge(f0.h_hi, hf * 8 + (u + 1))
                at = (slice(None), m, slice(half * HALF, (half + 1) * HALF))
                dve.tensor_tensor(h_lo[at], h_f[:, u % 2, :], h_hi[at].bitcast(F32), ALU.subtract)\
                    .then_inc(f0.h_lo, 1)

            def add_down(hf, b):
                dve.wait_ge(f0.down, hf * 8 + (NB + b + 1))
                dve.wait_ge(f0.added, hf * 8 + (b + 1))
                dve.tensor_tensor(acc[:, b, :], acc[:, b, :], y2[b % 2][:, :], ALU.add).then_inc(f0.added, 1)

            for u in range(8):
                square_lo(0, u)
            for b in range(NB):
                add_down(0, b)
            for u in range(8):
                square_lo(1, u)
            def add_norm(b):
                dve.wait_ge(f0.scaled, b + 1)
                dve.wait_ge(f0.beta_added, b + 1)
                dve.tensor_tensor(x[:, b, :], x[:, b, :], acc[:, b, :], ALU.add).then_inc(f0.x_done, 1)

            def statistics_x(b):
                dve.wait_ge(f0.x_done, b + 1)
                statistics(N[2], x, b)

            for j in range(NB):
                add_down(1, j)
                if j >= 3:
                    shift(N[2], j - 3)
                dve.wait_ge(f0.added, 2 * NB + j + 1)
                statistics(NA, acc, j)
                if j >= 2:
                    add_norm(j - 2)
                shift(NA, j)
                if j >= 4:
                    norm_lo(N[2], j - 4)
                if j >= 2:
                    statistics_x(j - 2)
            shift(N[2], 5)
            evacuate(L1, S1, 0, ("kv", 1))
            add_norm(6)
            statistics_x(6)
            evacuate(L1, S1, 0, ("kv", 3))
            add_norm(7)
            shift(N[2], 6)
            statistics_x(7)
            norm_lo(N[2], 4)
            shift(N[2], 7)
            norm_lo(N[2], 5)
            evacuate(L1, S1, 0, ("q", 1))
            norm_lo(N[2], 6)
            norm_lo(N[2], 7)
            evacuate(L1, S1, 0, ("q", 3))

            attention(L1, S1, N[3])

            def evac_z(half):
                dve.wait_ge(f1.z, half + 1)
                dve.wait_ge(ffn1_loaded, 80)
                dve.tensor_scalar(zT[:, half * HALF:(half + 1) * HALF], work[0:ZH, L1.last_bank["z", half], :],
                                  z_bias[:, :], None, ALU.add).then_inc(f1.z_evac, 1)

            evac_z(0)
            norm_lo(N[3], 6)
            add_h(2)
            norm_lo(N[3], 7)
            add_h(3)
            evac_z(1)
            add_h(4)
            dve.wait_ge(f1.small, 1)
            both = pt[:, 0, 0:2 * AC * NE].rearrange("p (a e) -> p a e", a=2)
            dve.tensor_reduce(absmax[:, :], both, AX.X, ALU.max, apply_absolute_value=True).then_inc(f1.dve, 1)
            dve.tensor_copy(hd[:, :, :, :].rearrange("p a c e -> p (a c e)"), pt[:, 0, 0:2 * AC * NE]).then_inc(f1.dve, 1)
            step = [2]

            def chained(ins):
                ins.then_inc(f1.dve, 1)
                step[0] += 1
                dve.wait_ge(f1.dve, step[0])

            def per_row(r):
                return r[:, :].unsqueeze(2).broadcast_to([P, AC, NE])

            dve.wait_ge(f1.allmax, 1)
            chained(dve.tensor_scalar(row[0][:, 0:2], allmax[:, :], 1e-6, None, ALU.max))
            chained(dve.reciprocal(row[1][:, 0:2], row[0][:, 0:2]))
            chained(dve.tensor_scalar(row[2][:, 0:2], row[1][:, 0:2], 0.5, None, ALU.mult))
            chained(dve.tensor_scalar(lg[0][:, :, :], hd[:, 0, :, :], row[2][:, 0:1], None, ALU.mult))
            chained(dve.scalar_tensor_tensor(out=lg[7][:, :, :], in0=hd[:, 1, :, :], scalar=row[2][:, 1:2],
                                             in1=lg[0][:, :, :], op0=ALU.mult, op1=ALU.add))
            chained(dve.tensor_reduce(row[3][:, :], lg[7][:, :, :], AX.X, ALU.max))
            chained(dve.tensor_tensor(lg[1][:, :, :], lg[7][:, :, :], per_row(row[3]), ALU.subtract))
            chained(dve.tensor_scalar(lg[1][:, :, :], lg[1][:, :, :], 1.0, None, ALU.mult))
            assert step[0] == 10
            add_h(5)
            dve.wait_ge(f1.exp, 1)
            chained(dve.tensor_reduce(row[4][:, :], lg[2][:, :, :], AX.X, ALU.add))
            chained(dve.reciprocal(row[5][:, :], row[4][:, :]))
            chained(dve.tensor_tensor(lg[6][:, :, :], lg[2][:, :, :], per_row(row[5]), ALU.mult))
            for c in range(AC):
                chained(dve.max(top8b[:, c, :], lg[6][:, c, :]))
            chained(dve.tensor_tensor(lg[3][:, :, :], lg[6][:, :, :],
                                      top8b[:, :, 1:2].broadcast_to([P, AC, NE]), ALU.subtract))
            assert step[0] == 13 + AC + 1
            add_h(6)
            dve.wait_ge(f1.exp, 2)
            chained(dve.tensor_scalar(lg[0][:, :, :], lg[4][:, :, :], 1.0, None, ALU.add))
            chained(dve.reciprocal(lg[1][:, :, :], lg[0][:, :, :]))
            chained(dve.tensor_tensor(lg[2][:, :, :], lg[1][:, :, :], lg[6][:, :, :], ALU.mult))
            chained(dve.tensor_reduce(row[0][:, :], lg[2][:, :, :], AX.X, ALU.add))
            chained(dve.tensor_scalar(row[1][:, :], row[0][:, :], 1e-9, None, ALU.add))
            chained(dve.reciprocal(row[2][:, :], row[1][:, :]))
            dve.tensor_tensor(lg[5][:, :, :], lg[2][:, :, :], per_row(row[2]), ALU.mult).then_inc(f1.w, 1)
            add_h(7)
            dve.wait_ge(f1.wT, 1)
            dve.tensor_copy(wT[:, :], pt[0:NE, 1, :]).then_inc(f1.wT_evac, 1)
            dve.wait_ge(f1.pmix, 1)
            for half in range(2):
                pairs = slice(half * HALF // 2, (half + 1) * HALF // 2)
                of_pairs = lambda t: t[0:RANK, :].rearrange("p (a two) -> p a two", two=2)[:, pairs, :]
                dve.scalar_tensor_tensor(out=of_pairs(zp), in0=of_pairs(zT), scalar=0.5,
                                         in1=yb[0:RANK, pairs].unsqueeze(2).broadcast_to([RANK, HALF // 2, 2]),
                                         op0=ALU.mult, op1=ALU.mult).then_inc(f1.zp, 1)
            for b in range(NB):
                dve.wait_ge(f1.delta, b + 1)
                dve.wait_ge(f1.H_added, b + 1)
                dve.tensor_tensor(x[:, b, :], x[:, b, :], d2[b % 2], ALU.add).then_inc(f1.done, 1)


def laid_out(i):
    def tiles(w):
        return w.reshape(-1, P, w.shape[-1]).transpose(1, 0, 2).reshape(P, -1)

    def rows(v):
        return np.broadcast_to(v, (P, v.shape[0]))

    wq, wk, wv, wo = (i[f"L0_xattn_W{n}"] for n in "qkvo")
    per_head = lambda w: w.reshape(4, -1, KT, P).transpose(0, 3, 2, 1)
    wo_heads = wo.reshape(HID, 4, G, 96).transpose(1, 3, 2, 0)
    a = {
        "x": i["x"],
        "ctxT": i["ctx_4096"].reshape(TOK, KT, P).transpose(2, 1, 0),
        "l0_q": per_head(wq).reshape(4, P, -1),
        "l0_kv": np.concatenate([per_head(wk), per_head(wv)], 3).reshape(4, P, -1),
        "l0_o": np.concatenate([wo_heads[:, :, :3], wo_heads[:, :, 3].reshape(4, 3, 32, HID).transpose(0, 2, 1, 3)], 1)
        .reshape(4, P, -1),
        "gate": i["L0_ffn_gate_w"].reshape(KT, P, NE).transpose(1, 0, 2),
        "up": i["L0_ffn_up_w"].reshape(KT, P, 2, HID).transpose(2, 1, 0, 3).reshape(2, P, -1),
        "down": i["L0_ffn_down_w"].reshape(2, 4, P, HID).transpose(0, 2, 1, 3).reshape(2, P, -1),
        "fc1": tiles(i["L0_ffn_fc1_w"]), "expert": tiles(i["L0_ffn_expert_w"]), "fc2": tiles(i["L0_ffn_fc2_w"]),
        "gamma": rows(i["L0_ffn_ln_gamma"]), "beta": rows(i["L0_ffn_ln_beta"]),
    }
    heads = lambda w, n: w.reshape(KT, P, 8, n).transpose(2, 1, 0, 3)
    wkv, bkv = i["L1_xattn_Wkv"], i["L1_xattn_bkv"]
    a["l1_q"] = heads(i["L1_xattn_Wq"], G * P).reshape(8, P, -1)
    w = np.concatenate([heads(wkv[:, :1024], P), heads(wkv[:, 1024:], P)], 3).reshape(8, P, -1)
    bq = i["L1_xattn_bq"].reshape(8, G, P).transpose(0, 2, 1)
    bk, bv = bkv[:1024].reshape(8, P, 1), bkv[1024:].reshape(8, P, 1)
    a["l1_kv"] = np.concatenate([w, bq, bk, bv], 2)
    a["l1_o"] = i["L1_xattn_Wo"].reshape(8, G, P, HID).transpose(0, 2, 1, 3).reshape(8, P, -1)
    a["bo"] = rows(i["L1_xattn_bo"])
    a["W"] = i["L1_ffn_W"].reshape(HID, KT, P).transpose(2, 1, 0).reshape(P, -1)
    z_h = np.concatenate([i["L1_ffn_A"].reshape(KT, P, RANK), i["L1_ffn_W"][:NE].T.reshape(KT, P, NE)], 2)
    a["A"] = z_h.transpose(1, 0, 2).reshape(P, -1)
    a["b"], a["Bmat"] = rows(i["L1_ffn_b"]), i["L1_ffn_Bmat"]
    a["LiMEs"] = i["L1_ffn_LiMEs"]
    a["pick"] = np.zeros((RANK + NE, 2 * NE), np.float32)
    a["pick"][RANK:, :NE] = np.eye(NE, dtype=np.float32)
    a["pick"][:RANK, NE:] = i["L1_ffn_LiMEs"].T
    a["z_bias"] = np.zeros((RANK + NE, 1), np.float32)
    a["z_bias"][RANK:, 0] = i["L1_ffn_b"][:NE]
    a["ident"] = np.eye(P, dtype=np.float32)
    return {n: np.ascontiguousarray(v) for n, v in a.items()}


def kernel(**inputs):
    import concourse.bacc as bacc
    from concourse.bass_utils import run_bass_kernel_spmd

    nc = bacc.Bacc("TRN2", target_bir_lowering=False, num_devices=1)
    arrays = laid_out({n: np.asarray(v) for n, v in inputs.items()})
    aps = {n: nc.dram_tensor(f"in_{n}", v.shape, mybir.dt.from_np(v.dtype), kind="ExternalInput").ap()
           for n, v in arrays.items()}
    out = nc.dram_tensor("out_0", (NB, P, HID), F32, kind="ExternalOutput").ap()
    build_program(nc, aps, out)
    result = run_bass_kernel_spmd(nc, [{f"in_{n}": v for n, v in arrays.items()}], core_ids=[0])
    return result.results[0]["out_0"]
```
